# Optimizing a Trainium2 kernel written in Bass

```python
import numpy as np
import jax
import jax.numpy as jnp

def _softmax(x, axis=-1):
    return jax.nn.softmax(x, axis=axis)

def _gelu(x):
    return jax.nn.gelu(x, approximate=True)

def _silu(x):
    return jax.nn.silu(x)

def _sigmoid(x):
    return jax.nn.sigmoid(x)

def _layernorm(x, axis=-1, eps=1e-05):
    m = jnp.mean(x, axis=axis, keepdims=True)
    v = jnp.var(x, axis=axis, keepdims=True)
    return (x - m) / jnp.sqrt(v + eps)

def _scatter_add(tgt, idx, src, axis=0):
    return tgt.at[idx].add(src)

def _segment_sum(src, seg, n):
    return jax.ops.segment_sum(src, seg, n)
kernel_name = 'mk_decoder_postln_d1_seqx_r4_013bb0'

def setup_inputs(seed: int=0):
    np.random.seed(seed)
    _w = jnp.asarray

    def _rec_inputs():
        import jax
        import jax.numpy as jnp
        _rk = jax.random.key(seed)
        x = -0.0002928 + 1 * jax.random.normal(jax.random.fold_in(_rk, 1), (4, 1024, 256), jnp.float32)
        _lenS = 1024 - jax.random.randint(jax.random.fold_in(_rk, 7), (4,), 0, max(1, 1024 // 4) + 1, jnp.int32)
        _lenS2 = 77 - jax.random.randint(jax.random.fold_in(_rk, 8), (4,), 0, max(1, 77 // 4) + 1, jnp.int32)
        _ctx_1024P = jax.random.normal(jax.random.fold_in(_rk, 11), (4, 16, 256), jnp.float32)
        _ctx_1024c = jax.random.dirichlet(jax.random.fold_in(_rk, 511), 0.3 * jnp.ones((16,), jnp.float32), (4, 77))
        _ctx_1024t = jnp.einsum('bsk,bkd->bsd', _ctx_1024c, _ctx_1024P)
        _ctx_1024t = _ctx_1024t * jax.lax.rsqrt(jnp.mean(jnp.square(_ctx_1024t)) + 1e-12) * 0.953939
        ctx_1024 = -1.39393e-06 + 0.999914 * (_ctx_1024t + 0.3 * jax.random.normal(jax.random.fold_in(_rk, 611), (4, 77, 256), jnp.float32))
        _validS = jnp.arange(1024)[None, :] < _lenS[:, None]
        _validS2 = jnp.arange(77)[None, :] < _lenS2[:, None]
        _causal = jnp.tril(jnp.ones((1024, 1024), dtype=bool))
        mask_Bx1x1xS2_ik0 = jnp.where(jnp.broadcast_to(_validS2[:, None, None, :], (4, 1, 1, 77)), 0, 1).astype(jnp.int32)
        return (x, ctx_1024, mask_Bx1x1xS2_ik0)
    x, ctx_1024, mask_Bx1x1xS2_ik0 = _rec_inputs()

    def _L0_attn_setup():
        import jax, jax.numpy as jnp
        import numpy as np
        import math
        DIM = 256
        NUM_HEADS = 16
        HEAD_DIM = DIM // NUM_HEADS
        MAX_BIAS = 8.0
        SCALE = HEAD_DIM ** (-0.5)

        def _alibi_slopes(n):

            def pow2(n):
                start = 2.0 ** (-2.0 ** (-(math.log2(n) - 3)))
                return [start * start ** i for i in range(n)]
            if math.log2(n).is_integer():
                return pow2(n)
            c = 2 ** math.floor(math.log2(n))
            return pow2(c) + _alibi_slopes(2 * c)[0::2][:n - c]

        def _rotate_half(t):
            t1, t2 = jnp.split(t, 2, axis=-1)
            return jnp.concatenate([-t2, t1], axis=-1)
        key = jax.random.key(seed)
        k1, k2, k3, k4 = jax.random.split(key, 4)
        B, N, C = (2, 512, DIM)
        x = jax.random.normal(k1, (B, N, C), dtype=jnp.float32)
        qkv_w = jax.random.normal(k2, (3 * C, C), dtype=jnp.float32) * C ** (-0.5)
        proj_w = jax.random.normal(k3, (C, C), dtype=jnp.float32) * C ** (-0.5)
        proj_b = jax.random.normal(k4, (C,), dtype=jnp.float32) * 0.01
        slopes = jnp.asarray(np.array(_alibi_slopes(NUM_HEADS), dtype=np.float32))
        return {'x': x, 'qkv_w': qkv_w, 'proj_w': proj_w, 'proj_b': proj_b, 'slopes': slopes}
    _L0_attn_all = _L0_attn_setup()
    _L0_attn_in = {k: v for k, v in _L0_attn_all.items() if k in ('qkv_w', 'proj_w', 'proj_b', 'slopes')}
    del _L0_attn_all

    def _L0_xattn_setup():
        import jax, jax.numpy as jnp
        import numpy as np
        HEADS = 16
        D_MODEL = 256
        HEAD_DIM = D_MODEL // HEADS
        NEG = -1000000000000000.0

        def _split_heads(x):
            B, L, _ = x.shape
            return x.reshape(B, L, HEADS, HEAD_DIM).transpose(0, 2, 1, 3)
        key = jax.random.key(seed)
        ks = jax.random.split(key, 13)
        B, L = (2, 512)
        scale = 1.0 / np.sqrt(D_MODEL)
        inp = {'q': jax.random.normal(ks[0], (B, L, D_MODEL), jnp.float32), 'k': jax.random.normal(ks[1], (B, L, D_MODEL), jnp.float32), 'v': jax.random.normal(ks[2], (B, L, D_MODEL), jnp.float32), 'mask': jax.random.randint(ks[3], (B, 1, 1, L), 0, 2, jnp.int32), 'Wq': jax.random.normal(ks[4], (D_MODEL, D_MODEL), jnp.float32) * scale, 'bq': jax.random.normal(ks[5], (D_MODEL,), jnp.float32) * scale, 'Wk': jax.random.normal(ks[6], (D_MODEL, D_MODEL), jnp.float32) * scale, 'bk': jax.random.normal(ks[7], (D_MODEL,), jnp.float32) * scale, 'Wv': jax.random.normal(ks[8], (D_MODEL, D_MODEL), jnp.float32) * scale, 'bv': jax.random.normal(ks[9], (D_MODEL,), jnp.float32) * scale, 'Wo': jax.random.normal(ks[10], (D_MODEL, D_MODEL), jnp.float32) * scale, 'bo': jax.random.normal(ks[11], (D_MODEL,), jnp.float32) * scale}
        return inp
    _L0_xattn_all = _L0_xattn_setup()
    _L0_xattn_in = {k: v for k, v in _L0_xattn_all.items() if k in ('Wq', 'bq', 'Wk', 'bk', 'Wv', 'bv', 'Wo', 'bo')}
    del _L0_xattn_all

    def _L0_ffn_setup():
        import jax, jax.numpy as jnp
        import numpy as np
        B, T, C, E, K, CAP, H = (8, 512, 256, 8, 2, 1024, 1024)
        key = jax.random.key(seed)
        ks = jax.random.split(key, 6)
        s = 0.02
        return {'x': jax.random.normal(ks[0], (B, T, C), jnp.float32), 'rw1': s * jax.random.normal(ks[1], (C, H), jnp.float32), 'rb1': jnp.zeros((H,), jnp.float32), 'rw2': s * jax.random.normal(ks[2], (H, E), jnp.float32), 'rb2': jnp.zeros((E,), jnp.float32), 'ew1': s * jax.random.normal(ks[3], (E, C, H), jnp.float32), 'eb1': jnp.zeros((E, H), jnp.float32), 'ew2': s * jax.random.normal(ks[4], (E, H, C), jnp.float32), 'eb2': jnp.zeros((E, C), jnp.float32)}
    _L0_ffn_all = _L0_ffn_setup()
    _L0_ffn_in = {k: v for k, v in _L0_ffn_all.items() if k in ('rw1', 'rb1', 'rw2', 'rb2', 'ew1', 'eb1', 'ew2', 'eb2')}
    del _L0_ffn_all
    return {'x': x, 'ctx_1024': ctx_1024, 'mask_Bx1x1xS2_ik0': mask_Bx1x1xS2_ik0, 'L0_attn_qkv_w': _L0_attn_in['qkv_w'], 'L0_attn_proj_w': _L0_attn_in['proj_w'], 'L0_attn_proj_b': _L0_attn_in['proj_b'], 'L0_attn_slopes': _L0_attn_in['slopes'], 'L0_xattn_Wq': _L0_xattn_in['Wq'], 'L0_xattn_bq': _L0_xattn_in['bq'], 'L0_xattn_Wk': _L0_xattn_in['Wk'], 'L0_xattn_bk': _L0_xattn_in['bk'], 'L0_xattn_Wv': _L0_xattn_in['Wv'], 'L0_xattn_bv': _L0_xattn_in['bv'], 'L0_xattn_Wo': _L0_xattn_in['Wo'], 'L0_xattn_bo': _L0_xattn_in['bo'], 'L0_ffn_rw1': _L0_ffn_in['rw1'], 'L0_ffn_rb1': _L0_ffn_in['rb1'], 'L0_ffn_rw2': _L0_ffn_in['rw2'], 'L0_ffn_rb2': _L0_ffn_in['rb2'], 'L0_ffn_ew1': _L0_ffn_in['ew1'], 'L0_ffn_eb1': _L0_ffn_in['eb1'], 'L0_ffn_ew2': _L0_ffn_in['ew2'], 'L0_ffn_eb2': _L0_ffn_in['eb2']}

def reference(x, ctx_1024, mask_Bx1x1xS2_ik0, L0_attn_qkv_w, L0_attn_proj_w, L0_attn_proj_b, L0_attn_slopes, L0_xattn_Wq, L0_xattn_bq, L0_xattn_Wk, L0_xattn_bk, L0_xattn_Wv, L0_xattn_bv, L0_xattn_Wo, L0_xattn_bo, L0_ffn_rw1, L0_ffn_rb1, L0_ffn_rw2, L0_ffn_rb2, L0_ffn_ew1, L0_ffn_eb1, L0_ffn_ew2, L0_ffn_eb2):
    import jax
    import jax.numpy as jnp

    def _L0_attn_ref(x, qkv_w, proj_w, proj_b, slopes):
        import jax, jax.numpy as jnp
        import numpy as np
        import math
        DIM = 256
        NUM_HEADS = 16
        HEAD_DIM = DIM // NUM_HEADS
        MAX_BIAS = 8.0
        SCALE = HEAD_DIM ** (-0.5)

        def _alibi_slopes(n):

            def pow2(n):
                start = 2.0 ** (-2.0 ** (-(math.log2(n) - 3)))
                return [start * start ** i for i in range(n)]
            if math.log2(n).is_integer():
                return pow2(n)
            c = 2 ** math.floor(math.log2(n))
            return pow2(c) + _alibi_slopes(2 * c)[0::2][:n - c]

        def _rotate_half(t):
            t1, t2 = jnp.split(t, 2, axis=-1)
            return jnp.concatenate([-t2, t1], axis=-1)
        B, N, C = x.shape
        H, D = (NUM_HEADS, HEAD_DIM)
        qkv = (x @ qkv_w.T).reshape(B, N, 3, H, D).transpose(2, 0, 3, 1, 4)
        q, k, v = (qkv[0], qkv[1], qkv[2])
        inv_freq = 1.0 / 10000.0 ** (jnp.arange(0, D, 2, dtype=jnp.float32) / D)
        freqs = jnp.arange(N, dtype=jnp.float32)[:, None] * inv_freq[None, :]
        sin = jnp.tile(jnp.sin(freqs), (1, 2))
        cos = jnp.tile(jnp.cos(freqs), (1, 2))
        q = q * cos + _rotate_half(q) * sin
        k = k * cos + _rotate_half(k) * sin
        attn = jnp.einsum('bhqd,bhkd->bhqk', q, k) * SCALE
        pos = jnp.arange(N, dtype=jnp.float32)
        diff = pos[None, :] - pos[:, None]
        diff = jnp.where(diff > 0, 0.0, diff)
        alibi = diff[None, :, :] * slopes[:, None, None] * MAX_BIAS
        attn = attn + alibi[None]
        w = jax.nn.softmax(attn, axis=-1)
        out = jnp.einsum('bhqk,bhkd->bhqd', w, v)
        out = out.transpose(0, 2, 1, 3).reshape(B, N, C)
        return out @ proj_w.T + proj_b

    def _L0_xattn_ref(q, k, v, mask, Wq, bq, Wk, bk, Wv, bv, Wo, bo):
        import jax, jax.numpy as jnp
        import numpy as np
        HEADS = 16
        D_MODEL = 256
        HEAD_DIM = D_MODEL // HEADS
        NEG = -1000000000000000.0

        def _split_heads(x):
            B, L, _ = x.shape
            return x.reshape(B, L, HEADS, HEAD_DIM).transpose(0, 2, 1, 3)
        B, L, _ = q.shape
        qh = _split_heads(q @ Wq.T + bq)
        kh = _split_heads(k @ Wk.T + bk)
        vh = _split_heads(v @ Wv.T + bv)
        scores = jnp.einsum('bhqd,bhkd->bhqk', qh, kh) / jnp.sqrt(jnp.float32(HEAD_DIM))
        scores = scores + mask.astype(scores.dtype) * NEG
        weights = jax.nn.softmax(scores, axis=-1)
        attn = jnp.einsum('bhqk,bhkd->bhqd', weights, vh)
        attn = attn.transpose(0, 2, 1, 3).reshape(B, L, D_MODEL)
        return attn @ Wo.T + bo

    def _L0_ffn_ref(x, rw1, rb1, rw2, rb2, ew1, eb1, ew2, eb2):
        import jax, jax.numpy as jnp
        import numpy as np
        B, T, C, E, K, CAP, H = (8, 512, 256, 8, 2, 1024, 1024)
        Bx, Tx, Cx = x.shape
        N = Bx * Tx
        logits = jax.nn.relu(x @ rw1 + rb1) @ rw2 + rb2
        vals, ids = jax.lax.top_k(logits, K)
        probs = jax.nn.softmax(vals, axis=-1)
        ids_f = ids.reshape(N * K)
        probs_f = probs.reshape(N * K)
        xr = jnp.repeat(x.reshape(N, Cx), K, axis=0)
        m = jax.nn.one_hot(ids_f, E, dtype=jnp.int32)
        pos = jnp.cumsum(m, axis=0) - 1
        pos_tok = jnp.take_along_axis(pos, ids_f[:, None], axis=1)[:, 0]
        keep = (pos_tok < CAP).astype(x.dtype)
        pos_c = jnp.clip(pos_tok, 0, CAP - 1)
        disp = jnp.zeros((E, CAP, Cx), x.dtype).at[ids_f, pos_c].add(xr * keep[:, None])
        h = jax.nn.relu(jnp.einsum('enc,ech->enh', disp, ew1) + eb1[:, None, :])
        eo = jnp.einsum('enh,ehc->enc', h, ew2) + eb2[:, None, :]
        y = eo[ids_f, pos_c] * (probs_f * keep)[:, None]
        return y.reshape(Bx, Tx, K, Cx).sum(axis=2)
    x = _layernorm(x + _L0_attn_ref(x, L0_attn_qkv_w, L0_attn_proj_w, L0_attn_proj_b, L0_attn_slopes), axis=-1)
    x = _layernorm(x + _L0_xattn_ref(x, ctx_1024, ctx_1024, mask_Bx1x1xS2_ik0, L0_xattn_Wq, L0_xattn_bq, L0_xattn_Wk, L0_xattn_bk, L0_xattn_Wv, L0_xattn_bv, L0_xattn_Wo, L0_xattn_bo), axis=-1)
    x = _layernorm(x + _L0_ffn_ref(x, L0_ffn_rw1, L0_ffn_rb1, L0_ffn_rw2, L0_ffn_rb2, L0_ffn_ew1, L0_ffn_eb1, L0_ffn_ew2, L0_ffn_eb2), axis=-1)
    return x

_drawn_inputs = setup_inputs


def setup_inputs(seed=0):
    import zlib

    import numpy as np

    out = dict(_drawn_inputs(seed))
    spreads = {'L0_ffn_rb1': (0.0, 0.1),
     'L0_ffn_rb2': (0.0, 0.1),
     'L0_ffn_eb1': (0.0, 0.335),
     'L0_ffn_eb2': (0.0, 0.1)}
    factors = {'L0_attn_proj_b': 5.184, 'L0_xattn_bq': 3.277, 'L0_xattn_bk': 8.0}
    for name, (base, spread) in spreads.items():
        noise = np.random.default_rng([zlib.crc32(name.encode()), seed]).standard_normal(out[name].shape)
        drawn = base * np.exp(spread * noise) if base else spread * noise
        out[name] = jnp.asarray(drawn.astype(out[name].dtype))
    for name, factor in factors.items():
        out[name] = (out[name] * factor).astype(out[name].dtype)
    return out
```

```python
import numpy as np
import concourse.bass as bass
from concourse import mybir
from contextlib import ExitStack

F32 = mybir.dt.float32
F32R = mybir.dt.float32r
BF16 = mybir.dt.bfloat16
I32 = mybir.dt.int32
U32 = mybir.dt.uint32
ALU = mybir.AluOpType
ACT = mybir.ActivationFunctionType
AX = mybir.AxisListType

P = 128
B, S, C = 4, 1024, 256
T = B * S
TT = T // P
H, D = 16, 16
CK = C // P
CH = 512
TPC = CH // P
HG = 4
NG = B * H // HG
KT = S // P
VW = D + 1


class Scope:

    def __init__(self, nc, stage):
        self.nc, self.stage, self.ctx = nc, stage, ExitStack()

    def __enter__(self):
        self.ctx.__enter__()
        return self

    def __exit__(self, *a):
        return self.ctx.__exit__(*a)

    def sb(self, name, shape, dt):
        return self.ctx.enter_context(self.nc.sbuf_tensor(f"{self.stage}_{name}", shape, dt))

    def pb(self, name, shape=(P, 512), dt=F32):
        return self.ctx.enter_context(self.nc.psum_tensor(f"{self.stage}_{name}", list(shape), dt))

    def sem(self, name):
        return self.ctx.enter_context(self.nc.semaphore(f"{self.stage}_{name}"))

    def block(self):
        return self.ctx.enter_context(self.nc.Block())


def wait_alone(eng, sem, value, apart):
    eng.wait_ge(sem, value)
    eng.sem_inc(apart, 1)


def parts3(hi_a, lo_a, hi_b, lo_b):
    return ((hi_a, hi_b), (hi_a, lo_b), (lo_a, hi_b))


def stage_qkv(nc, io, keep):
    with Scope(nc, "qkv") as s:
        x_all = s.sb("x_all", [P, CK, T], F32)
        w = s.sb("w", [P, CK, 3 * C], F32)
        w_hi = s.sb("w_hi", [P, CK, 3 * C], F32R)
        w_lo = s.sb("w_lo", [P, CK, 3 * C], F32R)
        x_hi = [s.sb(f"x_hi{i}", [P, CK, CH], F32R) for i in range(2)]
        x_lo = [s.sb(f"x_lo{i}", [P, CK, CH], F32R) for i in range(2)]
        rope = s.sb("rope", [P, KT, 2, 2, D], F32)
        ident = s.sb("ident", [P, P], F32)
        y_cos = [s.sb(f"y_cos{i}", [P, 2 * C], F32) for i in range(2)]
        y_sin = [s.sb(f"y_sin{i}", [P, 2 * C], F32) for i in range(2)]
        y = [s.sb(f"y{i}", [P, 2 * C], F32) for i in range(2)]
        t_hi = [[s.sb(f"t_hi{i}{k}", [P, CH], F32R) for k in range(4)] for i in range(2)]
        t_lo = [[s.sb(f"t_lo{i}{k}", [P, CH], F32R) for k in range(4)] for i in range(2)]
        btab = s.sb("btab", [P, S], F32)
        bval = s.sb("bval", [P, S], F32)
        b_hi = s.sb("b_hi", [P, S], F32R)
        b_lo = s.sb("b_lo", [P, S], F32R)
        slope = s.sb("slope", [P, 2], F32)
        qk_ps = [s.pb(f"qk_ps{i}") for i in range(2)]
        v_ps = [s.pb(f"v_ps{i}") for i in range(2)]
        t_ps = [s.pb(f"t_ps{k}") for k in range(4)]

        w_in = s.sem("w_in")
        x_in = [s.sem(f"x_in{c}") for c in range(2)]
        const_in = s.sem("const_in")
        bias_in = s.sem("bias_in")
        w_split = s.sem("w_split")
        xhi_done = s.sem("xhi_done")
        xlo_done = s.sem("xlo_done")
        qkv_done = s.sem("qkv_done")
        rope_done = s.sem("rope_done")
        v_done = s.sem("v_done")
        y_done = s.sem("y_done")
        t_done = s.sem("t_done")
        thi_done = s.sem("thi_done")
        tlo_done = s.sem("tlo_done")
        out_done = [s.sem(f"out_done{i}") for i in range(2)]
        bstep = s.sem("bstep")
        bout = s.sem("bout")
        vones = s.sem("vones")
        block = s.block()

        @block.sync
        def _(sp):
            for c in range(2):
                sp.sem_inc(out_done[c], 256)
            sp.dma_start(w[:, :, :], io["wqkvT"].rearrange("(c p) n -> p c n", p=P)).then_inc(w_in, 16)
            xt = io["xT"].rearrange("(c p) t -> p c t", p=P)
            for half in range(2):
                for q in range(2):
                    n0 = half * (T // 2) + q * (T // 4)
                    sp.dma_start(x_all[:, :, n0:n0 + T // 4], xt[:, :, n0:n0 + T // 4]).then_inc(x_in[half], 16)
                if half == 0:
                    sp.dma_start(rope[:, :, :, :, :], io["rope"]).then_inc(const_in, 16)
                    sp.dma_start(ident[:, :], io["ident"]).then_inc(const_in, 16)
            sp.dma_start(btab[:, :], io["bias_tab"]).then_inc(bias_in, 16)
            sp.dma_start(slope[:, :], io["slope_rep"]).then_inc(bias_in, 16)
            with sp.Fori(0, B) as i:
                for c in range(2):
                    sp.wait_ge(thi_done, 2 * i + c + 1)
                    sp.wait_ge(tlo_done, 2 * i + c + 2)
                    for k in range(4):
                        for part, tile in ((0, t_hi[c][k]), (1, t_lo[c][k])):
                            for r in range(2):
                                g = i * 4 + 2 * (k % 2) + r
                                sp.dma_start(io["qk_scr"][g, part, k // 2, :, c * CH:(c + 1) * CH],
                                             tile[64 * r:64 * r + 64, :].bitcast(F32)).then_inc(out_done[c], 16)
            for half in range(2):
                sp.wait_ge(bstep, 3 * half + 3)
                for part, tile in ((0, b_hi), (1, b_lo)):
                    sp.dma_start(io["bias_scr"][part, half * P:(half + 1) * P, :], tile[:, :].bitcast(F32)).then_inc(bout, 16)
            for c in range(2):
                sp.wait_ge(out_done[c], 256 * B + 256)
            sp.wait_ge(bout, 64)

        @block.gpsimd
        def _(pool):
            pool.sem_inc(y_done, 2)
            pool.memset(keep["v"][:, :, :, :], 1.0).then_inc(vones, 1)
            with pool.Fori(0, B) as i:
                for m in range(8):
                    pool.wait_ge(rope_done, 8 * i + m + 1 + 2)
                    pool.wait_ge(t_done, 8 * i + m + 1)
                    pool.tensor_tensor(y[m % 2][:, :], y_cos[m % 2][:, :], y_sin[m % 2][:, :], ALU.add).then_inc(y_done, 1)
            pool.wait_ge(bias_in, 32)
            for half in range(2):
                pool.tensor_scalar(bval[:, :], btab[:, :], slope[:, half:half + 1], 8.0, ALU.mult, ALU.mult).then_inc(bstep, 1)
                pool.wait_ge(bstep, 3 * half + 1)
                if half:
                    pool.wait_ge(bout, 32)
                pool.tensor_copy(b_hi[:, :], bval[:, :]).then_inc(bstep, 1)
                pool.wait_ge(bstep, 3 * half + 2)
                pool.tensor_tensor(b_lo[:, :], bval[:, :], b_hi[:, :].bitcast(F32), ALU.subtract).then_inc(bstep, 1)
                pool.wait_ge(bstep, 3 * half + 3)

        @block.scalar
        def _(act):
            act.sem_inc(v_done, 2)
            act.wait_ge(w_in, 16)
            nc.scalar.activation(w_hi[:, :, :], w[:, :, :], ACT.Copy).then_inc(w_split, 1)
            act.wait_ge(vones, 1)
            with act.Fori(0, B) as i:
                for c in range(2):
                    for half in range(2):
                        act.wait_ge(x_in[half], 32)
                    act.wait_ge(qkv_done, 8 * i + 4 * c + 4)
                    nc.scalar.activation(x_hi[c][:, :, :], x_all[:, :, bass.ds(i * (2 * CH) + c * CH, CH)],
                                         ACT.Copy).then_inc(xhi_done, 1)
                for m in range(8):
                    act.wait_ge(qkv_done, 8 * i + m + 1 + 8)
                    v_out = keep["v"][:, bass.ds(4 * i, 4), m, :].rearrange("p g (h e) -> p g h e", e=VW)
                    nc.scalar.activation(v_out[:, :, :, 0:D], v_ps[m % 2][:, 0:C].rearrange("p (g h d) -> p g h d", g=4, d=D),
                                         ACT.Copy).then_inc(v_done, 1)
                    if m in (4, 7):
                        c = 0 if m == 4 else 1
                        act.wait_ge(t_done, 8 * i + 4 * c + 4 + 2)
                        act.wait_ge(out_done[c], 256 * i + 256)
                        for k in range(4):
                            ins = nc.scalar.activation(t_hi[c][k][:, :], t_ps[k][:, :], ACT.Copy)
                        ins.then_inc(thi_done, 1)

        @block.vector
        def _(dve):
            dve.sem_inc(rope_done, 2)
            dve.sem_inc(tlo_done, 1)
            dve.wait_ge(w_split, 1)
            nc.vector.tensor_tensor(w_lo[:, :, :], w[:, :, :], w_hi[:, :, :].bitcast(F32), ALU.subtract).then_inc(w_split, 1)
            dve.wait_ge(const_in, 32)
            with dve.Fori(0, B) as i:
                for c in range(2):
                    dve.wait_ge(xhi_done, 2 * i + c + 1)
                    nc.vector.tensor_tensor(x_lo[c][:, :, :], x_all[:, :, bass.ds(i * (2 * CH) + c * CH, CH)],
                                            x_hi[c][:, :, :].bitcast(F32), ALU.subtract).then_inc(xlo_done, 1)
                for m in range(8):
                    dve.wait_ge(qkv_done, 8 * i + m + 1 + 8)
                    dve.wait_ge(y_done, 8 * i + m + 1)
                    qk = qk_ps[m % 2][:, :].rearrange("p (k h d) -> p k h d", k=2, h=H)
                    swapped = qk_ps[m % 2][:, :].rearrange("p (k h s e) -> p k h s e", k=2, h=H, s=2)[:, :, :, ::-1, :]
                    cos = rope[:, m, 0, :, :].unsqueeze(2).to_broadcast([P, 2, H, D])
                    nc.vector.tensor_tensor(y_cos[m % 2][:, :].rearrange("p (k h d) -> p k h d", k=2, h=H), qk, cos, ALU.mult)
                    for k in range(2):
                        sin = rope[:, m, 1, k, :].rearrange("p (s e) -> p s e", s=2).unsqueeze(1).to_broadcast([P, H, 2, D // 2])
                        ins = nc.vector.tensor_tensor(
                            y_sin[m % 2][:, k * C:(k + 1) * C].rearrange("p (h s e) -> p h s e", h=H, s=2),
                            swapped[:, k], sin, ALU.mult)
                    ins.then_inc(rope_done, 1)
                    if m in (4, 7):
                        c = 0 if m == 4 else 1
                        dve.wait_ge(thi_done, 2 * i + c + 1)
                        for k in range(4):
                            ins = nc.vector.tensor_tensor(t_lo[c][k][:, :], t_ps[k][:, :], t_hi[c][k][:, :].bitcast(F32), ALU.subtract)
                        ins.then_inc(tlo_done, 1)

        @block.tensor
        def _(pe):
            pe.sem_inc(qkv_done, 8)
            pe.sem_inc(t_done, 2)
            pe.wait_ge(w_split, 2)
            pe.wait_ge(const_in, 32)

            def transposes(i, m):
                pe.wait_ge(y_done, 8 * i + m + 1 + 2)
                if m % 4 == 0:
                    pe.wait_ge(tlo_done, 2 * i + m // 4 + 1)
                for k in range(4):
                    ins = nc.tensor.transpose(t_ps[k][:, (m % 4) * P:(m % 4 + 1) * P], y[m % 2][:, k * P:(k + 1) * P], ident[:, :])
                ins.then_inc(t_done, 1)

            with pe.Fori(0, B) as i:
                for m in range(8):
                    c = m // 4
                    if m % 4 == 0:
                        pe.wait_ge(xlo_done, 2 * i + c + 1)
                    pe.wait_ge(rope_done, 8 * i + m + 1)
                    pe.wait_ge(v_done, 8 * i + m + 1)
                    tok = slice((m % 4) * P, (m % 4 + 1) * P)
                    for out, cols in ((qk_ps[m % 2][:, :], slice(0, 2 * C)), (v_ps[m % 2][:, 0:C], slice(2 * C, 3 * C))):
                        prods = [(a[:, kc, tok], b[:, kc, cols]) for kc in range(CK)
                                 for a, b in parts3(x_hi[c], x_lo[c], w_hi, w_lo)]
                        for n, (a, b) in enumerate(prods):
                            ins = nc.tensor.matmul(out, a, b, start=(n == 0), stop=(n == len(prods) - 1))
                    ins.then_inc(qkv_done, 1)
                    if m:
                        transposes(i, m - 1)
                transposes(i, 7)


class Group:

    def __init__(self, n, buf, lap):
        self.n, self.buf, self.lap = n, buf, lap

    @staticmethod
    def of(n):
        return Group(n, n % 3, n // 3)

    def plus(self, k):
        if isinstance(self.n, int):
            return Group.of(self.n + k)
        b = self.buf + k
        return Group(self.n + k, b % 3, self.lap + b // 3)


def windows(eng, window):
    window(Group.of(0), True, False)
    with eng.Fori(0, 4) as i:
        for u in range(3):
            g = Group(3 * i + (u + 1), (u + 1) % 3, i + (u + 1) // 3)
            window(g, True, True)
    for n in range(13, NG):
        window(Group.of(n), n < NG - 1, True)


STEPS = 2 * KT
ROW_BIAS, ROW_MAX, ROWS = 64, 96, P


def stage_attention(nc, io, keep):
    with Scope(nc, "att") as s:
        qs = [s.sb(f"q_stack{i}", [P, HG, S], F32R) for i in range(3)]
        ks = [s.sb(f"k_stack{i}", [P, HG, S], F32R) for i in range(3)]
        vg = [s.sb(f"v_group{i}", [P, KT, HG * VW + 32 - VW + 1], F32) for i in range(3)]
        w_exp = [[s.sb(f"w_exp{i}{h}", [P, CH], F32) for h in range(HG)] for i in range(2)]
        min_mat = s.sb("min_mat", [P, P], F32)
        min_bf = s.sb("min_bf", [P, P], BF16)
        ident = s.sb("ident", [P, P], F32)
        slope8 = s.sb("slope8", [P, H], F32)
        slope_eye = s.sb("slope_eye", [P, H, P], BF16)
        zeros = s.sb("zeros", [P, 8 * C], F32)
        row_max = [s.sb(f"row_max{i}", [P, HG * 4, 2], F32) for i in range(2)]
        top = s.sb("top", [P, HG * 4], F32)
        neg_top = s.sb("neg_top", [P, 2, HG * 4], F32R)
        neg_top_t = [s.sb(f"neg_top_t{i}", [32, P], F32R) for i in range(2)]
        acc_sb = [s.sb(f"acc_sb{i}", [P, CH], F32) for i in range(2)]
        recip = s.sb("recip", [P, 4, HG], F32)
        att = [s.sb(f"att{i}", [P, 4, HG, D], F32) for i in range(2)]
        s_ps = [s.pb(f"s_ps{h}") for h in range(HG)]
        m_ps = [s.pb(f"m_ps{i}") for i in range(2)]
        a_ps = [s.pb(f"a_ps{i}") for i in range(2)]

        const_in = s.sem("const_in")
        prep = s.sem("prep")
        stack_in = [s.sem(f"stack_in{i}") for i in range(3)]
        top_in = [s.sem(f"top_in{i}") for i in range(2)]
        top_out = [s.sem(f"top_out{i}") for i in range(2)]
        score_done = s.sem("score_done")
        diag_done = s.sem("diag_done")
        exp_done = s.sem("exp_done")
        pv_done = s.sem("pv_done")
        acc_done = s.sem("acc_done")
        acc_t = s.sem("acc_t")
        recip_done = s.sem("recip_done")
        norm_done = s.sem("norm_done")
        att_out = [s.sem(f"att_out{i}") for i in range(2)]
        mm_done = s.sem("mm_done")
        max_done = s.sem("max_done")
        top_step = s.sem("top_step")
        top_ready = s.sem("top_ready")
        top_t = s.sem("top_t")
        top_copied = s.sem("top_copied")
        v_ready = s.sem("v_ready")
        pool_prep = s.sem("pool_prep")
        zeroed = s.sem("zeroed")
        block = s.block()

        def load_stacks(sp, g):
            b = g.buf
            for part, qk, tile, row in ((0, 0, qs, 0), (0, 0, qs, 16), (1, 0, qs, 32), (0, 1, ks, 0), (1, 1, ks, 16), (0, 1, ks, 32)):
                src = io["qk_scr"][bass.ds(g.n, 1), part, qk].rearrange("o (h d) t -> (o d) h t", d=D)
                sp.dma_start(tile[b][row:row + D, :, :].bitcast(F32), src).then_inc(stack_in[b], 16)
            for part in range(2):
                src = io["bias_scr"][part].rearrange("(h r) t -> r h t", r=16)[:, bass.ds((g.n % HG) * HG, HG), :]
                sp.dma_start(ks[b][ROW_BIAS + 16 * part:ROW_BIAS + 16 * part + 16, :, :].bitcast(F32), src).then_inc(stack_in[b], 16)

        def move_top(sp, g, half):
            sp.wait_ge(top_copied, 2 * g.n + half + 1)
            sp.dma_start(io["top_scr"][half], neg_top_t[half][:, :].bitcast(F32)).then_inc(top_out[half], 16)
            sp.wait_ge(top_out[half], 16 * g.n + 32)
            sp.dma_start(qs[g.buf][ROW_MAX:ROW_MAX + 2, :, half * CH:(half + 1) * CH].bitcast(F32),
                         io["top_scr"][half].rearrange("(a h q) t -> a h (q t)", a=2, h=HG)).then_inc(top_in[half], 16)

        def store_att(sp, g, c):
            sp.wait_ge(norm_done, 2 * g.n + c + 1 + 2)
            sp.dma_start(io["att_scr"][bass.ds(g.n, 1), :, 4 * c:4 * c + 4, :].rearrange("o p q e -> (o p) q e"),
                         att[c][:, :, :, :].rearrange("p q h d -> p q (h d)")).then_inc(att_out[c], 16)

        @block.sync
        def _(sp):
            for half in range(2):
                sp.sem_inc(top_out[half], 16)
                sp.sem_inc(att_out[half], 16)
            sp.dma_start(min_mat[:, :], io["min_mat"]).then_inc(const_in, 16)
            sp.dma_start(ident[:, :], io["ident"]).then_inc(const_in, 16)
            sp.dma_start(slope8[:, :], io["slopes"].partition_broadcast(P)).then_inc(const_in, 16)
            for i in range(2):
                sp.dma_start(w_exp[0][i][ROW_BIAS:ROW_MAX, :], io["q_rows"][:, i * CH:(i + 1) * CH]).then_inc(const_in, 16)
            sp.wait_ge(prep, 1)
            load_stacks(sp, Group.of(0))
            load_stacks(sp, Group.of(1))
            move_top(sp, Group.of(0), 0)
            move_top(sp, Group.of(0), 1)

            def window(g, with_max, has_last):
                if has_last:
                    sp.wait_ge(score_done, 64 * g.n)
                if not isinstance(g.n, int) or 1 <= g.n < NG - 2:
                    load_stacks(sp, g.plus(2))
                if isinstance(g.n, int) and g.n == 0:
                    load_stacks(sp, g.plus(2))
                if has_last:
                    store_att(sp, g.plus(-1), 1)
                if with_max:
                    move_top(sp, g.plus(1), 0)
                store_att(sp, g, 0)
                if with_max:
                    move_top(sp, g.plus(1), 1)

            windows(sp, window)
            store_att(sp, Group.of(NG - 1), 1)
            for c in range(2):
                sp.wait_ge(att_out[c], 16 * NG + 16)

        @block.gpsimd
        def _(pool):
            pool.memset(zeros[:, :], 0.0).then_inc(pool_prep, 1)
            pool.wait_ge(pool_prep, 1)
            rows = io["rows_scr"].rearrange("(a p r) e -> a p (r e)", a=8, p=P)
            for a in range(8):
                pool.dma_start(rows[a], zeros[:, :]).then_inc(zeroed, 16)
            for i in range(3):
                pool.memset(vg[i][:, :, :], 0.0).then_inc(pool_prep, 1)
            pool.wait_ge(pool_prep, 4)

            def take_v(g):
                dst = vg[g.buf][:, :, 0:HG * VW].unsqueeze(1)
                pool.tensor_copy(dst, keep["v"][:, bass.ds(g.n, 1), :, :]).then_inc(v_ready, 1)

            take_v(Group.of(0))

            def window(g, with_max, has_last):
                if with_max:
                    if has_last:
                        pool.wait_ge(pv_done, STEPS * (g.n - 1) + 2)
                    take_v(g.plus(1))

            windows(pool, window)
            pool.wait_ge(zeroed, 128)

        @block.scalar
        def _(act):
            act.sem_inc(exp_done, 4)
            def copy_acc(g, c):
                act.wait_ge(pv_done, STEPS * g.n + KT * (c + 1) + 2)
                act.wait_ge(acc_t, 2 * g.n + c + 1)
                nc.scalar.activation(acc_sb[c][:, :], a_ps[c][:, :], ACT.Copy).then_inc(acc_done, 1)

            def window(g, with_max, has_last):
                for st in range(STEPS):
                    c, kt = divmod(st, KT)
                    for h in range(HG):
                        if kt // 4 == c:
                            f = 4 * st + h if c == 0 else 16 + 4 * (st - 12) + h
                            act.wait_ge(diag_done, 32 * g.n + f + 1)
                        else:
                            act.wait_ge(score_done, 64 * g.n + 4 * st + h + 1)
                        if h == 0:
                            act.wait_ge(pv_done, STEPS * g.n + st + 1)
                        nc.scalar.activation(w_exp[st % 2][h][:, :], s_ps[h][:, :], ACT.Exp).then_inc(exp_done, 1)
                    if st == 1 and has_last:
                        copy_acc(g.plus(-1), 1)
                    if st == 9:
                        copy_acc(g, 0)

            windows(act, window)
            copy_acc(Group.of(NG - 1), 1)

        @block.vector
        def _(dve):
            for sem, n in ((max_done, 2), (norm_done, 2)):
                dve.sem_inc(sem, n)
            for i in range(3):
                nc.vector.memset(qs[i][:, :, :].bitcast(F32), 0.0)
                ins = nc.vector.memset(ks[i][:, :, :].bitcast(F32), 0.0)
            ins.then_inc(top_step, 1)
            dve.wait_ge(top_step, 1)
            dve.wait_ge(const_in, 80)
            for i in range(3):
                for h in range(HG):
                    for c in range(2):
                        nc.vector.tensor_copy(qs[i][ROW_BIAS:ROW_MAX, h, c * CH:(c + 1) * CH], w_exp[0][c][ROW_BIAS:ROW_MAX, :])
                nc.vector.memset(ks[i][ROW_MAX:ROW_MAX + 2, :, :].bitcast(F32), 1.0)
            nc.vector.tensor_copy(min_bf[:, :], min_mat[:, :])
            nc.vector.tensor_scalar(slope8[:, :], slope8[:, :], 8.0, None, ALU.mult).then_inc(top_step, 1)
            dve.wait_ge(top_step, 2)
            for h in range(H):
                ins = nc.vector.tensor_scalar(slope_eye[:, h, :], ident[:, :], slope8[:, h:h + 1], None, ALU.mult)
            ins.then_inc(prep, 1)

            def maxima(g, u):
                dve.wait_ge(mm_done, 64 * g.n + u + 1)
                half, v = divmod(u, 32)
                nc.vector.tensor_reduce(row_max[half][:, v // 2, v % 2:v % 2 + 1], m_ps[u % 2][:, :], AX.X, ALU.max).then_inc(max_done, 1)

            def top_parts(g, half):
                dve.wait_ge(max_done, 64 * g.n + 32 * half + 32 + 2)
                nc.vector.tensor_reduce(top[:, :], row_max[half][:, :, :], AX.X, ALU.max).then_inc(top_step, 1)
                dve.wait_ge(top_step, 2 + 4 * g.n + 2 * half + 1)
                if not (isinstance(g.n, int) and g.n == 0 and half == 0):
                    dve.wait_ge(top_t, 2 * g.n + half)
                nc.vector.tensor_scalar(neg_top[:, 0, :], top[:, :], -1.0, None, ALU.mult).then_inc(top_step, 1)
                dve.wait_ge(top_step, 2 + 4 * g.n + 2 * half + 2)
                nc.vector.scalar_tensor_tensor(neg_top[:, 1, :], top[:, :], -1.0, neg_top[:, 0, :].bitcast(F32),
                                               ALU.mult, ALU.subtract).then_inc(top_ready, 1)

            def copy_top(g, half):
                dve.wait_ge(top_t, 2 * g.n + half + 1)
                dve.wait_ge(top_out[half], 16 * g.n + 16)
                nc.vector.tensor_copy(neg_top_t[half][:, :], m_ps[0][0:32, 0:P]).then_inc(top_copied, 1)

            def normalise(g, c):
                dve.wait_ge(acc_t, 2 * g.n + c + 1 + 2)
                sums = a_ps[c][:, :].rearrange("p (q h e) -> p q h e", q=4, h=HG)
                nc.vector.reciprocal(recip[:, :, :], sums[:, :, :, D]).then_inc(recip_done, 1)
                dve.wait_ge(recip_done, 2 * g.n + c + 1)
                dve.wait_ge(att_out[c], 16 * g.n + 16)
                nc.vector.tensor_tensor(att[c][:, :, :, :], sums[:, :, :, 0:D],
                                        recip[:, :, :].unsqueeze(3).to_broadcast([P, 4, HG, D]), ALU.mult).then_inc(norm_done, 1)

            g0 = Group.of(0)
            for u in range(64):
                maxima(g0, u)
                if u % 32 == 31:
                    top_parts(g0, u // 32)
                    copy_top(g0, u // 32)

            def window(g, with_max, has_last):
                for st in range(STEPS):
                    c, kt = divmod(st, KT)
                    for h in range(HG):
                        if kt // 4 == c:
                            dve.wait_ge(score_done, 64 * g.n + 4 * st + h + 1)
                            d = s_ps[h][:, (kt % 4) * P:(kt % 4 + 1) * P]
                            slope = slope8[:, bass.ds((g.n % HG) * HG + h, 1)]
                            nc.vector.scalar_tensor_tensor(d, min_mat[:, :], slope, d, ALU.mult, ALU.add).then_inc(diag_done, 1)
                        if with_max:
                            maxima(g.plus(1), 4 * st + h)
                    if st == 2 and has_last:
                        normalise(g.plus(-1), 1)
                    if st == 11:
                        normalise(g, 0)
                    if with_max and st % 8 == 7:
                        top_parts(g.plus(1), st // 8)
                        copy_top(g.plus(1), st // 8)

            windows(dve, window)
            normalise(Group.of(NG - 1), 1)

        @block.tensor
        def _(pe):
            pe.sem_inc(pv_done, 2)
            pe.sem_inc(acc_t, 2)
            pe.wait_ge(prep, 1)

            def max_scores(g, u):
                half, v = divmod(u, 32)
                h, v = divmod(v, 8)
                qt, kk = half * 4 + v // 2, v % 2
                pe.wait_ge(max_done, 64 * g.n + u + 1)
                if u in (0, 32) and not (isinstance(g.n, int) and g.n == 0 and u == 0):
                    pe.wait_ge(top_copied, 2 * g.n + half)
                diag = qt // 4 == kk
                out = m_ps[kk]
                ins = nc.tensor.matmul(out[:, :], qs[g.buf][0:ROW_MAX, h, qt * P:(qt + 1) * P],
                                       ks[g.buf][0:ROW_MAX, h, kk * CH:(kk + 1) * CH], start=True, stop=not diag)
                if diag:
                    ins = nc.tensor.matmul(out[:, (qt % 4) * P:(qt % 4 + 1) * P], min_bf[:, :],
                                           slope_eye[:, bass.ds((g.n % HG) * HG + h, 1), :].rearrange("p o q -> p (o q)"),
                                           start=False, stop=True)
                ins.then_inc(mm_done, 1)

            def transpose_top(g, half):
                pe.wait_ge(top_ready, 2 * g.n + half + 1)
                nc.tensor.transpose(m_ps[0][0:32, 0:P], neg_top[:, :, :].rearrange("p a b -> p (a b)").bitcast(F32), ident[:, :]).then_inc(top_t, 1)

            def values(g, st):
                c, kt = divmod(st, KT)
                pe.wait_ge(exp_done, 64 * g.n + 4 * st + 4 + 4)
                if st == 0:
                    pe.wait_ge(v_ready, g.n + 1)
                if kt == 0:
                    pe.wait_ge(norm_done, 2 * g.n + c + 1)
                for h in range(HG):
                    ins = nc.tensor.matmul(a_ps[c][32 * h:32 * h + 32, :], vg[g.buf][:, kt, h * VW:h * VW + 32],
                                           w_exp[st % 2][h][:, :], start=(kt == 0), stop=(kt == KT - 1))
                ins.then_inc(pv_done, 1)

            def transpose_acc(g, c):
                pe.wait_ge(acc_done, 2 * g.n + c + 1)
                for q in range(4):
                    ins = nc.tensor.transpose(a_ps[c][:, q * P:(q + 1) * P], acc_sb[c][:, q * P:(q + 1) * P], ident[:, :])
                ins.then_inc(acc_t, 1)

            g0 = Group.of(0)
            pe.wait_ge(stack_in[0], 128)
            for u in range(64):
                max_scores(g0, u)
                if u % 32 == 31:
                    transpose_top(g0, u // 32)

            def window(g, with_max, has_last):
                if with_max:
                    n = g.plus(1)
                    pe.wait_ge(stack_in[n.buf], 128 * n.lap + 128)
                for st in range(STEPS):
                    c, kt = divmod(st, KT)
                    if kt == 0:
                        pe.wait_ge(top_in[c], 16 * g.n + 16)
                    for h in range(HG):
                        pe.wait_ge(exp_done, 64 * g.n + 4 * st + h + 1)
                        nc.tensor.matmul(s_ps[h][:, :], ks[g.buf][:, h, kt * P:(kt + 1) * P],
                                         qs[g.buf][:, h, c * CH:(c + 1) * CH], start=True, stop=True).then_inc(score_done, 1)
                        if with_max:
                            max_scores(n, 4 * st + h)
                    if st:
                        values(g, st - 1)
                    elif has_last:
                        values(g.plus(-1), STEPS - 1)
                    if st == 2 and has_last:
                        transpose_acc(g.plus(-1), 1)
                    if st == 10:
                        transpose_acc(g, 0)
                    if with_max and st % 8 == 7:
                        transpose_top(n, st // 8)

            windows(pe, window)
            last = Group.of(NG - 1)
            values(last, STEPS - 1)
            transpose_acc(last, 1)

EPS = 1e-5


class Norm:

    def __init__(self, nc, s, apart):
        self.nc, self.apart = nc, apart
        self.stats = s.sb("stats", [P, TPC, 6], F32)
        self.mv = s.sb("mv", [P, TPC, 2], F32)
        self.var = s.sb("var", [P, TPC, 1], F32)
        self.root = s.sb("root", [P, TPC, 1], F32)
        self.inv = s.sb("inv", [P, TPC, 1], F32)
        self.half = s.sb("half", [P, TPC, 1], F32)
        self.step = s.sem("norm_step")
        self.root_done = s.sem("root_done")

    def apply(self, dve, n, x, out):
        nc, at = self.nc, 7 * n
        for t in range(TPC):
            ins = nc.vector.bn_stats(self.stats[:, t, :], x[:, t, :])
        ins.then_inc(self.step, 1)
        wait_alone(dve, self.step, at + 1, self.apart)
        for t in range(TPC):
            ins = nc.vector.bn_aggr(self.mv[:, t, :], self.stats[:, t, :])
        ins.then_inc(self.step, 1)
        dve.wait_ge(self.step, at + 2)
        nc.vector.tensor_scalar(self.var[:, :, :], self.mv[:, :, 1:2], EPS, None, ALU.add).then_inc(self.step, 1)
        dve.wait_ge(self.root_done, n + 1)
        nc.vector.reciprocal(self.inv[:, :, :], self.root[:, :, :]).then_inc(self.step, 1)
        dve.wait_ge(self.step, at + 4)
        nc.vector.scalar_tensor_tensor(self.half[:, :, :], self.inv[:, :, :], -0.5, self.var[:, :, :], ALU.mult, ALU.mult).then_inc(self.step, 1)
        dve.wait_ge(self.step, at + 5)
        nc.vector.tensor_tensor(self.half[:, :, :], self.half[:, :, :], self.inv[:, :, :], ALU.mult).then_inc(self.step, 1)
        dve.wait_ge(self.step, at + 6)
        nc.vector.scalar_tensor_tensor(self.inv[:, :, :], self.half[:, :, :], 1.5, self.inv[:, :, :], ALU.add, ALU.mult).then_inc(self.step, 1)
        dve.wait_ge(self.step, at + 7)
        for t in range(TPC):
            ins = nc.vector.tensor_scalar(out[:, t, :], x[:, t, :], self.mv[:, t, 0:1], self.inv[:, t, :], ALU.subtract, ALU.mult)
        return ins

    def take_root(self, act, n):
        act.wait_ge(self.step, 7 * n + 3)
        self.nc.scalar.activation(self.root[:, :, :], self.var[:, :, :], ACT.Sqrt).then_inc(self.root_done, 1)


def stage_self_out(nc, io):
    with Scope(nc, "so") as s:
        w_raw = s.sb("w_raw", [P, 2, CK, C], F32)
        w_hi = s.sb("w_hi", [P, 2, CK, C], F32R)
        w_lo = s.sb("w_lo", [P, 2, CK, C], F32R)
        proj_b = s.sb("proj_b", [P, C], F32)
        bq = s.sb("bq", [P, CK], F32)
        ident = s.sb("ident", [P, P], F32)
        att = [s.sb(f"att{i}", [P, TPC, C], F32) for i in range(2)]
        x = [s.sb(f"x{i}", [P, TPC, C], F32) for i in range(2)]
        a_hi = [s.sb(f"a_hi{i}", [P, CK, CH], F32R) for i in range(2)]
        a_lo = [s.sb(f"a_lo{i}", [P, CK, CH], F32R) for i in range(2)]
        res = [s.sb(f"res{i}", [P, TPC, C], F32) for i in range(2)]
        x1 = [s.sb(f"x1{i}", [P, TPC, C], F32) for i in range(2)]
        x1_hi = [s.sb(f"x1_hi{i}", [P, CK, CH], F32R) for i in range(2)]
        x1_lo = [s.sb(f"x1_lo{i}", [P, CK, CH], F32R) for i in range(2)]
        q_sum = [s.sb(f"q_sum{i}", [P, CK, CH], F32) for i in range(2)]
        q_hi = [s.sb(f"q_hi{i}", [P, CK, CH], F32R) for i in range(2)]
        q_lo = [s.sb(f"q_lo{i}", [P, CK, CH], F32R) for i in range(2)]
        norm = Norm(nc, s, io["apart"])
        t_ps = s.pb("t_ps", (P, CK, CH))
        r_ps = s.pb("r_ps", (P, TPC, C))
        t1_ps = s.pb("t1_ps", (P, CK, CH))
        q_ps = s.pb("q_ps", (P, CK, CH))

        const_in = s.sem("const_in")
        w_split = s.sem("w_split")
        in_done = [s.sem(f"in_done{i}") for i in range(2)]
        t_done, t_hi, t_lo = s.sem("t_done"), s.sem("t_hi"), s.sem("t_lo")
        r_done, x_biased = s.sem("r_done"), s.sem("x_biased")
        res_done, x1_done = s.sem("res_done"), s.sem("x1_done")
        t1_done, x1_hi_done, x1_lo_done = s.sem("t1_done"), s.sem("x1_hi_done"), s.sem("x1_lo_done")
        q_done, q_sum_done = s.sem("q_done"), s.sem("q_sum_done")
        q_hi_done, q_lo_done = s.sem("q_hi_done"), s.sem("q_lo_done")
        out_done = [s.sem(f"out_done{i}") for i in range(2)]
        block = s.block()

        @block.sync
        def _(sp):
            for j, name in enumerate(("projT", "wqT")):
                sp.dma_start(w_raw[:, j], io[name].rearrange("(c p) n -> p c n", p=P)).then_inc(const_in, 16)
            sp.dma_start(ident[:, :], io["ident"]).then_inc(const_in, 16)
            sp.dma_start(proj_b[:, :], io["proj_b"].partition_broadcast(P)).then_inc(const_in, 16)
            sp.dma_start(bq[:, :], io["bq2"]).then_inc(const_in, 16)
            for c in range(2):
                sp.sem_inc(out_done[c], 48)
            def load(i, c):
                n = 2 * i + c
                sp.wait_ge(r_done, n + 1)
                sp.wait_ge(res_done, n + 1)
                for hq in range(4):
                    src = io["att_scr"][bass.ds(4 * i + hq, 1), :, 4 * c:4 * c + 4, :].rearrange("o p q e -> (o p) q e")
                    sp.dma_start(att[c][:, :, hq * 64:hq * 64 + 64], src).then_inc(in_done[c], 16)
                sp.dma_start(x[c][:, :, :], io["x"].rearrange("(n t p) e -> n p t e", p=P, t=TPC)[n]).then_inc(in_done[c], 16)

            def store(i, c):
                n = 2 * i + c
                sp.wait_ge(x1_done, n + 1 + 2)
                sp.dma_start(io["x1_scr"].rearrange("(n t p) e -> n p t e", p=P, t=TPC)[n], x1[c][:, :, :]).then_inc(out_done[c], 16)
                sp.wait_ge(q_lo_done, n + 1 + 2)
                for part, tile in ((0, q_hi[c]), (1, q_lo[c])):
                    sp.dma_start(io["q2_scr"][n, part].rearrange("k p t -> p k t"), tile[:, :, :].bitcast(F32)).then_inc(out_done[c], 16)

            load(0, 0)
            load(0, 1)
            with sp.Fori(0, B - 1) as i:
                for c in range(2):
                    load(i + 1, c)
                for c in range(2):
                    store(i, c)
            for c in range(2):
                store(B - 1, c)
            for c in range(2):
                sp.wait_ge(out_done[c], 48 * B + 48)

        @block.gpsimd
        def _(pool):
            pool.wait_ge(const_in, 80)
            with pool.Fori(0, B) as i:
                for c in range(2):
                    n = 2 * i + c
                    pool.wait_ge(in_done[c], 80 * i + 80)
                    pool.tensor_tensor(x[c][:, :, :], x[c][:, :, :], proj_b[:, :].unsqueeze(1).to_broadcast([P, TPC, C]), ALU.add).then_inc(x_biased, 1)

        @block.scalar
        def _(act):
            act.sem_inc(t_hi, 1)
            act.sem_inc(x1_hi_done, 1)
            act.wait_ge(const_in, 80)
            nc.scalar.activation(w_hi[:, :, :, :], w_raw[:, :, :, :], ACT.Copy).then_inc(w_split, 1)
            with act.Fori(0, B) as i:
                def split_att(c):
                    n = 2 * i + c
                    act.wait_ge(t_done, n + 1)
                    act.wait_ge(r_done, n + 1)
                    nc.scalar.activation(a_hi[c][:, :, :], t_ps[:, :, :], ACT.Copy).then_inc(t_hi, 1)

                def split_x1(c):
                    n = 2 * i + c
                    act.wait_ge(t1_done, n + 1)
                    act.wait_ge(q_done, n + 1)
                    nc.scalar.activation(x1_hi[c][:, :, :], t1_ps[:, :, :], ACT.Copy).then_inc(x1_hi_done, 1)

                def split_q(c):
                    n = 2 * i + c
                    act.wait_ge(q_sum_done, n + 1 + 1)
                    act.wait_ge(out_done[c], 48 * i + 48)
                    nc.scalar.activation(q_hi[c][:, :, :], q_sum[c][:, :, :], ACT.Copy).then_inc(q_hi_done, 1)

                split_att(0)
                split_att(1)
                for c in range(2):
                    norm.take_root(act, 2 * i + c)
                split_x1(0)
                split_q(0)
                split_x1(1)
                split_q(1)

        @block.vector
        def _(dve):
            dve.sem_inc(t_lo, 1)
            dve.sem_inc(x1_lo_done, 1)
            dve.sem_inc(q_sum_done, 1)
            dve.sem_inc(res_done, 2)
            dve.sem_inc(x1_done, 2)
            dve.sem_inc(q_lo_done, 2)
            dve.wait_ge(w_split, 1)
            nc.vector.tensor_tensor(w_lo[:, :, :, :], w_raw[:, :, :, :], w_hi[:, :, :, :].bitcast(F32), ALU.subtract).then_inc(w_split, 1)
            with dve.Fori(0, B) as i:
                def split_att(c):
                    dve.wait_ge(t_hi, 2 * i + c + 1 + 1)
                    nc.vector.tensor_tensor(a_lo[c][:, :, :], t_ps[:, :, :], a_hi[c][:, :, :].bitcast(F32), ALU.subtract).then_inc(t_lo, 1)

                def normalise(c):
                    n = 2 * i + c
                    dve.wait_ge(r_done, n + 1 + 2)
                    dve.wait_ge(x_biased, n + 1)
                    nc.vector.tensor_tensor(res[c][:, :, :], r_ps[:, :, :], x[c][:, :, :], ALU.add).then_inc(res_done, 1)
                    dve.wait_ge(res_done, n + 1 + 2)
                    dve.wait_ge(out_done[c], 48 * i + 48)
                    norm.apply(dve, n, res[c], x1[c]).then_inc(x1_done, 1)

                def split_x1(c):
                    dve.wait_ge(x1_hi_done, 2 * i + c + 1 + 1)
                    nc.vector.tensor_tensor(x1_lo[c][:, :, :], t1_ps[:, :, :], x1_hi[c][:, :, :].bitcast(F32), ALU.subtract).then_inc(x1_lo_done, 1)

                def bias_q(c):
                    n = 2 * i + c
                    dve.wait_ge(q_done, n + 1 + 2)
                    for k in range(CK):
                        ins = nc.vector.tensor_scalar(q_sum[c][:, k, :], q_ps[:, k, :], bq[:, k:k + 1], float(D) ** -0.5, ALU.add, ALU.mult)
                    ins.then_inc(q_sum_done, 1)

                def split_q(c):
                    n = 2 * i + c
                    dve.wait_ge(q_hi_done, n + 1)
                    nc.vector.tensor_tensor(q_lo[c][:, :, :], q_sum[c][:, :, :], q_hi[c][:, :, :].bitcast(F32), ALU.subtract).then_inc(q_lo_done, 1)

                split_att(0)
                split_att(1)
                normalise(0)
                normalise(1)
                split_x1(0)
                bias_q(0)
                split_x1(1)
                split_q(0)
                bias_q(1)
                split_q(1)

        @block.tensor
        def _(pe):
            pe.sem_inc(r_done, 2)
            pe.sem_inc(q_done, 2)
            pe.wait_ge(w_split, 2)
            pe.wait_ge(const_in, 80)

            def transpose(i, c, src, dst):
                for t in range(TPC):
                    for k in range(CK):
                        ins = nc.tensor.transpose(dst[:, k, t * P:(t + 1) * P], src[:, t, k * P:(k + 1) * P], ident[:, :])
                return ins

            with pe.Fori(0, B) as i:
                def transpose_att(c):
                    pe.wait_ge(in_done[c], 80 * i + 80)
                    pe.wait_ge(t_lo, 2 * i + c + 1)
                    transpose(i, c, att[c], t_ps).then_inc(t_done, 1)

                def project(c):
                    n = 2 * i + c
                    pe.wait_ge(t_lo, n + 1 + 1)
                    pe.wait_ge(res_done, n + 2)
                    for t in range(TPC):
                        prods = [(a[:, k, t * P:(t + 1) * P], b[:, 0, k, :]) for k in range(CK)
                                 for a, b in parts3(a_hi[c], a_lo[c], w_hi, w_lo)]
                        for m, (a, b) in enumerate(prods):
                            ins = nc.tensor.matmul(r_ps[:, t, :], a, b, start=(m == 0), stop=(m == len(prods) - 1))
                    ins.then_inc(r_done, 1)

                def transpose_x1(c):
                    n = 2 * i + c
                    pe.wait_ge(x1_done, n + 1 + 2)
                    pe.wait_ge(x1_lo_done, n + 1)
                    transpose(i, c, x1[c], t1_ps).then_inc(t1_done, 1)

                def queries(c):
                    n = 2 * i + c
                    pe.wait_ge(x1_lo_done, n + 1 + 1)
                    pe.wait_ge(q_sum_done, n + 1)
                    for m in range(CK):
                        prods = [(b[:, 1, k, m * P:(m + 1) * P], a[:, k, :]) for k in range(CK)
                                 for a, b in parts3(x1_hi[c], x1_lo[c], w_hi, w_lo)]
                        for j, (a, b) in enumerate(prods):
                            ins = nc.tensor.matmul(q_ps[:, m, :], a, b, start=(j == 0), stop=(j == len(prods) - 1))
                    ins.then_inc(q_done, 1)

                transpose_att(0)
                transpose_att(1)
                project(0)
                project(1)
                transpose_x1(0)
                queries(0)
                transpose_x1(1)
                queries(1)


L = 77
HL = H // CK
GL = HG * L
NEG = -1000000000000000.0


def stage_cross(nc, io):
    with Scope(nc, "cr") as s:
        ctx = s.sb("ctx", [P, CK, B * L], F32)
        ctx_hi = s.sb("ctx_hi", [P, CK, B * L], F32R)
        ctx_lo = s.sb("ctx_lo", [P, CK, B * L], F32R)
        kv_raw = s.sb("kv_raw", [P, 2, CK, C], F32)
        kv_hi = s.sb("kv_hi", [P, 2, CK, C], F32R)
        kv_lo = s.sb("kv_lo", [P, 2, CK, C], F32R)
        bk = s.sb("bk", [P, CK], F32)
        bv = s.sb("bv", [P, C], F32)
        head_of = s.sb("head_of", [P, HL], F32)
        k_sum = s.sb("k_sum", [P, CK, B * L], F32)
        k_hi = s.sb("k_hi", [P, CK, B * L], F32)
        k_lo = s.sb("k_lo", [P, CK, B * L], F32)
        k_blk = s.sb("k_blk", [P, 2, B, CK, HL * L], F32R)
        v_all = s.sb("v_all", [L, B, C + D], F32)
        v_now = s.sb("v_now", [L, C + D], F32)
        mask_i = s.sb("mask_i", [P, B * L], I32)
        mask_f = s.sb("mask_f", [P, B * L], F32)
        mask_w = s.sb("mask_w", [P, B, HG, L], F32R)
        mask_sel = s.sb("mask_sel", [P, P], F32R)
        wo_raw = s.sb("wo_raw", [P, HG, C], F32)
        wo_hi = s.sb("wo_hi", [P, HG, C], F32R)
        wo_lo = s.sb("wo_lo", [P, HG, C], F32R)
        bo = s.sb("bo", [P, C], F32)
        ident = s.sb("ident", [P, P], F32)
        q = [[s.sb(f"q{c}{part}", [P, CK, CH], F32R) for part in range(2)] for c in range(2)]
        x1 = [s.sb(f"x1{c}", [P, TPC, C], F32) for c in range(2)]
        e = [s.sb(f"e{i}", [P, H, L], F32) for i in range(2)]
        w = s.sb("w", [P, H, L], F32)
        w_t = s.sb("w_t", [L, H, CH], F32)
        top = [s.sb(f"top{i}", [P, H], F32) for i in range(2)]
        tot = [s.sb(f"tot{i}", [P, H], F32) for i in range(2)]
        rec = [s.sb(f"rec{i}", [P, H], F32) for i in range(2)]
        o_hi = s.sb("o_hi", [P, HG, CH], F32R)
        o_lo = s.sb("o_lo", [P, HG, CH], F32R)
        res = s.sb("res", [P, TPC, C], F32)
        x2 = [s.sb(f"x2{c}", [P, TPC, C], F32) for c in range(2)]
        norm = Norm(nc, s, io["apart"])
        s_ps = s.pb("s_ps", (P, HG, 512))
        t_ps = s.pb("t_ps", (P, HG, 512))

        ctx_in, const_in = s.sem("ctx_in"), s.sem("const_in")
        hi_done, lo_done = s.sem("hi_done"), s.sem("lo_done")
        k_done, v_done = s.sem("k_done"), s.sem("v_done")
        prep = s.sem("prep")
        in_done = [s.sem(f"in_done{c}") for c in range(2)]
        v_ready = s.sem("v_ready")
        x_biased = s.sem("x_biased")
        s_done = s.sem("s_done")
        top_done = s.sem("top_done")
        sub_done = s.sem("sub_done")
        exp_done = s.sem("exp_done")
        tot_done, rec_done = s.sem("tot_done"), s.sem("rec_done")
        w_done = s.sem("w_done")
        t_done = s.sem("t_done")
        wt_done = s.sem("wt_done")
        pv_done = s.sem("pv_done")
        o_hi_done, o_lo_done = s.sem("o_hi_done"), s.sem("o_lo_done")
        r_done = s.sem("r_done")
        res_done = s.sem("res_done")
        x2_done = s.sem("x2_done")
        out_done = [s.sem(f"out_done{c}") for c in range(2)]
        block = s.block()

        @block.sync
        def _(sp):
            sp.dma_start(ctx[:, :, :], io["ctxT"].rearrange("(c p) n -> p c n", p=P)).then_inc(ctx_in, 16)
            for j, name in enumerate(("wkT", "wvT")):
                sp.dma_start(kv_raw[:, j], io[name].rearrange("(c p) n -> p c n", p=P)).then_inc(ctx_in, 16)
            sp.dma_start(bk[:, :], io["bk2"]).then_inc(const_in, 16)
            sp.dma_start(bv[:, :], io["bv"].partition_broadcast(P)).then_inc(const_in, 16)
            sp.dma_start(head_of[:, :], io["head_of"]).then_inc(const_in, 16)
            sp.dma_start(ident[:, :], io["ident"]).then_inc(const_in, 16)
            sp.dma_start(bo[:, :], io["bo"].partition_broadcast(P)).then_inc(const_in, 16)
            for row in (0, 32):
                sp.dma_start(mask_i[row:row + 1, :], io["mask"]).then_inc(const_in, 16)
            sp.dma_start(wo_raw[:, :, :], io["woT"].rearrange("(g p) n -> p g n", p=P)).then_inc(const_in, 16)
            for c in range(2):
                sp.sem_inc(out_done[c], 16)
            with sp.Fori(0, B) as i:
                for c in range(2):
                    n = 2 * i + c
                    if c == 0:
                        sp.wait_ge(res_done, n + 1)
                    for part in range(2):
                        sp.dma_start(q[c][part][:, :, :].bitcast(F32), io["q2_scr"][n, part].rearrange("k p t -> p k t")).then_inc(in_done[c], 16)
                    sp.dma_start(x1[c][:, :, :], io["x1_scr"].rearrange("(n t p) e -> n p t e", p=P, t=TPC)[n]).then_inc(in_done[c], 16)
                for c in range(2):
                    n = 2 * i + c
                    sp.wait_ge(x2_done, n + 1)
                    sp.dma_start(io["x2_scr"].rearrange("(n t p) e -> n p t e", p=P, t=TPC)[n], x2[c][:, :, :]).then_inc(out_done[c], 16)
            for c in range(2):
                sp.wait_ge(out_done[c], 16 * B + 16)

        @block.gpsimd
        def _(pool):
            pool.sem_inc(w_done, 2)
            pool.wait_ge(prep, 20)
            with pool.Fori(0, B) as i:
                pool.wait_ge(pv_done, 2 * i + 1)
                pool.tensor_copy(v_now[:, :].unsqueeze(1), v_all[:, bass.ds(i, 1), :]).then_inc(v_ready, 1)
                for c in range(2):
                    pool.wait_ge(in_done[c], 48 * i + 48)
                    pool.tensor_tensor(x1[c][:, :, :], x1[c][:, :, :], bo[:, :].unsqueeze(1).to_broadcast([P, TPC, C]), ALU.add).then_inc(x_biased, 1)
                for m in range(8):
                    pool.wait_ge(rec_done, 8 * i + m + 1)
                    pool.wait_ge(t_done, 8 * i + m + 1)
                    pool.tensor_tensor(w[:, :, :], e[m % 2][:, :, :], rec[m % 2][:, :].unsqueeze(2).to_broadcast([P, H, L]), ALU.mult).then_inc(w_done, 1)

        @block.scalar
        def _(act):
            act.wait_ge(ctx_in, 48)
            nc.scalar.activation(ctx_hi[:, :, :], ctx[:, :, :], ACT.Copy).then_inc(hi_done, 1)
            nc.scalar.activation(kv_hi[:, :, :, :], kv_raw[:, :, :, :], ACT.Copy).then_inc(hi_done, 1)
            act.wait_ge(const_in, 128)
            nc.scalar.activation(wo_hi[:, :, :], wo_raw[:, :, :], ACT.Copy).then_inc(hi_done, 1)
            with act.Fori(0, B) as i:
                def weights(m):
                    act.wait_ge(sub_done, 8 * i + m + 1 + 1)
                    nc.scalar.activation(e[m % 2][:, :, :], e[m % 2][:, :, :], ACT.Exp).then_inc(exp_done, 1)

                def copy_t(m):
                    act.wait_ge(t_done, 8 * i + m + 1 + 1)
                    if m % 4 == 0:
                        act.wait_ge(pv_done, 2 * i + m // 4 + 1)
                    nc.scalar.activation(w_t[:, :, (m % 4) * P:(m % 4 + 1) * P].rearrange("p (g h) q -> p g h q", g=HG),
                                         t_ps[0:L, :, :].rearrange("p g (h q) -> p g h q", h=HG), ACT.Copy).then_inc(wt_done, 1)

                def split_o(c):
                    act.wait_ge(pv_done, 2 * i + c + 1 + 1)
                    act.wait_ge(r_done, 2 * i + c + 1)
                    nc.scalar.activation(o_hi[:, :, :], t_ps[:, :, :], ACT.Copy).then_inc(o_hi_done, 1)

                for m in range(8):
                    weights(m)
                    if m == 6:
                        norm.take_root(act, 2 * i)
                    if m >= 2:
                        copy_t(m - 2)
                    if m == 5:
                        split_o(0)
                copy_t(6)
                copy_t(7)
                split_o(1)
                norm.take_root(act, 2 * i + 1)

        @block.vector
        def _(dve):
            nc.vector.memset(v_all[:, :, :], 0.0)
            nc.vector.memset(mask_w[:, :, :, :].bitcast(F32), 0.0)
            nc.vector.memset(mask_sel[:, :].bitcast(F32), 0.0).then_inc(prep, 1)
            dve.wait_ge(prep, 1)
            nc.vector.memset(mask_sel[0:1, :].bitcast(F32), 1.0)
            nc.vector.memset(mask_sel[32:33, :].bitcast(F32), 1.0)
            dve.wait_ge(hi_done, 1)
            nc.vector.tensor_tensor(ctx_lo[:, :, :], ctx[:, :, :], ctx_hi[:, :, :].bitcast(F32), ALU.subtract)
            dve.wait_ge(hi_done, 2)
            nc.vector.tensor_tensor(kv_lo[:, :, :, :], kv_raw[:, :, :, :], kv_hi[:, :, :, :].bitcast(F32), ALU.subtract).then_inc(lo_done, 1)
            dve.wait_ge(const_in, 128)
            for row in (0, 32):
                ins = nc.vector.tensor_copy(mask_f[row:row + 1, :], mask_i[row:row + 1, :])
            ins.then_inc(prep, 1)
            dve.wait_ge(prep, 2)
            for row in (0, 32):
                ins = nc.vector.tensor_scalar(mask_f[row:row + 1, :], mask_f[row:row + 1, :], NEG, None, ALU.mult)
            ins.then_inc(prep, 1)
            dve.wait_ge(prep, 3)

            def on_heads(row):
                return mask_f[row:row + 1, :].rearrange("p (b k) -> p b k", b=B).unsqueeze(2).to_broadcast([1, B, HG, L])
            for row in (0, 32):
                ins = nc.vector.tensor_copy(mask_w[row:row + 1, :, :, :], on_heads(row))
            ins.then_inc(prep, 1)
            dve.wait_ge(prep, 4)
            nc.vector.tensor_tensor(mask_w[32:33, :, :, :], on_heads(32), mask_w[32:33, :, :, :].bitcast(F32), ALU.subtract).then_inc(prep, 1)
            dve.wait_ge(k_done, 1)
            for k in range(CK):
                ins = nc.vector.tensor_scalar(k_sum[:, k, :], s_ps[:, k, 0:B * L], bk[:, k:k + 1], None, ALU.add)
            ins.then_inc(prep, 1)
            dve.wait_ge(prep, 6)
            nc.vector.tensor_copy(k_hi[:, :, :].bitcast(F32R), k_sum[:, :, :]).then_inc(prep, 1)
            dve.wait_ge(prep, 7)
            nc.vector.tensor_tensor(k_lo[:, :, :], k_sum[:, :, :], k_hi[:, :, :], ALU.subtract).then_inc(prep, 1)
            dve.wait_ge(prep, 8)
            heads = head_of[:, :].unsqueeze(2).to_broadcast([P, HL, L])
            for part, src in enumerate((k_hi, k_lo)):
                for b in range(B):
                    for k in range(CK):
                        ins = nc.vector.tensor_tensor(k_blk[:, part, b, k, :].rearrange("p (h n) -> p h n", h=HL),
                                                      src[:, k, b * L:(b + 1) * L].unsqueeze(1).to_broadcast([P, HL, L]), heads, ALU.mult)
            ins.then_inc(prep, 1)
            dve.wait_ge(v_done, 1)
            for b in range(B):
                ins = nc.vector.tensor_tensor(v_all[:, b, 0:C], t_ps[0:L, b, 0:C], bv[0:L, :], ALU.add)
            ins.then_inc(prep, 1)
            dve.wait_ge(hi_done, 3)
            nc.vector.tensor_tensor(wo_lo[:, :, :], wo_raw[:, :, :], wo_hi[:, :, :].bitcast(F32), ALU.subtract).then_inc(prep, 10)
            dve.sem_inc(sub_done, 1)
            dve.sem_inc(res_done, 1)
            with dve.Fori(0, B) as i:
                def shift(m):
                    dve.wait_ge(s_done, 8 * i + m + 1)
                    v = s_ps[:, :, 0:GL].rearrange("p g (h n) -> p g h n", h=HG)
                    nc.vector.tensor_reduce(top[m % 2][:, :].rearrange("p (g h) -> p g h", g=HG), v, AX.X, ALU.max).then_inc(top_done, 1)
                    dve.wait_ge(top_done, 8 * i + m + 1)
                    dve.wait_ge(w_done, 8 * i + m + 1)
                    nc.vector.tensor_tensor(e[m % 2][:, :, :].rearrange("p (g h) n -> p g h n", g=HG), v,
                                            top[m % 2][:, :].rearrange("p (g h) -> p g h", g=HG).unsqueeze(3).to_broadcast([P, HG, HG, L]),
                                            ALU.subtract).then_inc(sub_done, 1)

                def totals(m):
                    dve.wait_ge(exp_done, 8 * i + m + 1)
                    nc.vector.tensor_reduce(tot[m % 2][:, :], e[m % 2][:, :, :], AX.X, ALU.add).then_inc(tot_done, 1)
                    dve.wait_ge(tot_done, 8 * i + m + 1)
                    nc.vector.reciprocal(rec[m % 2][:, :], tot[m % 2][:, :]).then_inc(rec_done, 1)

                def split_o(c):
                    dve.wait_ge(o_hi_done, 2 * i + c + 1)
                    nc.vector.tensor_tensor(o_lo[:, :, :], t_ps[:, :, :], o_hi[:, :, :].bitcast(F32), ALU.subtract).then_inc(o_lo_done, 1)

                def normalise(c):
                    n = 2 * i + c
                    dve.wait_ge(r_done, n + 1 + 1)
                    dve.wait_ge(x_biased, n + 1)
                    nc.vector.tensor_tensor(res[:, :, :], t_ps[:, 0:2, :].rearrange("p g (t e) -> p (g t) e", t=2), x1[c][:, :, :], ALU.add).then_inc(res_done, 1)
                    dve.wait_ge(res_done, n + 1 + 1)
                    dve.wait_ge(out_done[c], 16 * i + 16)
                    norm.apply(dve, n, res, x2[c]).then_inc(x2_done, 1)

                for m in range(8):
                    shift(m)
                    if m:
                        totals(m - 1)
                    if m == 6:
                        split_o(0)
                        normalise(0)
                totals(7)
                split_o(1)
                normalise(1)

        @block.tensor
        def _(pe):
            pe.sem_inc(t_done, 1)
            pe.sem_inc(pv_done, 1)
            pe.sem_inc(r_done, 1)
            pe.wait_ge(lo_done, 1)
            for m in range(CK):
                prods = [(b[:, 0, k, m * P:(m + 1) * P], a[:, k, :]) for k in range(CK)
                         for a, b in parts3(ctx_hi, ctx_lo, kv_hi, kv_lo)]
                for j, (a, b) in enumerate(prods):
                    ins = nc.tensor.matmul(s_ps[:, m, 0:B * L], a, b, start=(j == 0), stop=(j == len(prods) - 1))
            ins.then_inc(k_done, 1)
            for b4 in range(B):
                prods = [(a[:, k, b4 * L:(b4 + 1) * L], b[:, 1, k, :]) for k in range(CK)
                         for a, b in parts3(ctx_hi, ctx_lo, kv_hi, kv_lo)]
                for j, (a, b) in enumerate(prods):
                    ins = nc.tensor.matmul(t_ps[0:L, b4, 0:C], a, b, start=(j == 0), stop=(j == len(prods) - 1))
            ins.then_inc(v_done, 1)
            pe.wait_ge(prep, 20)
            with pe.Fori(0, B) as i:
                def scores(m):
                    c, t = divmod(m, 4)
                    if t == 0:
                        pe.wait_ge(in_done[c], 48 * i + 48)
                    pe.wait_ge(sub_done, 8 * i + m + 1)
                    tok = slice(t * P, (t + 1) * P)
                    for g in range(HG):
                        k, half = divmod(g, 2)
                        cols = slice(half * GL, (half + 1) * GL)
                        for j, (a, b) in enumerate(((0, 0), (0, 1), (1, 0))):
                            nc.tensor.matmul(s_ps[:, g, 0:GL], q[c][a][:, k, tok], k_blk[:, b, bass.ds(i, 1), k, cols].rearrange("p o n -> p (o n)"),
                                             start=(j == 0), stop=False)
                        ins = nc.tensor.matmul(s_ps[:, g, 0:GL], mask_sel[:, :], mask_w[:, bass.ds(i, 1), :, :].rearrange("p o h n -> p (o h n)"),
                                               start=False, stop=True)
                    ins.then_inc(s_done, 1)

                def transpose_w(m):
                    pe.wait_ge(w_done, 8 * i + m + 1 + 2)
                    if m % 4 == 0:
                        pe.wait_ge(res_done, 2 * i + m // 4 + 1)
                    if m:
                        pe.wait_ge(wt_done, 8 * i + m)
                    for h in range(H):
                        ins = nc.tensor.transpose(t_ps[0:L, h // HG, (h % HG) * P:(h % HG + 1) * P], w[:, h, :], ident[:, :])
                    ins.then_inc(t_done, 1)

                def values(c):
                    pe.wait_ge(wt_done, 8 * i + 4 * c + 4)
                    pe.wait_ge(v_ready, i + 1)
                    for g in range(HG):
                        for h in range(HG):
                            head = g * HG + h
                            ins = nc.tensor.matmul(t_ps[32 * h:32 * h + 32, g, :], v_now[:, head * D:head * D + 32], w_t[:, head, :], start=True, stop=True)
                    ins.then_inc(pv_done, 1)

                def project(c):
                    pe.wait_ge(o_lo_done, 2 * i + c + 1)
                    for t in range(TPC):
                        prods = [(a[:, g, t * P:(t + 1) * P], b[:, g, :]) for g in range(HG)
                                 for a, b in parts3(o_hi, o_lo, wo_hi, wo_lo)]
                        for j, (a, b) in enumerate(prods):
                            ins = nc.tensor.matmul(t_ps[:, t // 2, (t % 2) * C:(t % 2 + 1) * C], a, b, start=(j == 0), stop=(j == len(prods) - 1))
                    ins.then_inc(r_done, 1)

                for m in range(8):
                    scores(m)
                    if m in (2, 3, 4, 5):
                        transpose_w(m - 2)
                    if m == 5:
                        values(0)
                    if m == 6:
                        project(0)
                        transpose_w(4)
                transpose_w(5)
                transpose_w(6)
                transpose_w(7)
                values(1)
                project(1)


E = 8
CAP = 1024
HID = 1024
HM = HID // P
SLOTS = E * CAP


def chunk_rows(ap, n):
    return ap.rearrange("(n t p) e -> n p t e", p=P, t=TPC)[n]


def stage_router(nc, io, keep):
    with Scope(nc, "ro") as s:
        ident = s.sb("ident", [P, P], F32)
        w_raw = s.sb("w_raw", [P, CK, HID], F32)
        w_hi = s.sb("w_hi", [P, CK, HID], F32R)
        w_lo = s.sb("w_lo", [P, CK, HID], F32R)
        rb1 = s.sb("rb1", [P, HM], F32)
        rw2 = s.sb("rw2", [P, HM, 32], F32)
        rb2 = s.sb("rb2", [P, E], F32)
        x2 = [s.sb(f"x2{c}", [P, TPC, C], F32) for c in range(2)]
        x_hi = [s.sb(f"x_hi{c}", [P, CK, CH], F32R) for c in range(2)]
        x_lo = [s.sb(f"x_lo{c}", [P, CK, CH], F32R) for c in range(2)]
        hid = [s.sb(f"hid{c}", [P, HM, CH], F32) for c in range(2)]
        l_sb = s.sb("l_sb", [P, CH], F32)
        part = s.sb("part", [P, TPC, E], F32)
        logit = s.sb("logit", [P, TPC, E], F32)
        best = s.sb("best", [P, TPC, 8], F32)
        where = s.sb("where", [P, TPC, 8], U32)
        t_ps = s.pb("t_ps", (P, CK, CH))
        h_ps = [s.pb(f"h_ps{i}") for i in range(4)]
        l_ps = s.pb("l_ps")
        lt_ps = s.pb("lt_ps", (P, TPC, P))

        const_in = s.sem("const_in")
        w_split = s.sem("w_split")
        in_done = [s.sem(f"in_done{c}") for c in range(2)]
        t_done, x_hi_done, x_lo_done = s.sem("t_done"), s.sem("x_hi_done"), s.sem("x_lo_done")
        h_done, relu_done = s.sem("h_done"), s.sem("relu_done")
        l_done, l_copied = s.sem("l_done"), s.sem("l_copied")
        lt_done = s.sem("lt_done")
        sum_done, logit_done = s.sem("sum_done"), s.sem("logit_done")
        best_done, pick = s.sem("best_done"), s.sem("pick")
        block = s.block()

        @block.sync
        def _(sp):
            sp.dma_start(w_raw[:, :, :], io["rw1"].rearrange("(c p) n -> p c n", p=P)).then_inc(const_in, 16)
            sp.dma_start(ident[:, :], io["ident"]).then_inc(const_in, 16)
            sp.dma_start(rb1[:, :], io["rb1"]).then_inc(const_in, 16)
            sp.dma_start(rw2[:, :, :], io["rw2"]).then_inc(const_in, 16)
            sp.dma_start(rb2[:, :], io["rb2"].partition_broadcast(P)).then_inc(const_in, 16)
            with sp.Fori(0, B) as i:
                for c in range(2):
                    sp.wait_ge(t_done, 2 * i + c + 1)
                    sp.dma_start(x2[c][:, :, :], chunk_rows(io["x2_scr"], 2 * i + c)).then_inc(in_done[c], 16)

        @block.scalar
        def _(act):
            act.sem_inc(relu_done, 4)
            act.wait_ge(const_in, 80)
            nc.scalar.activation(w_hi[:, :, :], w_raw[:, :, :], ACT.Copy).then_inc(w_split, 1)
            with act.Fori(0, B) as i:
                def split_x(c):
                    act.wait_ge(t_done, 2 * i + c + 1 + 2)
                    act.wait_ge(h_done, 8 * (2 * i + c) + 8)
                    nc.scalar.activation(x_hi[c][:, :, :], t_ps[:, :, :], ACT.Copy).then_inc(x_hi_done, 1)

                def relus(c):
                    act.wait_ge(l_done, 2 * i + c + 1)
                    for m in range(HM):
                        act.wait_ge(h_done, 8 * (2 * i + c) + m + 1 + 16)
                        nc.scalar.activation(hid[c][:, m, :], h_ps[m % 4][:, :], ACT.Relu, bias=rb1[:, m:m + 1]).then_inc(relu_done, 1)

                def copy_l(c):
                    act.wait_ge(l_done, 2 * i + c + 1 + 2)
                    act.wait_ge(lt_done, 2 * i + c + 1)
                    nc.scalar.activation(l_sb[:, :], l_ps[:, :], ACT.Copy).then_inc(l_copied, 1)

                split_x(0)
                relus(0)
                split_x(1)
                copy_l(0)
                relus(1)
                copy_l(1)

        @block.vector
        def _(dve):
            dve.sem_inc(x_lo_done, 1)
            dve.sem_inc(sum_done, 1)
            dve.wait_ge(w_split, 1)
            nc.vector.tensor_tensor(w_lo[:, :, :], w_raw[:, :, :], w_hi[:, :, :].bitcast(F32), ALU.subtract).then_inc(w_split, 1)
            dve.wait_ge(const_in, 80)
            with dve.Fori(0, B) as i:
                def split_x(c):
                    dve.wait_ge(x_hi_done, 2 * i + c + 1)
                    nc.vector.tensor_tensor(x_lo[c][:, :, :], t_ps[:, :, :], x_hi[c][:, :, :].bitcast(F32), ALU.subtract).then_inc(x_lo_done, 1)

                def choose(c):
                    n = 2 * i + c
                    dve.wait_ge(lt_done, n + 1 + 1)
                    nc.vector.tensor_reduce(part[:, :, :], lt_ps[:, :, :].rearrange("p t (j e) -> p t e j", j=4)[:, :, 0:E, :], AX.X, ALU.add).then_inc(sum_done, 1)
                    dve.wait_ge(sum_done, n + 1 + 1)
                    nc.vector.tensor_tensor(logit[:, :, :], part[:, :, :], rb2[:, :].unsqueeze(1).to_broadcast([P, TPC, E]), ALU.add).then_inc(logit_done, 1)
                    wait_alone(dve, logit_done, n + 1, io["apart"])
                    for t in range(TPC):
                        ins = nc.vector.max(best[:, t, :], logit[:, t, :])
                    ins.then_inc(best_done, 1)
                    wait_alone(dve, best_done, n + 1, io["apart"])
                    for t in range(TPC):
                        ins = nc.vector.max_index(where[:, t, :], best[:, t, :], logit[:, t, :])
                    ins.then_inc(pick, 1)
                    dve.wait_ge(pick, 2 * n + 1)
                    nc.vector.tensor_copy(keep["value"][:, bass.ds(TPC * n, TPC), :], best[:, :, 0:2])
                    nc.vector.tensor_copy(keep["expert"][:, bass.ds(TPC * n, TPC), :], where[:, :, 0:2]).then_inc(pick, 1)

                split_x(0)
                split_x(1)
                choose(0)
                choose(1)

        @block.tensor
        def _(pe):
            pe.sem_inc(t_done, 2)
            pe.sem_inc(h_done, 16)
            pe.sem_inc(l_done, 2)
            pe.sem_inc(lt_done, 1)
            pe.wait_ge(w_split, 2)
            pe.wait_ge(const_in, 80)
            with pe.Fori(0, B) as i:
                def transpose_x(c):
                    pe.wait_ge(in_done[c], 16 * i + 16)
                    pe.wait_ge(x_lo_done, 2 * i + c + 1)
                    for t in range(TPC):
                        for k in range(CK):
                            ins = nc.tensor.transpose(t_ps[:, k, t * P:(t + 1) * P], x2[c][:, t, k * P:(k + 1) * P], ident[:, :])
                    ins.then_inc(t_done, 1)

                def hidden(c):
                    pe.wait_ge(x_lo_done, 2 * i + c + 1 + 1)
                    for m in range(HM):
                        pe.wait_ge(relu_done, 8 * (2 * i + c) + m + 1)
                        prods = [(b[:, k, m * P:(m + 1) * P], a[:, k, :]) for k in range(CK)
                                 for a, b in parts3(x_hi[c], x_lo[c], w_hi, w_lo)]
                        for j, (a, b) in enumerate(prods):
                            ins = nc.tensor.matmul(h_ps[m % 4][:, :], a, b, start=(j == 0), stop=(j == len(prods) - 1))
                        ins.then_inc(h_done, 1)

                def logits(c):
                    n = 2 * i + c
                    pe.wait_ge(relu_done, 8 * n + 8 + 4)
                    for m in range(HM):
                        j = m % 4
                        ins = nc.tensor.matmul(l_ps[32 * j:32 * j + 32, :], rw2[:, m, :], hid[c][:, m, :], start=(m < 4), stop=(m >= 4))
                    ins.then_inc(l_done, 1)

                def transpose_l(c):
                    n = 2 * i + c
                    pe.wait_ge(l_copied, n + 1)
                    pe.wait_ge(sum_done, n + 1)
                    for t in range(TPC):
                        ins = nc.tensor.transpose(lt_ps[:, t, :], l_sb[:, t * P:(t + 1) * P], ident[:, :])
                    ins.then_inc(lt_done, 1)

                transpose_x(0)
                hidden(0)
                transpose_x(1)
                logits(0)
                hidden(1)
                transpose_l(0)
                logits(1)
                transpose_l(1)


def stage_dispatch(nc, io, keep):
    with Scope(nc, "di") as s:
        before = s.sb("before", [P, P], F32)
        ones = s.sb("ones", [P, P], F32)
        iota = s.sb("iota", [P, E], F32)
        hot = s.sb("hot", [P, TT, 2, E], F32)
        both = s.sb("both", [P, TT, E], F32)
        total = s.sb("total", [P, TT, E], F32)
        run = s.sb("run", [P, TT, E], F32)
        place = s.sb("place", [P, TT, E], F32)
        mine = s.sb("mine", [P, TT, 2, E], F32)
        pos = s.sb("pos", [P, TT, 2], F32)
        kept = s.sb("kept", [P, TT, 2], F32)
        get = s.sb("get", [P, TT, 2], F32)
        put = s.sb("put", [P, TT, 2], F32)
        put_u = s.sb("put_u", [P, TT * 2], U32)
        put_now = [s.sb(f"put_now{c}", [P, TPC * 2], U32) for c in range(2)]
        x2 = [s.sb(f"x2{c}", [P, TPC, C], F32) for c in range(2)]
        diff = s.sb("diff", [P, TT], F32)
        share = s.sb("share", [P, TT, 2], F32)
        c_ps = s.pb("c_ps", (P, TT * E))
        n_ps = s.pb("n_ps", (P, TT * E))

        const_in = s.sem("const_in")
        step = s.sem("step")
        hot_done = s.sem("hot_done")
        count_done = s.sem("count_done")
        diff_done, exp_done = s.sem("diff_done"), s.sem("exp_done")
        put_done = s.sem("put_done")
        now_done = s.sem("now_done")
        in_done = [s.sem(f"in_done{c}") for c in range(2)]
        sent = [s.sem(f"sent{c}") for c in range(2)]
        block = s.block()

        @block.sync
        def _(sp):
            sp.dma_start(before[:, :], io["before"]).then_inc(const_in, 16)
            sp.dma_start(iota[:, :], io["iota"].partition_broadcast(P)).then_inc(const_in, 16)
            for c in range(2):
                sp.dma_start(x2[c][:, :, :], chunk_rows(io["x2_scr"], c)).then_inc(in_done[c], 16)
            with sp.Fori(0, B - 1) as i:
                for c in range(2):
                    sp.wait_ge(sent[c], 128 * i + 128)
                    sp.dma_start(x2[c][:, :, :], chunk_rows(io["x2_scr"], 2 * i + c + 2)).then_inc(in_done[c], 16)

        @block.gpsimd
        def _(pool):
            pool.wait_ge(put_done, 1)

            def scatter(i, c):
                pool.wait_ge(in_done[c], 16 * i + 16)
                pool.tensor_copy(put_now[c][:, :], put_u[:, bass.ds(2 * TPC * (2 * i + c), 2 * TPC)]).then_inc(now_done, 1)
                wait_alone(pool, now_done, 2 * i + c + 1, io["apart"])
                for t in range(TPC):
                    for k in range(2):
                        pool.indirect_dma_start(io["rows_scr"], bass.IndirectOffsetOnAxis(put_now[c][:, 2 * t + k:2 * t + k + 1], 0),
                                                x2[c][:, t, :], None, bounds_check=SLOTS - 1, oob_is_err=False).then_inc(sent[c], 16)

            with pool.Fori(0, B) as i:
                for c in range(2):
                    scatter(i, c)
            for c in range(2):
                pool.wait_ge(sent[c], 128 * B)

        @block.scalar
        def _(act):
            act.wait_ge(diff_done, 1)
            nc.scalar.activation(diff[:, :], diff[:, :], ACT.Exp).then_inc(exp_done, 1)

        @block.vector
        def _(dve):
            n = [0]

            def then(ins):
                n[0] += 1
                ins.then_inc(step, 1)
                dve.wait_ge(step, n[0])

            nc.vector.memset(ones[:, :], 1.0)
            nc.vector.tensor_tensor(diff[:, :], keep["value"][:, :, 1], keep["value"][:, :, 0], ALU.subtract).then_inc(diff_done, 1)
            dve.wait_ge(const_in, 32)
            experts = keep["expert"][:, :, :].unsqueeze(3).to_broadcast([P, TT, 2, E])
            for k in range(2):
                ins = nc.vector.tensor_tensor(hot[:, :, k, :], experts[:, :, k, :], iota[:, :].unsqueeze(1).to_broadcast([P, TT, E]), ALU.is_equal)
            then(ins)
            nc.vector.tensor_tensor(both[:, :, :], hot[:, :, 0, :], hot[:, :, 1, :], ALU.add).then_inc(hot_done, 1)
            dve.wait_ge(count_done, 1)
            then(nc.vector.tensor_copy(total[:, :, :], n_ps[:, :].rearrange("p (t e) -> p t e", e=E)))
            for e in range(E):
                ins = nc.vector.tensor_tensor_scan(run[:, :, e], ones[:, 0:TT], total[:, :, e], 0.0, ALU.mult, ALU.add)
            then(ins)
            then(nc.vector.tensor_tensor(run[:, :, :], run[:, :, :], total[:, :, :], ALU.subtract))
            then(nc.vector.tensor_tensor(place[:, :, :], c_ps[:, :].rearrange("p (t e) -> p t e", e=E), run[:, :, :], ALU.add))
            for k in range(2):
                ins = nc.vector.tensor_tensor(mine[:, :, k, :], hot[:, :, k, :], place[:, :, :], ALU.mult)
            then(ins)
            then(nc.vector.tensor_reduce(pos[:, :, :], mine[:, :, :, :], AX.X, ALU.add))
            nc.vector.tensor_scalar(kept[:, :, :], pos[:, :, :], float(CAP), None, ALU.is_lt)
            then(nc.vector.tensor_scalar(get[:, :, :], pos[:, :, :], float(CAP - 1), None, ALU.min))
            then(nc.vector.scalar_tensor_tensor(get[:, :, :], keep["expert"][:, :, :], float(CAP), get[:, :, :], ALU.mult, ALU.add))
            nc.vector.tensor_copy(keep["get"][:, :], get[:, :, :].rearrange("p t k -> p (t k)"))
            then(nc.vector.scalar_tensor_tensor(put[:, :, :], kept[:, :, :], -float(SLOTS), get[:, :, :], ALU.mult, ALU.add))
            then(nc.vector.tensor_scalar(put[:, :, :], put[:, :, :], float(SLOTS), None, ALU.add))
            nc.vector.tensor_copy(put_u[:, :], put[:, :, :].rearrange("p t k -> p (t k)")).then_inc(put_done, 1)
            dve.wait_ge(exp_done, 1)
            then(nc.vector.tensor_scalar(share[:, :, 0], diff[:, :], 1.0, None, ALU.add))
            then(nc.vector.reciprocal(share[:, :, 0], share[:, :, 0]))
            then(nc.vector.tensor_tensor(share[:, :, 1], share[:, :, 0], diff[:, :], ALU.mult))
            then(nc.vector.tensor_tensor(keep["share"][:, :].rearrange("p (t k) -> p t k", k=2), share[:, :, :], kept[:, :, :], ALU.mult))

        @block.tensor
        def _(pe):
            pe.wait_ge(const_in, 32)
            pe.wait_ge(hot_done, 1)
            chosen = both[:, :, :].rearrange("p t e -> p (t e)")
            nc.tensor.matmul(c_ps[:, :], before[:, :], chosen, start=True, stop=True)
            nc.tensor.matmul(n_ps[:, :], ones[:, :], chosen, start=True, stop=True).then_inc(count_done, 1)


def stage_experts(nc, io, keep):
    with Scope(nc, "ex") as s:
        ident = s.sb("ident", [P, P], F32)
        w1_raw = s.sb("w1_raw", [P, CK, HID], F32)
        w2_raw = s.sb("w2_raw", [P, HM, C], F32)
        w1_hi = [s.sb(f"w1_hi{i}", [P, CK, HID], F32R) for i in range(2)]
        w1_lo = [s.sb(f"w1_lo{i}", [P, CK, HID], F32R) for i in range(2)]
        w2_hi = [s.sb(f"w2_hi{i}", [P, HM, C], F32R) for i in range(2)]
        w2_lo = [s.sb(f"w2_lo{i}", [P, HM, C], F32R) for i in range(2)]
        b1 = s.sb("b1", [P, E, HM], F32)
        b2 = [s.sb(f"b2{i}", [P, C], F32) for i in range(2)]
        rows = [s.sb(f"rows{c}", [P, TPC, C], F32) for c in range(2)]
        x_hi = [s.sb(f"x_hi{c}", [P, CK, CH], F32R) for c in range(2)]
        x_lo = [s.sb(f"x_lo{c}", [P, CK, CH], F32R) for c in range(2)]
        hid = [s.sb(f"hid{i}", [P, CH], F32) for i in range(2)]
        h_hi = [s.sb(f"h_hi{c}", [P, HM, CH], F32R) for c in range(2)]
        h_lo = [s.sb(f"h_lo{c}", [P, HM, CH], F32R) for c in range(2)]
        y = [s.sb(f"y{c}", [P, TPC, C], F32) for c in range(2)]
        t_ps = s.pb("t_ps", (P, CK, CH))
        h_ps = [s.pb(f"h_ps{i}") for i in range(2)]
        y_ps = [s.pb(f"y_ps{i}") for i in range(4)]

        const_in = s.sem("const_in")
        w_in = s.sem("w_in")
        w_hi_done, w_lo_done = s.sem("w_hi_done"), s.sem("w_lo_done")
        in_done = [s.sem(f"in_done{c}") for c in range(2)]
        t_done, x_hi_done, x_lo_done = s.sem("t_done"), s.sem("x_hi_done"), s.sem("x_lo_done")
        h_done, relu_done = s.sem("h_done"), s.sem("relu_done")
        h_hi_done, h_lo_done = s.sem("h_hi_done"), s.sem("h_lo_done")
        y_done, biased = s.sem("y_done"), s.sem("biased")
        out_done = [s.sem(f"out_done{c}") for c in range(2)]
        block = s.block()

        @block.sync
        def _(sp):
            sp.dma_start(ident[:, :], io["ident"]).then_inc(const_in, 16)
            sp.dma_start(b1[:, :, :], io["eb1"]).then_inc(const_in, 16)
            for c in range(2):
                sp.sem_inc(out_done[c], 16)
            rows_v = io["rows_scr"].rearrange("(n t p) e -> n p t e", p=P, t=TPC)
            y_v = io["y_scr"].rearrange("(n t p) e -> n p t e", p=P, t=TPC)
            for c in range(2):
                sp.dma_start(rows[c][:, :, :], rows_v[c]).then_inc(in_done[c], 16)

            def load_weights(e, par):
                sp.dma_start(w1_raw[:, :, :], io["ew1"].rearrange("e (c p) n -> e p c n", p=P)[e]).then_inc(w_in, 16)
                sp.dma_start(w2_raw[:, :, :], io["ew2"].rearrange("e (m p) n -> e p m n", p=P)[e]).then_inc(w_in, 16)
                sp.dma_start(b2[par][:, :], io["eb2"][e].partition_broadcast(P)).then_inc(w_in, 16)

            load_weights(0, 0)

            def expert(e, par, last):
                if not last:
                    sp.wait_ge(w_lo_done, 2 * e + 2)
                    sp.wait_ge(biased, 8 * e + 4)
                    load_weights(e + 1, 1 - par)
                for c in range(2):
                    h = 2 * e + c
                    if not last:
                        sp.wait_ge(t_done, h + 1)
                        sp.dma_start(rows[c][:, :, :], rows_v[h + 2]).then_inc(in_done[c], 16)
                    if c == 1 or not (isinstance(e, int) and e == 0):
                        hh = h - 1
                        sp.wait_ge(biased, 4 * hh + 4 + 4)
                        sp.dma_start(y_v[hh], y[(c + 1) % 2][:, :, :]).then_inc(out_done[(c + 1) % 2], 16)

            expert(0, 0, False)
            with sp.Fori(0, 3) as i:
                expert(2 * i + 1, 1, False)
                expert(2 * i + 2, 0, False)
            expert(E - 1, 1, True)
            sp.wait_ge(biased, 8 * E + 4)
            sp.dma_start(y_v[2 * E - 1], y[1][:, :, :]).then_inc(out_done[1], 16)
            for c in range(2):
                sp.wait_ge(out_done[c], 16 * E + 16)

        @block.scalar
        def _(act):
            act.sem_inc(relu_done, 2)
            act.wait_ge(const_in, 32)

            def split_weights(e, par):
                act.wait_ge(w_in, 48 * e + 48)
                if not (isinstance(e, int) and e < 2):
                    act.wait_ge(y_done, 8 * (e - 1))
                nc.scalar.activation(w1_hi[par][:, :, :], w1_raw[:, :, :], ACT.Copy).then_inc(w_hi_done, 1)
                nc.scalar.activation(w2_hi[par][:, :, :], w2_raw[:, :, :], ACT.Copy).then_inc(w_hi_done, 1)

            def split_x(h, c):
                act.wait_ge(t_done, h + 1)
                act.wait_ge(h_done, 8 * h + 8)
                nc.scalar.activation(x_hi[c][:, :, :], t_ps[:, :, :], ACT.Copy).then_inc(x_hi_done, 1)

            def relus(h, c, e):
                for m in range(HM):
                    act.wait_ge(h_done, 8 * h + m + 1 + 16)
                    act.wait_ge(h_lo_done, 8 * h + m + 1)
                    nc.scalar.activation(hid[m % 2][:, :], h_ps[m % 2][:, :], ACT.Relu,
                                         bias=b1[:, bass.ds(e, 1), m:m + 1].rearrange("p a b -> p (a b)") if not isinstance(e, int) else b1[:, e, m:m + 1]).then_inc(relu_done, 1)

            def expert(e, par, last):
                h = 2 * e
                split_x(h + 1, 1)
                relus(h, 0, e)
                if not last:
                    split_weights(e + 1, 1 - par)
                    split_x(h + 2, 0)
                relus(h + 1, 1, e)

            split_weights(0, 0)
            split_x(0, 0)
            expert(0, 0, False)
            with act.Fori(0, 3) as i:
                expert(2 * i + 1, 1, False)
                expert(2 * i + 2, 0, False)
            expert(E - 1, 1, True)

        @block.vector
        def _(dve):
            dve.sem_inc(h_lo_done, 2)
            dve.sem_inc(biased, 4)

            def split_weights(e, par):
                for j, (raw, hi, lo) in enumerate(((w1_raw, w1_hi, w1_lo), (w2_raw, w2_hi, w2_lo))):
                    dve.wait_ge(w_hi_done, 2 * e + j + 1)
                    nc.vector.tensor_tensor(lo[par][:, :, :], raw[:, :, :], hi[par][:, :, :].bitcast(F32), ALU.subtract).then_inc(w_lo_done, 1)

            def split_x(h, c):
                dve.wait_ge(x_hi_done, h + 1)
                nc.vector.tensor_tensor(x_lo[c][:, :, :], t_ps[:, :, :], x_hi[c][:, :, :].bitcast(F32), ALU.subtract).then_inc(x_lo_done, 1)

            def split_hidden(h, c, m):
                if m == 0 and not (isinstance(h, int) and h < 2):
                    dve.wait_ge(y_done, 4 * (h - 1))
                dve.wait_ge(relu_done, 8 * h + m + 1 + 2)
                nc.vector.tensor_copy(h_hi[c][:, m, :], hid[m % 2][:, :]).then_inc(h_hi_done, 1)
                dve.wait_ge(h_hi_done, 8 * h + m + 1)
                nc.vector.tensor_tensor(h_lo[c][:, m, :], hid[m % 2][:, :], h_hi[c][:, m, :].bitcast(F32), ALU.subtract).then_inc(h_lo_done, 1)

            def bias_y(h, e, c, par, t):
                if t == 0:
                    dve.wait_ge(out_done[c], 16 * e + 16)
                dve.wait_ge(y_done, 4 * h + t + 1)
                nc.vector.tensor_tensor(y[c][:, t, :], y_ps[t][:, 0:C], b2[par][:, :], ALU.add).then_inc(biased, 1)

            def expert(e, par, last, first):
                h = 2 * e
                split_x(h + 1, 1)
                for m in range(HM):
                    split_hidden(h, 0, m)
                if not first:
                    for t in range(TPC):
                        bias_y(h - 1, e - 1, 1, 1 - par, t)
                if not last:
                    split_weights(e + 1, 1 - par)
                    split_x(h + 2, 0)
                for m in range(HM):
                    split_hidden(h + 1, 1, m)
                for t in range(TPC):
                    bias_y(h, e, 0, par, t)

            split_weights(0, 0)
            split_x(0, 0)
            expert(0, 0, False, True)
            with dve.Fori(0, 3) as i:
                expert(2 * i + 1, 1, False, False)
                expert(2 * i + 2, 0, False, False)
            expert(E - 1, 1, True, False)
            for t in range(TPC):
                bias_y(2 * E - 1, E - 1, 1, 1, t)

        @block.tensor
        def _(pe):
            pe.sem_inc(h_done, 16)
            pe.wait_ge(const_in, 32)

            def transpose_rows(h, e, c):
                pe.wait_ge(in_done[c], 16 * e + 16)
                if not (isinstance(h, int) and h == 0):
                    pe.wait_ge(x_lo_done, h)
                for t in range(TPC):
                    for k in range(CK):
                        ins = nc.tensor.transpose(t_ps[:, k, t * P:(t + 1) * P], rows[c][:, t, k * P:(k + 1) * P], ident[:, :])
                ins.then_inc(t_done, 1)

            def hidden(h, c, e, par):
                pe.wait_ge(x_lo_done, h + 1)
                pe.wait_ge(w_lo_done, 2 * e + 2)
                for m in range(HM):
                    pe.wait_ge(relu_done, 8 * h + m + 1)
                    prods = [(b[:, k, m * P:(m + 1) * P], a[:, k, :]) for k in range(CK)
                             for a, b in parts3(x_hi[c], x_lo[c], w1_hi[par], w1_lo[par])]
                    for j, (a, b) in enumerate(prods):
                        ins = nc.tensor.matmul(h_ps[m % 2][:, :], a, b, start=(j == 0), stop=(j == len(prods) - 1))
                    ins.then_inc(h_done, 1)

            def results(h, c, par):
                pe.wait_ge(h_lo_done, 8 * h + 8 + 2)
                for t in range(TPC):
                    pe.wait_ge(biased, 4 * h + t + 1)
                    prods = [(a[:, m, t * P:(t + 1) * P], b[:, m, :]) for m in range(HM)
                             for a, b in parts3(h_hi[c], h_lo[c], w2_hi[par], w2_lo[par])]
                    for j, (a, b) in enumerate(prods):
                        ins = nc.tensor.matmul(y_ps[t][:, 0:C], a, b, start=(j == 0), stop=(j == len(prods) - 1))
                    ins.then_inc(y_done, 1)

            def expert(e, par, last, first):
                h = 2 * e
                transpose_rows(h + 1, e, 1)
                hidden(h, 0, e, par)
                if not first:
                    results(h - 1, 1, 1 - par)
                if not last:
                    transpose_rows(h + 2, e + 1, 0)
                hidden(h + 1, 1, e, par)
                results(h, 0, par)

            transpose_rows(0, 0, 0)
            expert(0, 0, False, True)
            with pe.Fori(0, 3) as i:
                expert(2 * i + 1, 1, False, False)
                expert(2 * i + 2, 0, False, False)
            expert(E - 1, 1, True, False)
            results(2 * E - 1, 1, 1)


def stage_combine(nc, io, keep):
    with Scope(nc, "co") as s:
        x2 = [s.sb(f"x2{c}", [P, TPC, C], F32) for c in range(2)]
        got = [s.sb(f"got{c}", [P, TPC, 2, C], F32) for c in range(2)]
        get_now = [s.sb(f"get_now{c}", [P, TPC * 2], U32) for c in range(2)]
        share_now = [s.sb(f"share_now{c}", [P, TPC * 2], F32) for c in range(2)]
        out = [s.sb(f"out{c}", [P, TPC, C], F32) for c in range(2)]
        norm = Norm(nc, s, io["apart"])
        in_done = [s.sem(f"in_done{c}") for c in range(2)]
        now_done = s.sem("now_done")
        got_done = [s.sem(f"got_done{c}") for c in range(2)]
        step = s.sem("step")
        norm_done = s.sem("norm_done")
        out_done = [s.sem(f"out_done{c}") for c in range(2)]
        block = s.block()

        @block.sync
        def _(sp):
            for c in range(2):
                sp.sem_inc(out_done[c], 16)
            with sp.Fori(0, B) as i:
                for c in range(2):
                    sp.wait_ge(norm_done, 2 * i + c + 1)
                    sp.dma_start(x2[c][:, :, :], chunk_rows(io["x2_scr"], 2 * i + c)).then_inc(in_done[c], 16)
                for c in range(2):
                    sp.wait_ge(norm_done, 2 * i + c + 1 + 2)
                    sp.dma_start(chunk_rows(io["out"], 2 * i + c), out[c][:, :, :]).then_inc(out_done[c], 16)
            for c in range(2):
                sp.wait_ge(out_done[c], 16 * B + 16)

        @block.gpsimd
        def _(pool):
            def gather(n, c):
                pool.wait_ge(norm_done, n + 1)
                pool.tensor_copy(get_now[c][:, :], keep["get"][:, bass.ds(2 * TPC * n, 2 * TPC)])
                pool.tensor_copy(share_now[c][:, :], keep["share"][:, bass.ds(2 * TPC * n, 2 * TPC)]).then_inc(now_done, 1)
                wait_alone(pool, now_done, n + 1, io["apart"])
                for t in range(TPC):
                    for k in range(2):
                        pool.indirect_dma_start(got[c][:, t, k, :], None, io["y_scr"],
                                                bass.IndirectOffsetOnAxis(get_now[c][:, 2 * t + k:2 * t + k + 1], 0)).then_inc(got_done[c], 16)

            gather(0, 0)
            with pool.Fori(0, B - 1) as i:
                gather(2 * i + 1, 1)
                gather(2 * i + 2, 0)
            gather(2 * B - 1, 1)

        @block.scalar
        def _(act):
            with act.Fori(0, B) as i:
                for c in range(2):
                    norm.take_root(act, 2 * i + c)

        @block.vector
        def _(dve):
            dve.sem_inc(norm_done, 2)
            with dve.Fori(0, B) as i:
                for c in range(2):
                    n = 2 * i + c
                    dve.wait_ge(in_done[c], 16 * i + 16)
                    dve.wait_ge(now_done, n + 1)
                    dve.wait_ge(got_done[c], 128 * i + 128)
                    for k in range(2):
                        for t in range(TPC):
                            ins = nc.vector.scalar_tensor_tensor(x2[c][:, t, :], got[c][:, t, k, :], share_now[c][:, 2 * t + k:2 * t + k + 1],
                                                                 x2[c][:, t, :], ALU.mult, ALU.add)
                        ins.then_inc(step, 1)
                        dve.wait_ge(step, 2 * n + k + 1)
                    dve.wait_ge(out_done[c], 16 * i + 16)
                    norm.apply(dve, n, x2[c], out[c]).then_inc(norm_done, 1)


def consts():
    f = np.float32
    pos = np.arange(S, dtype=f)
    inv = (f(1.0) / f(10000.0) ** (np.arange(0, D, 2, dtype=f) / f(D))).astype(f)
    ang = (pos[:, None] * inv[None, :]).astype(f)
    sin, cos = np.sin(ang).astype(f), np.cos(ang).astype(f)
    cos, sin = np.tile(cos, (1, 2)), np.concatenate([-sin, sin], 1)
    scale = f(D) ** f(-0.5)
    rope = np.stack([np.stack([cos * scale, cos], 1), np.stack([sin * scale, sin], 1)], 1)
    rope = np.ascontiguousarray(rope.reshape(KT, P, 2, 2, D).transpose(1, 0, 2, 3, 4)).astype(f)
    k = np.arange(S)
    qb = np.arange(KT)[:, None]
    past = (k[None, :] // P) < qb
    tab = np.concatenate([np.where(past, k[None, :] - P * qb, 0), np.where(past, -1, 0)], 0).astype(f)
    one = ((k[None, :] // P) == qb).astype(f)
    q_rows = np.concatenate([one, one * (k[None, :] % P)], 0)
    a = np.arange(P)
    e = np.arange(HL)
    return {
        "head_of": (a[:, None] // D == e[None, :]).astype(f),
        "before": (a[:, None] < a[None, :]).astype(f),
        "iota": np.arange(E, dtype=f),
        "rope": rope,
        "ident": np.eye(P, dtype=f),
        "bias_tab": np.tile(tab, (P // 16, 1)).astype(f),
        "q_rows": np.concatenate([q_rows, q_rows], 0).astype(f),
        "min_mat": np.minimum(a[:, None] - a[None, :], 0).astype(f),
    }


def padded_wo(w):
    out = np.zeros((H, 2 * D, C), w.dtype)
    out[:, :D] = w.T.reshape(H, D, C)
    return out.reshape(H * 2 * D, C)


def padded_rw2(w):
    out = np.zeros((P, HM, 32), w.dtype)
    out[:, :, :E] = w.reshape(HM, P, E).transpose(1, 0, 2)
    return out


_DRAM_IN = {
    "x": ("x", lambda a: a.reshape(T, C)),
    "xT": ("x", lambda a: a.reshape(T, C).T),
    "ctxT": ("ctx_1024", lambda a: a.reshape(B * L, C).T),
    "mask": ("mask_Bx1x1xS2_ik0", lambda a: a.reshape(1, B * L)),
    "wqkvT": ("L0_attn_qkv_w", lambda a: a.T),
    "projT": ("L0_attn_proj_w", lambda a: a.T),
    "proj_b": ("L0_attn_proj_b", lambda a: a),
    "slopes": ("L0_attn_slopes", lambda a: a),
    "slope_rep": ("L0_attn_slopes", lambda a: np.repeat(a, 16).reshape(2, P).T),
    "wqT": ("L0_xattn_Wq", lambda a: a.T),
    "bq2": ("L0_xattn_bq", lambda a: a.reshape(CK, P).T),
    "wkT": ("L0_xattn_Wk", lambda a: a.T),
    "bk2": ("L0_xattn_bk", lambda a: a.reshape(CK, P).T),
    "wvT": ("L0_xattn_Wv", lambda a: a.T),
    "bv": ("L0_xattn_bv", lambda a: a),
    "woT": ("L0_xattn_Wo", padded_wo),
    "bo": ("L0_xattn_bo", lambda a: a),
    "rw1": ("L0_ffn_rw1", lambda a: a),
    "rb1": ("L0_ffn_rb1", lambda a: a.reshape(HM, P).T),
    "rw2": ("L0_ffn_rw2", padded_rw2),
    "rb2": ("L0_ffn_rb2", lambda a: a),
    "ew1": ("L0_ffn_ew1", lambda a: a),
    "eb1": ("L0_ffn_eb1", lambda a: a.reshape(E, HM, P).transpose(2, 0, 1)),
    "ew2": ("L0_ffn_ew2", lambda a: a),
    "eb2": ("L0_ffn_eb2", lambda a: a),
}


def build(nc, io, upto=9):
    nc.disable_value_cache = True

    def scratch(name, shape):
        io[name] = nc.dram_tensor(name, shape, F32, kind="Internal").ap()

    scratch("qk_scr", [NG, 2, 2, HG * D, S])
    scratch("bias_scr", [2, H * 16, S])
    scratch("top_scr", [2, 32, P])
    scratch("att_scr", [NG, P, KT, HG * D])
    scratch("x1_scr", [T, C])
    scratch("q2_scr", [T // CH, 2, CK, P, CH])
    scratch("x2_scr", [T, C])
    scratch("rows_scr", [SLOTS, C])
    scratch("y_scr", [SLOTS, C])
    with nc.semaphore("apart") as apart:
        io["apart"] = apart
        with nc.sbuf_tensor("keep_v", [P, NG, KT, HG * VW], F32) as v:
            stage_qkv(nc, io, {"v": v})
            if upto >= 2:
                stage_attention(nc, io, {"v": v})
        if upto >= 3:
            stage_self_out(nc, io)
        if upto >= 4:
            stage_cross(nc, io)
        if upto >= 5:
            with nc.sbuf_tensor("keep_value", [P, TT, 2], F32) as value, nc.sbuf_tensor("keep_expert", [P, TT, 2], F32) as expert, \
                    nc.sbuf_tensor("keep_get", [P, TT * 2], U32) as get, nc.sbuf_tensor("keep_share", [P, TT * 2], F32) as share:
                keep = {"value": value, "expert": expert, "get": get, "share": share}
                stage_router(nc, io, keep)
                stage_dispatch(nc, io, keep)
                stage_experts(nc, io, keep)
                stage_combine(nc, io, keep)


def kernel(**inputs):
    import concourse.bacc as bacc
    from concourse.bass_utils import run_bass_kernel_spmd

    nc = bacc.Bacc("TRN2", target_bir_lowering=False, num_devices=1)
    arrays = {name: np.ascontiguousarray(layout(np.asarray(inputs[source]))) for name, (source, layout) in _DRAM_IN.items()}
    arrays.update(consts())
    io = {name: nc.dram_tensor(name, a.shape, mybir.dt.from_np(a.dtype), kind="ExternalInput").ap() for name, a in arrays.items()}
    io["out"] = nc.dram_tensor("out", (T, C), F32, kind="ExternalOutput").ap()
    build(nc, io)
    r = run_bass_kernel_spmd(nc, [arrays], core_ids=[0])
    return r.results[0]["out"].reshape(B, S, C)
```

```python
import numpy as np
import concourse.bass as bass
from concourse import mybir
from contextlib import ExitStack

F32 = mybir.dt.float32
F32R = mybir.dt.float32r
BF16 = mybir.dt.bfloat16
I32 = mybir.dt.int32
U32 = mybir.dt.uint32
ALU = mybir.AluOpType
ACT = mybir.ActivationFunctionType
AX = mybir.AxisListType

P = 128
B, S, C = 4, 1024, 256
T = B * S
TT = T // P
H, D = 16, 16
CK = C // P
CH = 512
TPC = CH // P
HG = 4
NG = B * H // HG
KT = S // P
VW = D + 1


class Scope:

    def __init__(self, nc, stage):
        self.nc, self.stage, self.ctx = nc, stage, ExitStack()

    def __enter__(self):
        self.ctx.__enter__()
        return self

    def __exit__(self, *a):
        return self.ctx.__exit__(*a)

    def sb(self, name, shape, dt):
        return self.ctx.enter_context(self.nc.sbuf_tensor(f"{self.stage}_{name}", shape, dt))

    def pb(self, name, shape=(P, 512), dt=F32):
        return self.ctx.enter_context(self.nc.psum_tensor(f"{self.stage}_{name}", list(shape), dt))

    def sem(self, name):
        return self.ctx.enter_context(self.nc.semaphore(f"{self.stage}_{name}"))

    def block(self):
        return self.ctx.enter_context(self.nc.Block())


def wait_alone(eng, sem, value, apart):
    eng.wait_ge(sem, value)
    eng.sem_inc(apart, 1)


def parts3(hi_a, lo_a, hi_b, lo_b):
    return ((hi_a, hi_b), (hi_a, lo_b), (lo_a, hi_b))


def load_stacks(sp, io, g, qs, ks, stack_in):
    for part, qk, tile, row in ((0, 0, qs, 0), (0, 0, qs, 16), (1, 0, qs, 32), (0, 1, ks, 0), (1, 1, ks, 16), (0, 1, ks, 32)):
        src = io["qk_scr"][bass.ds(g.n, 1), part, qk].rearrange("o (h d) t -> (o d) h t", d=D)
        sp.dma_start(tile[row:row + D, :, :].bitcast(F32), src).then_inc(stack_in, 16)
    for part in range(2):
        src = io["bias_scr"][part].rearrange("(h r) t -> r h t", r=16)[:, bass.ds((g.n % HG) * HG, HG), :]
        sp.dma_start(ks[ROW_BIAS + 16 * part:ROW_BIAS + 16 * part + 16, :, :].bitcast(F32), src).then_inc(stack_in, 16)


ROW_BIAS, ROW_MAX, ROWS = 64, 96, P


def stage_qkv(nc, io, keep):
    with Scope(nc, "qkv") as s:
        x_all = s.sb("x_all", [P, CK, T], F32)
        w = s.sb("w", [P, CK, 3 * C], F32)
        w_hi = s.sb("w_hi", [P, CK, 3 * C], F32R)
        w_lo = s.sb("w_lo", [P, CK, 3 * C], F32R)
        x_hi = [s.sb(f"x_hi{i}", [P, CK, CH], F32R) for i in range(2)]
        x_lo = [s.sb(f"x_lo{i}", [P, CK, CH], F32R) for i in range(2)]
        rope = s.sb("rope", [P, KT, 2, 2, D], F32)
        ident, min_mat, slope8, slope_eye = keep["ident"], keep["min_mat"], keep["slope8"], keep["slope_eye"]
        min_t = s.sb("min_t", [P, P], F32)
        slope_bf = s.sb("slope_bf", [P, 3, H], BF16)
        slope_left = s.sb("slope_left", [P, 3, H], F32)
        slope_parts = keep["slope_parts"]
        y_cos = [s.sb(f"y_cos{i}", [P, 2 * C], F32) for i in range(2)]
        y_sin = [s.sb(f"y_sin{i}", [P, 2 * C], F32) for i in range(2)]
        y = [s.sb(f"y{i}", [P, 2 * C], F32) for i in range(2)]
        t_hi = [s.sb(f"t_hi{i}", [P, 4, CH], F32R) for i in range(2)]
        t_lo = [s.sb(f"t_lo{i}", [P, 4, CH], F32R) for i in range(2)]
        btab = s.sb("btab", [P, S], F32)
        bval = s.sb("bval", [P, S], F32)
        b_hi, b_lo = [[t[1][:, 2 * i:2 * i + 2, :].rearrange("p a t -> p (a t)") for i in range(2)] for t in (t_hi, t_lo)]
        slope = s.sb("slope", [P, 2], F32)
        qk_ps = [s.pb(f"qk_ps{i}") for i in range(2)]
        v_ps = [s.pb(f"v_ps{i}") for i in range(2)]
        t_ps = [s.pb(f"t_ps{k}") for k in range(4)]

        w_in = s.sem("w_in")
        x_in = [s.sem(f"x_in{c}") for c in range(2)]
        const_in = s.sem("const_in")
        bias_in = s.sem("bias_in")
        w_split = s.sem("w_split")
        xhi_done = s.sem("xhi_done")
        xlo_done = s.sem("xlo_done")
        qkv_done = s.sem("qkv_done")
        rope_done = s.sem("rope_done")
        v_done = s.sem("v_done")
        y_done = s.sem("y_done")
        t_done = s.sem("t_done")
        thi_done = s.sem("thi_done")
        tlo_done = s.sem("tlo_done")
        out_done = [s.sem(f"out_done{i}") for i in range(2)]
        slope_step = s.sem("slope_step")
        bstep = s.sem("bstep")
        bout = s.sem("bout")
        vones = s.sem("vones")
        rows_done = s.sem("rows_done")
        block = s.block()

        @block.sync
        def _(sp):
            for c in range(2):
                sp.sem_inc(out_done[c], 256)
            sp.dma_start(w[:, :, :], io["wqkvT"].rearrange("(c p) n -> p c n", p=P)).then_inc(w_in, 16)
            sp.dma_start(btab[:, :], io["bias_tab"]).then_inc(bias_in, 16)
            sp.dma_start(slope[:, :], io["slope_rep"]).then_inc(bias_in, 16)
            sp.dma_start(keep["q_rows"][ROW_BIAS:ROW_MAX, :], io["q_rows"]).then_inc(bias_in, 16)
            sp.dma_start(slope8[:, :], io["slopes"].partition_broadcast(P)).then_inc(bias_in, 16)
            sp.dma_start(ident[:, :], io["ident"]).then_inc(bias_in, 16)
            sp.dma_start(min_mat[:, :], io["min_mat"]).then_inc(bias_in, 16)
            sp.dma_start(min_t[:, :], io["min_t"]).then_inc(bias_in, 16)
            xt = io["xT"].rearrange("(c p) t -> p c t", p=P)
            for half in range(2):
                for q in range(2):
                    n0 = half * (T // 2) + q * (T // 4)
                    sp.dma_start(x_all[:, :, n0:n0 + T // 4], xt[:, :, n0:n0 + T // 4]).then_inc(x_in[half], 16)
                if half == 0:
                    sp.dma_start(rope[:, :, :, :, :], io["rope"]).then_inc(const_in, 16)
            for half in range(2):
                sp.wait_ge(bstep, 3 * half + 3)
                for part, tile in ((0, b_hi[half]), (1, b_lo[half])):
                    sp.dma_start(io["bias_scr"][part, half * P:(half + 1) * P, :], tile.bitcast(F32)).then_inc(bout, 16)

            def store(i):
                for c in range(2):
                    sp.wait_ge(thi_done, 2 * i + c + 1)
                    sp.wait_ge(tlo_done, 2 * i + c + 2)
                    for k in range(4):
                        for part, tile in ((0, t_hi[c][:, k, :]), (1, t_lo[c][:, k, :])):
                            for r in range(2):
                                g = i * 4 + 2 * (k % 2) + r
                                sp.dma_start(io["qk_scr"][g, part, k // 2, :, c * CH:(c + 1) * CH],
                                             tile[64 * r:64 * r + 64].bitcast(F32)).then_inc(out_done[c], 16)

            with sp.Fori(0, B - 1) as i:
                store(i)
            for c in range(2):
                sp.wait_ge(out_done[c], 512)
            sp.wait_ge(bout, 64)
            sp.wait_ge(rows_done, 1)
            sp.wait_ge(vones, 3)
            load_stacks(sp, io, Group.of(0), keep["q_stack"], keep["k_stack"], keep["stack_in"])
            store(B - 1)
            for c in range(2):
                sp.wait_ge(out_done[c], 256 * B + 256)

        @block.gpsimd
        def _(pool):
            pool.sem_inc(y_done, 2)
            pool.memset(keep["v"][:, :, :, :], 1.0).then_inc(vones, 1)
            pool.memset(keep["q_stack"][:, :, :].bitcast(F32), 0.0)
            pool.memset(keep["k_stack"][:, :, :].bitcast(F32), 0.0).then_inc(vones, 1)
            pool.wait_ge(vones, 2)
            pool.memset(keep["k_stack"][ROW_MAX:ROW_MAX + 2, :, :].bitcast(F32), 1.0).then_inc(vones, 1)
            pool.wait_ge(vones, 3)
            with pool.Fori(0, B) as i:
                for m in range(8):
                    pool.wait_ge(rope_done, 8 * i + m + 1 + 2)
                    pool.wait_ge(t_done, 8 * i + m + 1)
                    pool.tensor_tensor(y[m % 2][:, :], y_cos[m % 2][:, :], y_sin[m % 2][:, :], ALU.add).then_inc(y_done, 1)

        @block.scalar
        def _(act):
            act.sem_inc(v_done, 2)
            act.wait_ge(w_in, 16)
            nc.scalar.activation(w_hi[:, :, :], w[:, :, :], ACT.Copy).then_inc(w_split, 1)
            act.wait_ge(vones, 2)
            act.wait_ge(bias_in, 112)
            for h in range(HG):
                ins = nc.scalar.activation(keep["q_stack"][ROW_BIAS:ROW_MAX, h, :], keep["q_rows"][ROW_BIAS:ROW_MAX, :], ACT.Copy)
            ins.then_inc(rows_done, 1)
            act.wait_ge(bout, 64)
            with act.Fori(0, B) as i:
                for c in range(2):
                    for half in range(2):
                        act.wait_ge(x_in[half], 32)
                    act.wait_ge(qkv_done, 8 * i + 4 * c + 4)
                    nc.scalar.activation(x_hi[c][:, :, :], x_all[:, :, bass.ds(i * (2 * CH) + c * CH, CH)],
                                         ACT.Copy).then_inc(xhi_done, 1)
                for m in range(8):
                    act.wait_ge(qkv_done, 8 * i + m + 1 + 8)
                    v_out = keep["v"][:, bass.ds(4 * i, 4), m, :].rearrange("p g (h e) -> p g h e", e=VW)
                    nc.scalar.activation(v_out[:, :, :, 0:D], v_ps[m % 2][:, 0:C].rearrange("p (g h d) -> p g h d", g=4, d=D),
                                         ACT.Copy).then_inc(v_done, 1)
                    if m in (4, 7):
                        c = 0 if m == 4 else 1
                        act.wait_ge(t_done, 8 * i + 4 * c + 4 + 2)
                        act.wait_ge(out_done[c], 256 * i + 256)
                        for k in range(4):
                            ins = nc.scalar.activation(t_hi[c][:, k, :], t_ps[k][:, :], ACT.Copy)
                        ins.then_inc(thi_done, 1)

        @block.vector
        def _(dve):
            dve.sem_inc(rope_done, 2)
            dve.sem_inc(tlo_done, 1)
            dve.wait_ge(bias_in, 112)
            for half in range(2):
                nc.vector.tensor_scalar(bval[:, :], btab[:, :], slope[:, half:half + 1], 8.0, ALU.mult, ALU.mult).then_inc(bstep, 1)
                dve.wait_ge(bstep, 3 * half + 1)
                nc.vector.tensor_copy(b_hi[half], bval[:, :]).then_inc(bstep, 1)
                dve.wait_ge(bstep, 3 * half + 2)
                nc.vector.tensor_tensor(b_lo[half], bval[:, :], b_hi[half].bitcast(F32), ALU.subtract).then_inc(bstep, 1)
                dve.wait_ge(bstep, 3 * half + 3)
            nc.vector.tensor_copy(keep["min_bf"][:, :], min_mat[:, :])
            nc.vector.tensor_copy(keep["min_t_bf"][:, :], min_t[:, :])
            nc.vector.tensor_scalar(slope8[:, :], slope8[:, :], 8.0, None, ALU.mult).then_inc(slope_step, 1)
            dve.wait_ge(slope_step, 1)
            for part in range(3):
                left = slope_left[:, part, :] if part else slope8[:, :]
                nc.vector.tensor_copy(slope_bf[:, part, :], left).then_inc(slope_step, 1)
                dve.wait_ge(slope_step, 2 * part + 2)
                if part < 2:
                    nc.vector.tensor_tensor(slope_left[:, part + 1, :], left, slope_bf[:, part, :], ALU.subtract).then_inc(slope_step, 1)
                    dve.wait_ge(slope_step, 2 * part + 3)
            nc.vector.tensor_copy(slope_parts[:, :, :], slope_bf[:, :, :]).then_inc(slope_step, 1)
            dve.wait_ge(slope_step, 7)
            for h in range(H):
                nc.vector.tensor_scalar(slope_eye[:, 0, h, :], ident[:, :], slope_parts[:, 0, h:h + 1], None, ALU.mult)
            dve.wait_ge(w_split, 1)
            nc.vector.tensor_tensor(w_lo[:, :, :], w[:, :, :], w_hi[:, :, :].bitcast(F32), ALU.subtract).then_inc(w_split, 1)
            dve.wait_ge(const_in, 16)
            with dve.Fori(0, B) as i:
                for c in range(2):
                    dve.wait_ge(xhi_done, 2 * i + c + 1)
                    nc.vector.tensor_tensor(x_lo[c][:, :, :], x_all[:, :, bass.ds(i * (2 * CH) + c * CH, CH)],
                                            x_hi[c][:, :, :].bitcast(F32), ALU.subtract).then_inc(xlo_done, 1)
                for m in range(8):
                    dve.wait_ge(qkv_done, 8 * i + m + 1 + 8)
                    dve.wait_ge(y_done, 8 * i + m + 1)
                    qk = qk_ps[m % 2][:, :].rearrange("p (k h d) -> p k h d", k=2, h=H)
                    swapped = qk_ps[m % 2][:, :].rearrange("p (k h s e) -> p k h s e", k=2, h=H, s=2)[:, :, :, ::-1, :]
                    cos = rope[:, m, 0, :, :].unsqueeze(2).to_broadcast([P, 2, H, D])
                    nc.vector.tensor_tensor(y_cos[m % 2][:, :].rearrange("p (k h d) -> p k h d", k=2, h=H), qk, cos, ALU.mult)
                    for k in range(2):
                        sin = rope[:, m, 1, k, :].rearrange("p (s e) -> p s e", s=2).unsqueeze(1).to_broadcast([P, H, 2, D // 2])
                        ins = nc.vector.tensor_tensor(
                            y_sin[m % 2][:, k * C:(k + 1) * C].rearrange("p (h s e) -> p h s e", h=H, s=2),
                            swapped[:, k], sin, ALU.mult)
                    ins.then_inc(rope_done, 1)
                    if m in (4, 7):
                        c = 0 if m == 4 else 1
                        dve.wait_ge(thi_done, 2 * i + c + 1)
                        for k in range(4):
                            ins = nc.vector.tensor_tensor(t_lo[c][:, k, :], t_ps[k][:, :], t_hi[c][:, k, :].bitcast(F32), ALU.subtract)
                        ins.then_inc(tlo_done, 1)

        @block.tensor
        def _(pe):
            pe.sem_inc(qkv_done, 8)
            pe.sem_inc(t_done, 2)
            pe.wait_ge(w_split, 2)
            pe.wait_ge(bias_in, 112)

            def transposes(i, m):
                pe.wait_ge(y_done, 8 * i + m + 1 + 2)
                if m % 4 == 0:
                    pe.wait_ge(tlo_done, 2 * i + m // 4 + 1)
                for k in range(4):
                    ins = nc.tensor.transpose(t_ps[k][:, (m % 4) * P:(m % 4 + 1) * P], y[m % 2][:, k * P:(k + 1) * P], ident[:, :])
                ins.then_inc(t_done, 1)

            with pe.Fori(0, B) as i:
                for m in range(8):
                    c = m // 4
                    if m % 4 == 0:
                        pe.wait_ge(xlo_done, 2 * i + c + 1)
                    pe.wait_ge(rope_done, 8 * i + m + 1)
                    pe.wait_ge(v_done, 8 * i + m + 1)
                    tok = slice((m % 4) * P, (m % 4 + 1) * P)
                    for out, cols in ((qk_ps[m % 2][:, :], slice(0, 2 * C)), (v_ps[m % 2][:, 0:C], slice(2 * C, 3 * C))):
                        prods = [(a[:, kc, tok], b[:, kc, cols]) for kc in range(CK)
                                 for a, b in parts3(x_hi[c], x_lo[c], w_hi, w_lo)]
                        for n, (a, b) in enumerate(prods):
                            ins = nc.tensor.matmul(out, a, b, start=(n == 0), stop=(n == len(prods) - 1))
                    ins.then_inc(qkv_done, 1)
                    if m:
                        transposes(i, m - 1)
                transposes(i, 7)


class Group:

    def __init__(self, n, buf, lap):
        self.n, self.buf, self.lap = n, buf, lap

    @staticmethod
    def of(n):
        return Group(n, n % 3, n // 3)

    def plus(self, k):
        if isinstance(self.n, int):
            return Group.of(self.n + k)
        b = self.buf + k
        return Group(self.n + k, b % 3, self.lap + b // 3)


def windows(eng, window):
    window(Group.of(0), True, False)
    with eng.Fori(0, 4) as i:
        for u in range(3):
            g = Group(3 * i + (u + 1), (u + 1) % 3, i + (u + 1) // 3)
            window(g, True, True)
    for n in range(13, NG):
        window(Group.of(n), n < NG - 1, True)


STEPS = 2 * KT
TILES = 4 * STEPS
RING = 3
TOP0_AT = 39


def ring_order(first, with_max):
    order = []
    for st in range(STEPS):
        order += [("max", 4 * st + h) for h in range(4) if with_max]
        if st == 1:
            order.append(("top", 1))
        if st == 2 and not first:
            order.append(("acc", 1))
        if st == 9 and with_max:
            order.append(("top", 0))
        if st == 10:
            order.append(("acc", 0))
    return order


PROLOGUE = [("max", u) for u in range(TOP0_AT + 1)] + [("top", 0)] + [("max", u) for u in range(TOP0_AT + 1, TILES)]
FIRST, MIDDLE, LAST = ring_order(True, True), ring_order(False, True), ring_order(False, False)


class Place:

    def __init__(self, g, what):
        n = None if g is None else g.n
        if n is None:
            at, order, bank0 = 0, PROLOGUE, 0
        elif isinstance(n, int) and n == 0:
            at, order, bank0 = len(PROLOGUE), FIRST, len(PROLOGUE)
        else:
            short = len(PROLOGUE) + len(FIRST) - len(MIDDLE)
            at, bank0 = short + len(MIDDLE) * n, short + len(MIDDLE) * g.buf
            order = LAST if isinstance(n, int) and n == NG - 1 else MIDDLE
            if what == ("acc", "end"):
                self.at, self.bank = at + len(LAST), (bank0 + len(LAST)) % RING
                return
        i = order.index(what)
        self.at, self.bank = at + i, (bank0 + i) % RING
def stage_attention(nc, io, keep):
    with Scope(nc, "att") as s:
        qs = [keep["q_stack"]] + [s.sb(f"q_stack{i}", [P, HG, S], F32R) for i in (1, 2)]
        ks = [keep["k_stack"]] + [s.sb(f"k_stack{i}", [P, HG, S], F32R) for i in (1, 2)]
        vg = [s.sb(f"v_group{i}", [P, KT, HG * VW + 32 - VW + 1], F32) for i in range(3)]
        w_exp = [[s.sb(f"w_exp{i}{h}", [P, CH], F32) for h in range(HG)] for i in range(2)]
        ident, min_mat, min_bf, min_t_bf = keep["ident"], keep["min_mat"], keep["min_bf"], keep["min_t_bf"]
        slope8, slope_eye = keep["slope8"], keep["slope_eye"]
        zeros = s.sb("zeros", [P, 8 * C], F32)
        row_max = [s.sb(f"row_max{i}", [P, HG * 4, 2], F32) for i in range(2)]
        top = s.sb("top", [P, HG * 4], F32)
        neg_top = s.sb("neg_top", [P, 2, HG * 4], F32R)
        neg_top_t = [s.sb(f"neg_top_t{i}", [32, P], F32R) for i in range(2)]
        acc_sb = [s.sb(f"acc_sb{i}", [P, CH], F32) for i in range(2)]
        recip = s.sb("recip", [P, 4, HG], F32)
        att = [s.sb(f"att{i}", [P, 4, HG, D], F32) for i in range(2)]
        s_ps = [s.pb(f"s_ps{h}") for h in range(HG)]
        ring = [s.pb(f"ring{i}") for i in range(3)]
        a_ps = s.pb("a_ps")

        stack_in = [keep["stack_in"]] + [s.sem(f"stack_in{i}") for i in (1, 2)]
        top_in = [s.sem(f"top_in{i}") for i in range(2)]
        top_out = [s.sem(f"top_out{i}") for i in range(2)]
        score_done = s.sem("score_done")
        diag_done = s.sem("diag_done")
        exp_done = s.sem("exp_done")
        pv_done = s.sem("pv_done")
        acc_done = s.sem("acc_done")
        recip_done = s.sem("recip_done")
        att_out = [s.sem(f"att_out{i}") for i in range(2)]
        ring_full = s.sem("ring_full")
        ring_free = s.sem("ring_free")
        top_step = s.sem("top_step")
        top_ready = s.sem("top_ready")
        top_copied = s.sem("top_copied")
        v_ready = s.sem("v_ready")
        pool_prep = s.sem("pool_prep")
        act_prep = s.sem("act_prep")
        zeroed = s.sem("zeroed")
        block = s.block()

        def move_top(sp, g, half, place):
            sp.wait_ge(ring_free, place.at + 1 + RING)
            sp.dma_start(io["top_scr"][half], neg_top_t[half][:, :].bitcast(F32)).then_inc(top_out[half], 16)
            sp.wait_ge(top_out[half], 16 * g.n + 32)
            sp.dma_start(qs[g.buf][ROW_MAX:ROW_MAX + 2, :, half * CH:(half + 1) * CH].bitcast(F32),
                         io["top_scr"][half].rearrange("(a h q) t -> a h (q t)", a=2, h=HG)).then_inc(top_in[half], 16)

        def store_att(sp, g, c, place):
            sp.wait_ge(ring_free, place.at + 1 + RING)
            sp.dma_start(io["att_scr"][bass.ds(g.n, 1), :, 4 * c:4 * c + 4, :].rearrange("o p q e -> (o p) q e"),
                         att[c][:, :, :, :].rearrange("p q h d -> p q (h d)")).then_inc(att_out[c], 16)

        @block.sync
        def _(sp):
            for half in range(2):
                sp.sem_inc(top_out[half], 16)
                sp.sem_inc(att_out[half], 16)
            sp.wait_ge(pool_prep, 2)
            sp.wait_ge(act_prep, 2)
            load_stacks(sp, io, Group.of(1), qs[1], ks[1], stack_in[1])
            move_top(sp, Group.of(0), 0, Place(None, ("top", 0)))

            def window(g, with_max, has_last):
                if has_last:
                    sp.wait_ge(score_done, TILES * g.n)
                if not isinstance(g.n, int) or g.n < NG - 2:
                    if isinstance(g.n, int) and g.n == 0:
                        sp.wait_ge(pool_prep, 4)
                        sp.wait_ge(act_prep, 3)
                    new = g.plus(2)
                    load_stacks(sp, io, new, qs[new.buf], ks[new.buf], stack_in[new.buf])
                move_top(sp, g, 1, Place(g, ("top", 1)))
                if has_last:
                    store_att(sp, g.plus(-1), 1, Place(g, ("acc", 1)))
                if with_max:
                    move_top(sp, g.plus(1), 0, Place(g, ("top", 0)))
                store_att(sp, g, 0, Place(g, ("acc", 0)))

            windows(sp, window)
            last = Group.of(NG - 1)
            store_att(sp, last, 1, Place(last, ("acc", "end")))
            for c in range(2):
                sp.wait_ge(att_out[c], 16 * NG + 16)

        @block.gpsimd
        def _(pool):
            for i in (1, 2):
                pool.memset(qs[i][:, :, :].bitcast(F32), 0.0)
                pool.memset(ks[i][:, :, :].bitcast(F32), 0.0).then_inc(pool_prep, 1)
                pool.wait_ge(pool_prep, 2 * i - 1)
                pool.memset(ks[i][ROW_MAX:ROW_MAX + 2, :, :].bitcast(F32), 1.0).then_inc(pool_prep, 1)
                pool.wait_ge(pool_prep, 2 * i)
                if i == 1:
                    for j in range(3):
                        pool.memset(vg[j][:, :, :], 0.0)
            pool.memset(zeros[:, :], 0.0).then_inc(pool_prep, 1)
            pool.wait_ge(pool_prep, 5)
            rows = io["rows_scr"].rearrange("(a p r) e -> a p (r e)", a=8, p=P)
            for a in range(8):
                pool.dma_start(rows[a], zeros[:, :]).then_inc(zeroed, 16)

            def take_v(g):
                dst = vg[g.buf][:, :, 0:HG * VW].unsqueeze(1)
                pool.tensor_copy(dst, keep["v"][:, bass.ds(g.n, 1), :, :]).then_inc(v_ready, 1)

            take_v(Group.of(0))

            def window(g, with_max, has_last):
                if with_max:
                    if has_last:
                        pool.wait_ge(pv_done, STEPS * (g.n - 1) + 2)
                    take_v(g.plus(1))

            windows(pool, window)
            pool.wait_ge(zeroed, 128)

        @block.scalar
        def _(act):
            act.sem_inc(exp_done, 4)
            act.sem_inc(acc_done, 1)
            for part in (1, 2):
                for h in range(H):
                    ins = nc.scalar.activation(slope_eye[:, part, h, :], ident[:, :], ACT.Copy, scale=keep["slope_parts"][:, part, h:h + 1])
            ins.then_inc(act_prep, 1)
            for i in (1, 2):
                act.wait_ge(pool_prep, 2 * i - 1)
                for h in range(HG):
                    ins = nc.scalar.activation(qs[i][ROW_BIAS:ROW_MAX, h, :], keep["q_rows"][ROW_BIAS:ROW_MAX, :], ACT.Copy)
                ins.then_inc(act_prep, 1)

            def copy_acc(g, c):
                act.wait_ge(pv_done, STEPS * g.n + KT * (c + 1) + 2)
                nc.scalar.activation(acc_sb[c][:, :], a_ps[:, :], ACT.Copy).then_inc(acc_done, 1)

            def window(g, with_max, has_last):
                for st in range(STEPS):
                    c, kt = divmod(st, KT)
                    for h in range(HG):
                        if kt // 4 == c and h % 2 == 0:
                            f = (2 * st if c == 0 else 8 + 2 * (st - 12)) + h // 2
                            act.wait_ge(diag_done, 16 * g.n + f + 1)
                        else:
                            act.wait_ge(score_done, 64 * g.n + 4 * st + h + 1)
                        if h == 0:
                            act.wait_ge(pv_done, STEPS * g.n + st + 1)
                        nc.scalar.activation(w_exp[st % 2][h][:, :], s_ps[h][:, :], ACT.Exp).then_inc(exp_done, 1)
                        if st == 1 and h == 1 and has_last:
                            copy_acc(g.plus(-1), 1)
                        if st == 9 and h == 1:
                            copy_acc(g, 0)

            windows(act, window)
            copy_acc(Group.of(NG - 1), 1)

        @block.vector
        def _(dve):
            dve.sem_inc(ring_free, RING)
            def maxima(g, u, place):
                dve.wait_ge(ring_full, place.at + 1)
                half, v = divmod(u, 32)
                nc.vector.tensor_reduce(row_max[half][:, v // 2, v % 2:v % 2 + 1], ring[place.bank][:, :], AX.X, ALU.max).then_inc(ring_free, 1)

            def top_parts(g, half, place):
                dve.wait_ge(ring_free, place.at + 1 + RING)
                nc.vector.tensor_reduce(top[:, :], row_max[half][:, :, :], AX.X, ALU.max).then_inc(top_step, 1)
                dve.wait_ge(top_step, 4 * g.n + 2 * half + 1)
                nc.vector.tensor_scalar(neg_top[:, 0, :], top[:, :], -1.0, None, ALU.mult).then_inc(top_step, 1)
                dve.wait_ge(top_step, 4 * g.n + 2 * half + 2)
                nc.vector.scalar_tensor_tensor(neg_top[:, 1, :], top[:, :], -1.0, neg_top[:, 0, :].bitcast(F32),
                                               ALU.mult, ALU.subtract).then_inc(top_ready, 1)

            def copy_top(g, half, place):
                dve.wait_ge(ring_full, place.at + 1)
                dve.wait_ge(top_out[half], 16 * g.n + 16)
                nc.vector.tensor_copy(neg_top_t[half][:, :], ring[place.bank][0:32, 0:P]).then_inc(ring_free, 1)

            def normalise(g, c, place):
                dve.wait_ge(ring_full, place.at + 1)
                sums = ring[place.bank][:, :].rearrange("p (q h e) -> p q h e", q=4, h=HG)
                nc.vector.reciprocal(recip[:, :, :], sums[:, :, :, D]).then_inc(recip_done, 1)
                dve.wait_ge(recip_done, 2 * g.n + c + 1)
                dve.wait_ge(att_out[c], 16 * g.n + 16)
                nc.vector.tensor_tensor(att[c][:, :, :, :], sums[:, :, :, 0:D],
                                        recip[:, :, :].unsqueeze(3).to_broadcast([P, 4, HG, D]), ALU.mult).then_inc(ring_free, 1)

            g0 = Group.of(0)
            for u in range(TILES):
                place = Place(None, ("max", u))
                maxima(g0, u, place)
                if u % 32 == 31:
                    top_parts(g0, u // 32, place)
                if u == TOP0_AT:
                    copy_top(g0, 0, Place(None, ("top", 0)))

            def window(g, with_max, has_last):
                for st in range(STEPS):
                    c, kt = divmod(st, KT)
                    for h in range(HG):
                        if kt // 4 == c and h % 2 == 0:
                            dve.wait_ge(score_done, TILES * g.n + 4 * st + h + 1)
                            d = s_ps[h][:, (kt % 4) * P:(kt % 4 + 1) * P]
                            slope = slope8[:, bass.ds((g.n % HG) * HG + h, 1)]
                            nc.vector.scalar_tensor_tensor(d, min_mat[:, :], slope, d, ALU.mult, ALU.add).then_inc(diag_done, 1)
                        if with_max:
                            maxima(g.plus(1), 4 * st + h, Place(g, ("max", 4 * st + h)))
                    if with_max and st % 8 == 7:
                        top_parts(g.plus(1), st // 8, Place(g, ("max", 4 * st + 3)))
                    if st == 1:
                        copy_top(g, 1, Place(g, ("top", 1)))
                    if st == 2 and has_last:
                        normalise(g.plus(-1), 1, Place(g, ("acc", 1)))
                    if st == 9 and with_max:
                        copy_top(g.plus(1), 0, Place(g, ("top", 0)))
                    if st == 10:
                        normalise(g, 0, Place(g, ("acc", 0)))

            windows(dve, window)
            last = Group.of(NG - 1)
            normalise(last, 1, Place(last, ("acc", "end")))

        @block.tensor
        def _(pe):
            pe.sem_inc(pv_done, 2)

            def max_scores(g, u, place):
                half, v = divmod(u, 32)
                h, v = divmod(v, 8)
                qt, kk = half * 4 + v // 2, v % 2
                pe.wait_ge(ring_free, place.at + 1)
                diag = qt // 4 == kk
                out = ring[place.bank]
                ins = nc.tensor.matmul(out[:, :], qs[g.buf][0:ROW_MAX, h, qt * P:(qt + 1) * P],
                                       ks[g.buf][0:ROW_MAX, h, kk * CH:(kk + 1) * CH], start=True, stop=not diag)
                if diag:
                    ins = nc.tensor.matmul(out[:, (qt % 4) * P:(qt % 4 + 1) * P], min_bf[:, :],
                                           slope_eye[:, 0, bass.ds((g.n % HG) * HG + h, 1), :].rearrange("p o q -> p (o q)"),
                                           start=False, stop=True)
                ins.then_inc(ring_full, 1)

            def transpose_top(g, half, place):
                pe.wait_ge(top_ready, 2 * g.n + half + 1)
                pe.wait_ge(ring_free, place.at + 1)
                nc.tensor.transpose(ring[place.bank][0:32, 0:P], neg_top[:, :, :].rearrange("p a b -> p (a b)").bitcast(F32),
                                    ident[:, :]).then_inc(ring_full, 1)

            def values(g, st):
                c, kt = divmod(st, KT)
                pe.wait_ge(exp_done, 64 * g.n + 4 * st + 4 + 4)
                if st == 0:
                    pe.wait_ge(v_ready, g.n + 1)
                if kt == 0:
                    pe.wait_ge(acc_done, 2 * g.n + c + 1)
                for h in range(HG):
                    ins = nc.tensor.matmul(a_ps[32 * h:32 * h + 32, :], vg[g.buf][:, kt, h * VW:h * VW + 32],
                                           w_exp[st % 2][h][:, :], start=(kt == 0), stop=(kt == KT - 1))
                ins.then_inc(pv_done, 1)

            def transpose_acc(g, c, place):
                pe.wait_ge(acc_done, 2 * g.n + c + 1 + 1)
                pe.wait_ge(ring_free, place.at + 1)
                for q in range(4):
                    ins = nc.tensor.transpose(ring[place.bank][:, q * P:(q + 1) * P], acc_sb[c][:, q * P:(q + 1) * P], ident[:, :])
                ins.then_inc(ring_full, 1)

            g0 = Group.of(0)
            pe.wait_ge(stack_in[0], 128)
            for u in range(TILES):
                max_scores(g0, u, Place(None, ("max", u)))
                if u == TOP0_AT:
                    transpose_top(g0, 0, Place(None, ("top", 0)))

            def window(g, with_max, has_last):
                if with_max:
                    n = g.plus(1)
                    pe.wait_ge(stack_in[n.buf], 128 * n.lap + 128)
                for st in range(STEPS):
                    c, kt = divmod(st, KT)
                    if kt == 0:
                        pe.wait_ge(top_in[c], 16 * g.n + 16)
                    for h in range(HG):
                        pe.wait_ge(exp_done, TILES * g.n + 4 * st + h + 1)
                        diag = kt // 4 == c and h % 2 == 1
                        ins = nc.tensor.matmul(s_ps[h][:, :], ks[g.buf][:, h, kt * P:(kt + 1) * P],
                                               qs[g.buf][:, h, c * CH:(c + 1) * CH], start=True, stop=not diag)
                        for part in range(3 if diag else 0):
                            eye = slope_eye[:, part, bass.ds((g.n % HG) * HG + h, 1), :].rearrange("p o q -> p (o q)")
                            ins = nc.tensor.matmul(s_ps[h][:, (kt % 4) * P:(kt % 4 + 1) * P], min_t_bf[:, :], eye, start=False, stop=part == 2)
                        ins.then_inc(score_done, 1)
                        if with_max:
                            max_scores(n, 4 * st + h, Place(g, ("max", 4 * st + h)))
                    if st:
                        values(g, st - 1)
                    elif has_last:
                        values(g.plus(-1), STEPS - 1)
                    if st == 1:
                        transpose_top(g, 1, Place(g, ("top", 1)))
                    if st == 2 and has_last:
                        transpose_acc(g.plus(-1), 1, Place(g, ("acc", 1)))
                    if st == 9 and with_max:
                        transpose_top(n, 0, Place(g, ("top", 0)))
                    if st == 10:
                        transpose_acc(g, 0, Place(g, ("acc", 0)))

            pe.wait_ge(act_prep, 1)
            windows(pe, window)
            last = Group.of(NG - 1)
            values(last, STEPS - 1)
            transpose_acc(last, 1, Place(last, ("acc", "end")))


EPS = 1e-5


class Norm:

    def __init__(self, nc, s, apart):
        self.nc, self.apart = nc, apart
        self.stats = s.sb("stats", [P, TPC, 6], F32)
        self.mv = s.sb("mv", [P, TPC, 2], F32)
        self.var = s.sb("var", [P, TPC, 1], F32)
        self.root = s.sb("root", [P, TPC, 1], F32)
        self.inv = s.sb("inv", [P, TPC, 1], F32)
        self.half = s.sb("half", [P, TPC, 1], F32)
        self.step = s.sem("norm_step")
        self.root_done = s.sem("root_done")

    def apply(self, dve, n, x, out):
        self.moments(dve, n, x)
        return self.scale(dve, n, x, out)

    def moments(self, dve, n, x):
        nc, at = self.nc, 7 * n
        for t in range(TPC):
            ins = nc.vector.bn_stats(self.stats[:, t, :], x[:, t, :])
        ins.then_inc(self.step, 1)
        wait_alone(dve, self.step, at + 1, self.apart)
        for t in range(TPC):
            ins = nc.vector.bn_aggr(self.mv[:, t, :], self.stats[:, t, :])
        ins.then_inc(self.step, 1)
        dve.wait_ge(self.step, at + 2)
        nc.vector.tensor_scalar(self.var[:, :, :], self.mv[:, :, 1:2], EPS, None, ALU.add).then_inc(self.step, 1)

    def scale(self, dve, n, x, out):
        nc, at = self.nc, 7 * n
        dve.wait_ge(self.root_done, n + 1)
        nc.vector.reciprocal(self.inv[:, :, :], self.root[:, :, :]).then_inc(self.step, 1)
        dve.wait_ge(self.step, at + 4)
        nc.vector.scalar_tensor_tensor(self.half[:, :, :], self.inv[:, :, :], -0.5, self.var[:, :, :], ALU.mult, ALU.mult).then_inc(self.step, 1)
        dve.wait_ge(self.step, at + 5)
        nc.vector.tensor_tensor(self.half[:, :, :], self.half[:, :, :], self.inv[:, :, :], ALU.mult).then_inc(self.step, 1)
        dve.wait_ge(self.step, at + 6)
        nc.vector.scalar_tensor_tensor(self.inv[:, :, :], self.half[:, :, :], 1.5, self.inv[:, :, :], ALU.add, ALU.mult).then_inc(self.step, 1)
        dve.wait_ge(self.step, at + 7)
        for t in range(TPC):
            ins = nc.vector.tensor_scalar(out[:, t, :], x[:, t, :], self.mv[:, t, 0:1], self.inv[:, t, :], ALU.subtract, ALU.mult)
        return ins

    def take_root(self, act, n):
        act.wait_ge(self.step, 7 * n + 3)
        self.nc.scalar.activation(self.root[:, :, :], self.var[:, :, :], ACT.Sqrt).then_inc(self.root_done, 1)


def chunk_rows(ap, n):
    return ap.rearrange("(n t p) e -> n p t e", p=P, t=TPC)[n]


def stage_self_out(nc, io):
    with Scope(nc, "so") as s:
        w_raw = s.sb("w_raw", [P, 2, CK, C], F32)
        w_hi = s.sb("w_hi", [P, 2, CK, C], F32R)
        w_lo = s.sb("w_lo", [P, 2, CK, C], F32R)
        proj_b = s.sb("proj_b", [P, C], F32)
        bq = s.sb("bq", [P, CK], F32)
        ident = s.sb("ident", [P, P], F32)
        att = [s.sb(f"att{i}", [P, TPC, C], F32) for i in range(2)]
        x = [s.sb(f"x{i}", [P, TPC, C], F32) for i in range(2)]
        a_hi = [s.sb(f"a_hi{i}", [P, CK, CH], F32R) for i in range(2)]
        a_lo = [s.sb(f"a_lo{i}", [P, CK, CH], F32R) for i in range(2)]
        res = [s.sb(f"res{i}", [P, TPC, C], F32) for i in range(2)]
        x1 = [s.sb(f"x1{i}", [P, TPC, C], F32) for i in range(2)]
        x1_hi = [s.sb(f"x1_hi{i}", [P, CK, CH], F32R) for i in range(2)]
        x1_lo = [s.sb(f"x1_lo{i}", [P, CK, CH], F32R) for i in range(2)]
        q_sum = [s.sb(f"q_sum{i}", [P, CK, CH], F32) for i in range(2)]
        q_hi = [s.sb(f"q_hi{i}", [P, CK, CH], F32R) for i in range(2)]
        q_lo = [s.sb(f"q_lo{i}", [P, CK, CH], F32R) for i in range(2)]
        norm = Norm(nc, s, io["apart"])
        t_ps = s.pb("t_ps", (P, CK, CH))
        r_ps = s.pb("r_ps", (P, TPC, C))
        t1_ps = s.pb("t1_ps", (P, CK, CH))
        q_ps = s.pb("q_ps", (P, CK, CH))

        const_in = s.sem("const_in")
        w_split = s.sem("w_split")
        in_done = [s.sem(f"in_done{i}") for i in range(2)]
        t_done, t_hi, t_lo = s.sem("t_done"), s.sem("t_hi"), s.sem("t_lo")
        r_done, x_biased = s.sem("r_done"), s.sem("x_biased")
        res_done, x1_done = s.sem("res_done"), s.sem("x1_done")
        t1_done, x1_hi_done, x1_lo_done = s.sem("t1_done"), s.sem("x1_hi_done"), s.sem("x1_lo_done")
        q_done, q_sum_done = s.sem("q_done"), s.sem("q_sum_done")
        q_hi_done, q_lo_done = s.sem("q_hi_done"), s.sem("q_lo_done")
        out_done = [s.sem(f"out_done{i}") for i in range(2)]
        block = s.block()

        @block.sync
        def _(sp):
            for j, name in enumerate(("projT", "wqT")):
                sp.dma_start(w_raw[:, j], io[name].rearrange("(c p) n -> p c n", p=P)).then_inc(const_in, 16)
            sp.dma_start(ident[:, :], io["ident"]).then_inc(const_in, 16)
            sp.dma_start(proj_b[:, :], io["proj_b"].partition_broadcast(P)).then_inc(const_in, 16)
            sp.dma_start(bq[:, :], io["bq2"]).then_inc(const_in, 16)
            for c in range(2):
                sp.sem_inc(out_done[c], 48)
            def load(i, c):
                n = 2 * i + c
                sp.wait_ge(r_done, n + 1)
                sp.wait_ge(res_done, n + 1)
                for hq in range(4):
                    src = io["att_scr"][bass.ds(4 * i + hq, 1), :, 4 * c:4 * c + 4, :].rearrange("o p q e -> (o p) q e")
                    sp.dma_start(att[c][:, :, hq * 64:hq * 64 + 64], src).then_inc(in_done[c], 16)
                sp.dma_start(x[c][:, :, :], io["x"].rearrange("(n t p) e -> n p t e", p=P, t=TPC)[n]).then_inc(in_done[c], 16)

            def store(i, c):
                n = 2 * i + c
                sp.wait_ge(x1_done, n + 1 + 2)
                sp.dma_start(io["x1_scr"].rearrange("(n t p) e -> n p t e", p=P, t=TPC)[n], x1[c][:, :, :]).then_inc(out_done[c], 16)
                sp.wait_ge(q_lo_done, n + 1 + 2)
                for part, tile in ((0, q_hi[c]), (1, q_lo[c])):
                    sp.dma_start(io["q2_scr"][n, part].rearrange("k p t -> p k t"), tile[:, :, :].bitcast(F32)).then_inc(out_done[c], 16)

            load(0, 0)
            load(0, 1)
            with sp.Fori(0, B - 1) as i:
                for c in range(2):
                    load(i + 1, c)
                for c in range(2):
                    store(i, c)
            for c in range(2):
                store(B - 1, c)
            for c in range(2):
                sp.wait_ge(out_done[c], 48 * B + 48)

        @block.gpsimd
        def _(pool):
            pool.wait_ge(const_in, 80)
            with pool.Fori(0, B) as i:
                for c in range(2):
                    n = 2 * i + c
                    pool.wait_ge(in_done[c], 80 * i + 80)
                    pool.tensor_tensor(x[c][:, :, :], x[c][:, :, :], proj_b[:, :].unsqueeze(1).to_broadcast([P, TPC, C]), ALU.add).then_inc(x_biased, 1)

        @block.scalar
        def _(act):
            act.sem_inc(t_hi, 1)
            act.sem_inc(x1_hi_done, 1)
            act.wait_ge(const_in, 80)
            nc.scalar.activation(w_hi[:, :, :, :], w_raw[:, :, :, :], ACT.Copy).then_inc(w_split, 1)
            with act.Fori(0, B) as i:
                def split_att(c):
                    n = 2 * i + c
                    act.wait_ge(t_done, n + 1)
                    act.wait_ge(r_done, n + 1)
                    nc.scalar.activation(a_hi[c][:, :, :], t_ps[:, :, :], ACT.Copy).then_inc(t_hi, 1)

                def split_x1(c):
                    n = 2 * i + c
                    act.wait_ge(t1_done, n + 1)
                    act.wait_ge(q_done, n + 1)
                    nc.scalar.activation(x1_hi[c][:, :, :], t1_ps[:, :, :], ACT.Copy).then_inc(x1_hi_done, 1)

                def split_q(c):
                    n = 2 * i + c
                    act.wait_ge(q_sum_done, n + 1 + 1)
                    act.wait_ge(out_done[c], 48 * i + 48)
                    nc.scalar.activation(q_hi[c][:, :, :], q_sum[c][:, :, :], ACT.Copy).then_inc(q_hi_done, 1)

                split_att(0)
                split_att(1)
                for c in range(2):
                    norm.take_root(act, 2 * i + c)
                split_x1(0)
                split_q(0)
                split_x1(1)
                split_q(1)

        @block.vector
        def _(dve):
            dve.sem_inc(t_lo, 1)
            dve.sem_inc(x1_lo_done, 1)
            dve.sem_inc(q_sum_done, 1)
            dve.sem_inc(res_done, 2)
            dve.sem_inc(x1_done, 2)
            dve.sem_inc(q_lo_done, 2)
            dve.wait_ge(w_split, 1)
            nc.vector.tensor_tensor(w_lo[:, :, :, :], w_raw[:, :, :, :], w_hi[:, :, :, :].bitcast(F32), ALU.subtract).then_inc(w_split, 1)
            with dve.Fori(0, B) as i:
                def split_att(c):
                    dve.wait_ge(t_hi, 2 * i + c + 1 + 1)
                    nc.vector.tensor_tensor(a_lo[c][:, :, :], t_ps[:, :, :], a_hi[c][:, :, :].bitcast(F32), ALU.subtract).then_inc(t_lo, 1)

                def normalise(c):
                    n = 2 * i + c
                    dve.wait_ge(r_done, n + 1 + 2)
                    dve.wait_ge(x_biased, n + 1)
                    nc.vector.tensor_tensor(res[c][:, :, :], r_ps[:, :, :], x[c][:, :, :], ALU.add).then_inc(res_done, 1)
                    dve.wait_ge(res_done, n + 1 + 2)
                    dve.wait_ge(out_done[c], 48 * i + 48)
                    norm.apply(dve, n, res[c], x1[c]).then_inc(x1_done, 1)

                def split_x1(c):
                    dve.wait_ge(x1_hi_done, 2 * i + c + 1 + 1)
                    nc.vector.tensor_tensor(x1_lo[c][:, :, :], t1_ps[:, :, :], x1_hi[c][:, :, :].bitcast(F32), ALU.subtract).then_inc(x1_lo_done, 1)

                def bias_q(c):
                    n = 2 * i + c
                    dve.wait_ge(q_done, n + 1 + 2)
                    for k in range(CK):
                        ins = nc.vector.tensor_scalar(q_sum[c][:, k, :], q_ps[:, k, :], bq[:, k:k + 1], float(D) ** -0.5, ALU.add, ALU.mult)
                    ins.then_inc(q_sum_done, 1)

                def split_q(c):
                    n = 2 * i + c
                    dve.wait_ge(q_hi_done, n + 1)
                    nc.vector.tensor_tensor(q_lo[c][:, :, :], q_sum[c][:, :, :], q_hi[c][:, :, :].bitcast(F32), ALU.subtract).then_inc(q_lo_done, 1)

                split_att(0)
                split_att(1)
                normalise(0)
                normalise(1)
                split_x1(0)
                bias_q(0)
                split_x1(1)
                split_q(0)
                bias_q(1)
                split_q(1)

        @block.tensor
        def _(pe):
            pe.sem_inc(r_done, 2)
            pe.sem_inc(q_done, 2)
            pe.wait_ge(w_split, 2)
            pe.wait_ge(const_in, 80)

            def transpose(i, c, src, dst):
                for t in range(TPC):
                    for k in range(CK):
                        ins = nc.tensor.transpose(dst[:, k, t * P:(t + 1) * P], src[:, t, k * P:(k + 1) * P], ident[:, :])
                return ins

            with pe.Fori(0, B) as i:
                def transpose_att(c):
                    pe.wait_ge(in_done[c], 80 * i + 80)
                    pe.wait_ge(t_lo, 2 * i + c + 1)
                    transpose(i, c, att[c], t_ps).then_inc(t_done, 1)

                def project(c):
                    n = 2 * i + c
                    pe.wait_ge(t_lo, n + 1 + 1)
                    pe.wait_ge(res_done, n + 2)
                    for t in range(TPC):
                        prods = [(a[:, k, t * P:(t + 1) * P], b[:, 0, k, :]) for k in range(CK)
                                 for a, b in parts3(a_hi[c], a_lo[c], w_hi, w_lo)]
                        for m, (a, b) in enumerate(prods):
                            ins = nc.tensor.matmul(r_ps[:, t, :], a, b, start=(m == 0), stop=(m == len(prods) - 1))
                    ins.then_inc(r_done, 1)

                def transpose_x1(c):
                    n = 2 * i + c
                    pe.wait_ge(x1_done, n + 1 + 2)
                    pe.wait_ge(x1_lo_done, n + 1)
                    transpose(i, c, x1[c], t1_ps).then_inc(t1_done, 1)

                def queries(c):
                    n = 2 * i + c
                    pe.wait_ge(x1_lo_done, n + 1 + 1)
                    pe.wait_ge(q_sum_done, n + 1)
                    for m in range(CK):
                        prods = [(b[:, 1, k, m * P:(m + 1) * P], a[:, k, :]) for k in range(CK)
                                 for a, b in parts3(x1_hi[c], x1_lo[c], w_hi, w_lo)]
                        for j, (a, b) in enumerate(prods):
                            ins = nc.tensor.matmul(q_ps[:, m, :], a, b, start=(j == 0), stop=(j == len(prods) - 1))
                    ins.then_inc(q_done, 1)

                transpose_att(0)
                transpose_att(1)
                project(0)
                project(1)
                transpose_x1(0)
                queries(0)
                transpose_x1(1)
                queries(1)


L = 77
HL = H // CK
GL = HG * L
NEG = -1000000000000000.0


CPB = 2
TPB = CPB * TPC


def cross_schedule(first, last=False):
    order = []
    for m in range(TPB):
        ago, tile = (1, m + TPB - 2) if m < 2 else (0, m - 2)
        if not (first and ago) and not (last and not ago):
            order += [("transpose", ago, tile, half) for half in range(2)]
        if m % TPC == 1 and not (first and m == 1) and not (last and m != 1):
            order += [("values", int(m == 1), int(m == 1), j) for j in range(2)]
        if m % TPC == 2 and not (first and m == 2) and not (last and m != 2):
            order.append(("project", int(m == 2), int(m == 2), 0))
    return order


class Use:

    def __init__(self, i, what, end=False):
        first, rest = cross_schedule(True), cross_schedule(False)
        order = cross_schedule(False, True) if end else first if isinstance(i, int) and i == 0 else rest
        n = order.index(what)
        start = 0 if order is first else len(first)
        self.bank = (start + n) % 2
        if n >= 2:
            self.before = order[n - 2]
        elif order is first:
            self.before = None
        else:
            kind, ago, which, half = (first if isinstance(i, int) and i == 1 else rest)[n - 2]
            self.before = (kind, ago + 1, which, half)


def stage_cross(nc, io):
    with Scope(nc, "cr") as s:
        ctx = s.sb("ctx", [P, CK, B * L], F32)
        ctx_hi = s.sb("ctx_hi", [P, CK, B * L], F32R)
        ctx_lo = s.sb("ctx_lo", [P, CK, B * L], F32R)
        kv_raw = s.sb("kv_raw", [P, 2, CK, C], F32)
        kv_hi = s.sb("kv_hi", [P, 2, CK, C], F32R)
        kv_lo = s.sb("kv_lo", [P, 2, CK, C], F32R)
        bk = s.sb("bk", [P, CK], F32)
        bv = s.sb("bv", [P, C], F32)
        head_of = s.sb("head_of", [P, HL], F32)
        k_sum = s.sb("k_sum", [P, CK, B * L], F32)
        k_hi = s.sb("k_hi", [P, CK, B * L], F32)
        k_lo = s.sb("k_lo", [P, CK, B * L], F32)
        k_blk = s.sb("k_blk", [P, 2, B, CK, HL * L], F32R)
        v_all = s.sb("v_all", [L, B, C + D], F32)
        v_now = s.sb("v_now", [L, C + D], F32)
        mask_i = s.sb("mask_i", [P, B * L], I32)
        mask_f = s.sb("mask_f", [P, B * L], F32)
        mask_w = s.sb("mask_w", [P, B, HG, L], F32R)
        mask_sel = s.sb("mask_sel", [P, P], F32R)
        wo_raw = s.sb("wo_raw", [P, HG, C], F32)
        wo_hi = s.sb("wo_hi", [P, HG, C], F32R)
        wo_lo = s.sb("wo_lo", [P, HG, C], F32R)
        bo = s.sb("bo", [P, C], F32)
        ident = s.sb("ident", [P, P], F32)
        q = [[s.sb(f"q{c}{part}", [P, CK, CH], F32R) for part in range(2)] for c in range(2)]
        x1 = [s.sb(f"x1{c}", [P, TPC, C], F32) for c in range(2)]
        e = [s.sb(f"e{i}", [P, H, L], F32) for i in range(4)]
        w_t = s.sb("w_t", [L, H, CH], F32)
        top = [s.sb(f"top{i}", [P, H], F32) for i in range(2)]
        tot = [s.sb(f"tot{i}", [P, H], F32) for i in range(2)]
        rec = [s.sb(f"rec{i}", [P, H], F32) for i in range(2)]
        o_hi = s.sb("o_hi", [P, HG, CH], F32R)
        o_lo = s.sb("o_lo", [P, HG, CH], F32R)
        res = s.sb("res", [P, TPC, C], F32)
        x2 = [s.sb(f"x2{c}", [P, TPC, C], F32) for c in range(2)]
        norm = Norm(nc, s, io["apart"])
        s_ps = [s.pb(f"s_ps{i}", (P, 2, 512)) for i in range(2)]
        t_ps = [s.pb(f"t_ps{i}", (P, 2, 512)) for i in range(2)]

        ctx_in, const_in = s.sem("ctx_in"), s.sem("const_in")
        hi_done, lo_done = s.sem("hi_done"), s.sem("lo_done")
        k_done, v_done = s.sem("k_done"), s.sem("v_done")
        prep = s.sem("prep")
        q_in = [s.sem(f"q_in{c}") for c in range(2)]
        x_in = [s.sem(f"x_in{c}") for c in range(2)]
        v_ready = s.sem("v_ready")
        x_biased = s.sem("x_biased")
        s_done = s.sem("s_done")
        top_done = s.sem("top_done")
        sub_done = s.sem("sub_done")
        exp_done = s.sem("exp_done")
        tot_done, rec_done = s.sem("tot_done"), s.sem("rec_done")
        w_done = s.sem("w_done")
        t_done = s.sem("t_done")
        wt_done = s.sem("wt_done")
        pv_done = s.sem("pv_done")
        o_hi_done, o_lo_done = s.sem("o_hi_done"), s.sem("o_lo_done")
        r_done = s.sem("r_done")
        res_done = s.sem("res_done")
        x2_done = s.sem("x2_done")
        out_done = [s.sem(f"out_done{c}") for c in range(2)]
        block = s.block()

        @block.sync
        def _(sp):
            sp.dma_start(ctx[:, :, :], io["ctxT"].rearrange("(c p) n -> p c n", p=P)).then_inc(ctx_in, 16)
            for j, name in enumerate(("wkT", "wvT")):
                sp.dma_start(kv_raw[:, j], io[name].rearrange("(c p) n -> p c n", p=P)).then_inc(ctx_in, 16)
            sp.dma_start(bk[:, :], io["bk2"]).then_inc(const_in, 16)
            sp.dma_start(bv[:, :], io["bv"].partition_broadcast(P)).then_inc(const_in, 16)
            sp.dma_start(head_of[:, :], io["head_of"]).then_inc(const_in, 16)
            sp.dma_start(ident[:, :], io["ident"]).then_inc(const_in, 16)
            sp.dma_start(bo[:, :], io["bo"].partition_broadcast(P)).then_inc(const_in, 16)
            for row in (0, 32):
                sp.dma_start(mask_i[row:row + 1, :], io["mask"]).then_inc(const_in, 16)
            sp.dma_start(wo_raw[:, :, :], io["woT"].rearrange("(g p) n -> p g n", p=P)).then_inc(const_in, 16)
            for c in range(2):
                sp.sem_inc(out_done[c], 16)

            def load_q(n, c):
                for part in range(2):
                    sp.dma_start(q[c][part][:, :, :].bitcast(F32), io["q2_scr"][n, part].rearrange("k p t -> p k t")).then_inc(q_in[c], 16)

            def load_x(n, c):
                sp.dma_start(x1[c][:, :, :], chunk_rows(io["x1_scr"], n)).then_inc(x_in[c], 16)

            def store(n, c):
                sp.wait_ge(x2_done, n + 1)
                sp.dma_start(chunk_rows(io["x2_scr"], n), x2[c][:, :, :]).then_inc(out_done[c], 16)

            def body(i, first, last):
                if not first:
                    store(2 * i - 2, 0)
                    sp.wait_ge(res_done, 2 * i)
                    load_x(2 * i + 1, 1)
                if not last:
                    sp.wait_ge(s_done, 2 * TPB * i + 2 * TPC)
                    load_q(2 * i + 2, 0)
                if not first:
                    store(2 * i - 1, 1)
                if not last:
                    sp.wait_ge(res_done, 2 * i + 1)
                    load_x(2 * i + 2, 0)
                    sp.wait_ge(s_done, 2 * TPB * (i + 1))
                    load_q(2 * i + 3, 1)

            load_q(0, 0)
            load_q(1, 1)
            load_x(0, 0)
            load_x(1, 1)
            body(0, True, False)
            with sp.Fori(1, B - 1) as i:
                body(i, False, False)
            body(B - 1, False, True)
            for c in range(2):
                store(2 * B - 2 + c, c)
            for c in range(2):
                sp.wait_ge(out_done[c], 16 * B + 16)

        @block.gpsimd
        def _(pool):
            pool.wait_ge(prep, 20)

            def bias_x(i, c):
                pool.wait_ge(x_in[c], 16 * i + 16)
                pool.tensor_tensor(x1[c][:, :, :], x1[c][:, :, :], bo[:, :].unsqueeze(1).to_broadcast([P, TPC, C]), ALU.add).then_inc(x_biased, 1)

            def body(i, first):
                for m in range(TPB):
                    if m == 2:
                        if not first:
                            pool.wait_ge(pv_done, 4 * i + 2)
                        pool.tensor_copy(v_now[:, :].unsqueeze(1), v_all[:, bass.ds(i, 1), :]).then_inc(v_ready, 1)
                    if m == 3:
                        bias_x(i, 0)
                    if m == 7:
                        bias_x(i, 1)
                    pool.wait_ge(rec_done, TPB * i + m + 1)
                    pool.tensor_tensor(e[m % 4][:, :, :], e[m % 4][:, :, :], rec[m % 2][:, :].unsqueeze(2).to_broadcast([P, H, L]), ALU.mult).then_inc(w_done, 1)

            body(0, True)
            with pool.Fori(1, B) as i:
                body(i, False)

        @block.scalar
        def _(act):
            act.wait_ge(ctx_in, 48)
            nc.scalar.activation(ctx_hi[:, :, :], ctx[:, :, :], ACT.Copy).then_inc(hi_done, 1)
            nc.scalar.activation(kv_hi[:, :, :, :], kv_raw[:, :, :, :], ACT.Copy).then_inc(hi_done, 1)
            act.wait_ge(const_in, 128)
            nc.scalar.activation(wo_hi[:, :, :], wo_raw[:, :, :], ACT.Copy).then_inc(hi_done, 1)

            def weights(i, m):
                act.wait_ge(sub_done, 2 * (TPB * i + m) + 2 + 2)
                nc.scalar.activation(e[m % 4][:, :, :], e[m % 4][:, :, :], ACT.Exp).then_inc(exp_done, 1)

            def copy_t(i, use, ago, m):
                for half in range(2):
                    act.wait_ge(t_done, 2 * (TPB * (i - ago) + m) + half + 1 + 8)
                    if m % TPC == 0 and half == 0:
                        act.wait_ge(pv_done, 4 * (i - ago) + 2 * (m // TPC) + 2)
                    nc.scalar.activation(
                        w_t[:, half * HL:(half + 1) * HL, (m % TPC) * P:(m % TPC + 1) * P].rearrange("p (g h) q -> p g h q", g=2),
                        t_ps[use(("transpose", ago, m, half)).bank][0:L, :, :].rearrange("p g (h q) -> p g h q", h=HG),
                        ACT.Copy).then_inc(wt_done, 1)

            def split_o(i, use, ago, c):
                n = 2 * (i - ago) + c
                act.wait_ge(r_done, n + 1)
                for j in range(2):
                    act.wait_ge(pv_done, 2 * n + j + 1 + 2)
                    nc.scalar.activation(o_hi[:, 2 * j:2 * j + 2, :], t_ps[use(("values", ago, c, j)).bank][:, :, :], ACT.Copy).then_inc(o_hi_done, 1)

            def body(i, first):
                def use(what):
                    return Use(i, what)
                for m in range(TPB):
                    if m >= 2:
                        copy_t(i, use, 0, m - 2)
                    elif not first:
                        copy_t(i, use, 1, m + TPB - 2)
                    weights(i, m)
                    if m == 5:
                        split_o(i, use, 0, 0)
                    if m == 1 and not first:
                        split_o(i, use, 1, 1)
                    if m == 3 and not first:
                        norm.take_root(act, 2 * i - 1)
                    if m == 7:
                        norm.take_root(act, 2 * i)

            body(0, True)
            with act.Fori(1, B) as i:
                body(i, False)

            def use(what):
                return Use(B, what, True)
            copy_t(B, use, 1, TPB - 2)
            copy_t(B, use, 1, TPB - 1)
            split_o(B, use, 1, 1)
            norm.take_root(act, 2 * B - 1)

        @block.vector
        def _(dve):
            nc.vector.memset(v_all[:, :, :], 0.0)
            nc.vector.memset(mask_w[:, :, :, :].bitcast(F32), 0.0)
            nc.vector.memset(mask_sel[:, :].bitcast(F32), 0.0).then_inc(prep, 1)
            dve.wait_ge(prep, 1)
            nc.vector.memset(mask_sel[0:1, :].bitcast(F32), 1.0)
            nc.vector.memset(mask_sel[32:33, :].bitcast(F32), 1.0)
            dve.wait_ge(hi_done, 1)
            nc.vector.tensor_tensor(ctx_lo[:, :, :], ctx[:, :, :], ctx_hi[:, :, :].bitcast(F32), ALU.subtract)
            dve.wait_ge(hi_done, 2)
            nc.vector.tensor_tensor(kv_lo[:, :, :, :], kv_raw[:, :, :, :], kv_hi[:, :, :, :].bitcast(F32), ALU.subtract).then_inc(lo_done, 1)
            dve.wait_ge(const_in, 128)
            for row in (0, 32):
                ins = nc.vector.tensor_copy(mask_f[row:row + 1, :], mask_i[row:row + 1, :])
            ins.then_inc(prep, 1)
            dve.wait_ge(prep, 2)
            for row in (0, 32):
                ins = nc.vector.tensor_scalar(mask_f[row:row + 1, :], mask_f[row:row + 1, :], NEG, None, ALU.mult)
            ins.then_inc(prep, 1)
            dve.wait_ge(prep, 3)

            def on_heads(row):
                return mask_f[row:row + 1, :].rearrange("p (b k) -> p b k", b=B).unsqueeze(2).to_broadcast([1, B, HG, L])
            for row in (0, 32):
                ins = nc.vector.tensor_copy(mask_w[row:row + 1, :, :, :], on_heads(row))
            ins.then_inc(prep, 1)
            dve.wait_ge(prep, 4)
            nc.vector.tensor_tensor(mask_w[32:33, :, :, :], on_heads(32), mask_w[32:33, :, :, :].bitcast(F32), ALU.subtract).then_inc(prep, 1)
            dve.wait_ge(k_done, 1)
            for k in range(CK):
                ins = nc.vector.tensor_scalar(k_sum[:, k, :], s_ps[0][:, k, 0:B * L], bk[:, k:k + 1], None, ALU.add)
            ins.then_inc(prep, 1)
            dve.wait_ge(prep, 6)
            nc.vector.tensor_copy(k_hi[:, :, :].bitcast(F32R), k_sum[:, :, :]).then_inc(prep, 1)
            dve.wait_ge(prep, 7)
            nc.vector.tensor_tensor(k_lo[:, :, :], k_sum[:, :, :], k_hi[:, :, :], ALU.subtract).then_inc(prep, 1)
            dve.wait_ge(prep, 8)
            heads = head_of[:, :].unsqueeze(2).to_broadcast([P, HL, L])
            for part, src in enumerate((k_hi, k_lo)):
                for b in range(B):
                    for k in range(CK):
                        ins = nc.vector.tensor_tensor(k_blk[:, part, b, k, :].rearrange("p (h n) -> p h n", h=HL),
                                                      src[:, k, b * L:(b + 1) * L].unsqueeze(1).to_broadcast([P, HL, L]), heads, ALU.mult)
            ins.then_inc(prep, 1)
            dve.wait_ge(v_done, 1)
            for b in range(B):
                ins = nc.vector.tensor_tensor(v_all[:, b, 0:C], t_ps[b // 2][0:L, b % 2, 0:C], bv[0:L, :], ALU.add)
            ins.then_inc(prep, 1)
            dve.wait_ge(hi_done, 3)
            nc.vector.tensor_tensor(wo_lo[:, :, :], wo_raw[:, :, :], wo_hi[:, :, :].bitcast(F32), ALU.subtract).then_inc(prep, 10)
            dve.sem_inc(sub_done, 2)

            def shift(i, m):
                tile = TPB * i + m
                views = [x[:, :, 0:GL].rearrange("p g (h n) -> p g h n", h=HG) for x in s_ps]
                for half in range(2):
                    dve.wait_ge(s_done, 2 * tile + half + 1)
                    ins = nc.vector.tensor_reduce(top[m % 2][:, half * HL:(half + 1) * HL].rearrange("p (g h) -> p g h", g=2), views[half], AX.X, ALU.max)
                ins.then_inc(top_done, 1)
                dve.wait_ge(top_done, tile + 1)
                dve.wait_ge(t_done, 2 * tile + 2)
                for half in range(2):
                    nc.vector.tensor_tensor(e[m % 4][:, half * HL:(half + 1) * HL, :].rearrange("p (g h) n -> p g h n", g=2), views[half],
                                            top[m % 2][:, half * HL:(half + 1) * HL].rearrange("p (g h) -> p g h", g=2).unsqueeze(3).to_broadcast([P, 2, HG, L]),
                                            ALU.subtract).then_inc(sub_done, 1)

            def totals(i, m):
                dve.wait_ge(exp_done, TPB * i + m + 1)
                nc.vector.tensor_reduce(tot[m % 2][:, :], e[m % 4][:, :, :], AX.X, ALU.add).then_inc(tot_done, 1)
                dve.wait_ge(tot_done, TPB * i + m + 1)
                if not (isinstance(i, int) and i == 0 and m < 2):
                    dve.wait_ge(w_done, TPB * i + m - 1)
                nc.vector.reciprocal(rec[m % 2][:, :], tot[m % 2][:, :]).then_inc(rec_done, 1)

            def split_o(i, use, ago, c):
                n = 2 * (i - ago) + c
                for j in range(2):
                    dve.wait_ge(o_hi_done, 2 * n + j + 1)
                    nc.vector.tensor_tensor(o_lo[:, 2 * j:2 * j + 2, :], t_ps[use(("values", ago, c, j)).bank][:, :, :],
                                            o_hi[:, 2 * j:2 * j + 2, :].bitcast(F32), ALU.subtract).then_inc(o_lo_done, 1)

            def residual(i, use, ago, c):
                n = 2 * (i - ago) + c
                dve.wait_ge(r_done, n + 1 + 1)
                dve.wait_ge(x_biased, n + 1)
                nc.vector.tensor_tensor(res[:, :, :], t_ps[use(("project", ago, c, 0)).bank][:, :, :].rearrange("p g (t e) -> p (g t) e", t=2),
                                        x1[c][:, :, :], ALU.add).then_inc(res_done, 1)

            def moments(n):
                dve.wait_ge(res_done, n + 1)
                norm.moments(dve, n, res)

            def scale(n, i, c):
                dve.wait_ge(out_done[c], 16 * i + 16)
                norm.scale(dve, n, res, x2[c]).then_inc(x2_done, 1)

            def body(i, first):
                def use(what):
                    return Use(i, what)
                for m in range(TPB):
                    if m == 3 and not first:
                        residual(i, use, 1, 1)
                    if m == 7:
                        residual(i, use, 0, 0)
                    if m == 6:
                        split_o(i, use, 0, 0)
                    if m == 2 and not first:
                        split_o(i, use, 1, 1)
                    shift(i, m)
                    if m == 3 and not first:
                        moments(2 * i - 1)
                    if m == 4 and not first:
                        scale(2 * i - 1, i - 1, 1)
                    if m == 7:
                        moments(2 * i)
                    if m == 0 and not first:
                        scale(2 * i - 2, i - 1, 0)
                    totals(i, m)

            body(0, True)
            with dve.Fori(1, B) as i:
                body(i, False)

            def use(what):
                return Use(B, what, True)
            split_o(B, use, 1, 1)
            scale(2 * B - 2, B - 1, 0)
            dve.wait_ge(x2_done, 2 * B - 1)
            residual(B, use, 1, 1)
            moments(2 * B - 1)
            scale(2 * B - 1, B - 1, 1)

        @block.tensor
        def _(pe):
            pe.sem_inc(t_done, 8)
            pe.sem_inc(pv_done, 2)
            pe.sem_inc(r_done, 1)
            pe.wait_ge(lo_done, 1)
            for m in range(CK):
                prods = [(b[:, 0, k, m * P:(m + 1) * P], a[:, k, :]) for k in range(CK)
                         for a, b in parts3(ctx_hi, ctx_lo, kv_hi, kv_lo)]
                for j, (a, b) in enumerate(prods):
                    ins = nc.tensor.matmul(s_ps[0][:, m, 0:B * L], a, b, start=(j == 0), stop=(j == len(prods) - 1))
            ins.then_inc(k_done, 1)
            for n in range(B):
                prods = [(a[:, k, n * L:(n + 1) * L], b[:, 1, k, :]) for k in range(CK)
                         for a, b in parts3(ctx_hi, ctx_lo, kv_hi, kv_lo)]
                for j, (a, b) in enumerate(prods):
                    ins = nc.tensor.matmul(t_ps[n // 2][0:L, n % 2, 0:C], a, b, start=(j == 0), stop=(j == len(prods) - 1))
            ins.then_inc(v_done, 1)
            pe.wait_ge(prep, 20)

            def scores(i, m):
                c, t = divmod(m, TPC)
                if t == 0:
                    pe.wait_ge(q_in[c], 32 * i + 32)
                tok = slice(t * P, (t + 1) * P)
                for k in range(CK):
                    pe.wait_ge(sub_done, 2 * (TPB * i + m) + k + 1)
                    for half in range(2):
                        cols = slice(half * GL, (half + 1) * GL)
                        for j, (a, b) in enumerate(((0, 0), (0, 1), (1, 0))):
                            nc.tensor.matmul(s_ps[k][:, half, 0:GL], q[c][a][:, k, tok], k_blk[:, b, bass.ds(i, 1), k, cols].rearrange("p o n -> p (o n)"),
                                             start=(j == 0), stop=False)
                        ins = nc.tensor.matmul(s_ps[k][:, half, 0:GL], mask_sel[:, :], mask_w[:, bass.ds(i, 1), :, :].rearrange("p o h n -> p (o h n)"),
                                               start=False, stop=True)
                    ins.then_inc(s_done, 1)

            def wait_free(i, u):
                if u.before is None:
                    return
                kind, ago, which, half = u.before
                j = i - ago
                if kind == "transpose":
                    pe.wait_ge(wt_done, 2 * (TPB * j + which) + half + 1)
                elif kind == "values":
                    pe.wait_ge(o_lo_done, 2 * (2 * j + which) + half + 1)
                else:
                    pe.wait_ge(res_done, 2 * j + which + 1)

            def transpose_w(i, use, ago, m):
                pe.wait_ge(w_done, TPB * (i - ago) + m + 1)
                for half in range(2):
                    u = use(("transpose", ago, m, half))
                    wait_free(i, u)
                    for h in range(HL):
                        ins = nc.tensor.transpose(t_ps[u.bank][0:L, h // HG, (h % HG) * P:(h % HG + 1) * P], e[m % 4][:, half * HL + h, :], ident[:, :])
                    ins.then_inc(t_done, 1)

            def values(i, use, ago, c):
                n = 2 * (i - ago) + c
                pe.wait_ge(wt_done, 8 * n + 8)
                pe.wait_ge(v_ready, i - ago + 1)
                for j in range(2):
                    u = use(("values", ago, c, j))
                    wait_free(i, u)
                    for g in range(2):
                        for h in range(HG):
                            head = (2 * j + g) * HG + h
                            ins = nc.tensor.matmul(t_ps[u.bank][32 * h:32 * h + 32, g, :], v_now[:, head * D:head * D + 32], w_t[:, head, :], start=True, stop=True)
                    ins.then_inc(pv_done, 1)

            def project(i, use, ago, c):
                n = 2 * (i - ago) + c
                u = use(("project", ago, c, 0))
                pe.wait_ge(o_lo_done, 2 * n + 2)
                wait_free(i, u)
                for t in range(TPC):
                    prods = [(a[:, g, t * P:(t + 1) * P], b[:, g, :]) for g in range(HG)
                             for a, b in parts3(o_hi, o_lo, wo_hi, wo_lo)]
                    for j, (a, b) in enumerate(prods):
                        ins = nc.tensor.matmul(t_ps[u.bank][:, t // 2, (t % 2) * C:(t % 2 + 1) * C], a, b, start=(j == 0), stop=(j == len(prods) - 1))
                ins.then_inc(r_done, 1)

            def body(i, first):
                def use(what):
                    return Use(i, what)
                for m in range(TPB):
                    scores(i, m)
                    if m >= 2:
                        transpose_w(i, use, 0, m - 2)
                    elif not first:
                        transpose_w(i, use, 1, m + TPB - 2)
                    if m == 1 and not first:
                        values(i, use, 1, 1)
                    if m == 2 and not first:
                        project(i, use, 1, 1)
                    if m == 5:
                        values(i, use, 0, 0)
                    if m == 6:
                        project(i, use, 0, 0)

            body(0, True)
            body(1, False)
            with pe.Fori(2, B) as i:
                body(i, False)

            def use(what):
                return Use(B, what, True)
            transpose_w(B, use, 1, TPB - 2)
            transpose_w(B, use, 1, TPB - 1)
            values(B, use, 1, 1)
            project(B, use, 1, 1)


E = 8
CAP = 1024
HID = 1024
HM = HID // P
SLOTS = E * CAP


def stage_router(nc, io, keep):
    with Scope(nc, "ro") as s:
        ident = s.sb("ident", [P, P], F32)
        w_raw = s.sb("w_raw", [P, CK, HID], F32)
        w_hi = s.sb("w_hi", [P, CK, HID], F32R)
        w_lo = s.sb("w_lo", [P, CK, HID], F32R)
        rb1 = s.sb("rb1", [P, HM], F32)
        rw2 = s.sb("rw2", [P, HM, 32], F32)
        rb2 = s.sb("rb2", [P, E], F32)
        x2 = [s.sb(f"x2{c}", [P, TPC, C], F32) for c in range(2)]
        x_hi = [s.sb(f"x_hi{c}", [P, CK, CH], F32R) for c in range(2)]
        x_lo = [s.sb(f"x_lo{c}", [P, CK, CH], F32R) for c in range(2)]
        hid = [s.sb(f"hid{c}", [P, HM, CH], F32) for c in range(2)]
        l_sb = s.sb("l_sb", [P, CH], F32)
        part = s.sb("part", [P, TPC, E], F32)
        logit = s.sb("logit", [P, TPC, E], F32)
        best = s.sb("best", [P, TPC, 8], F32)
        where = s.sb("where", [P, TPC, 8], U32)
        t_ps = s.pb("t_ps", (P, CK, CH))
        h_ps = [s.pb(f"h_ps{i}") for i in range(4)]
        l_ps = s.pb("l_ps")
        lt_ps = s.pb("lt_ps", (P, TPC, P))

        const_in = s.sem("const_in")
        w_split = s.sem("w_split")
        in_done = [s.sem(f"in_done{c}") for c in range(2)]
        t_done, x_hi_done, x_lo_done = s.sem("t_done"), s.sem("x_hi_done"), s.sem("x_lo_done")
        h_done, relu_done = s.sem("h_done"), s.sem("relu_done")
        l_done, l_copied = s.sem("l_done"), s.sem("l_copied")
        lt_done = s.sem("lt_done")
        sum_done, logit_done = s.sem("sum_done"), s.sem("logit_done")
        best_done, pick = s.sem("best_done"), s.sem("pick")
        block = s.block()

        @block.sync
        def _(sp):
            sp.dma_start(w_raw[:, :, :], io["rw1"].rearrange("(c p) n -> p c n", p=P)).then_inc(const_in, 16)
            sp.dma_start(ident[:, :], io["ident"]).then_inc(const_in, 16)
            sp.dma_start(rb1[:, :], io["rb1"]).then_inc(const_in, 16)
            sp.dma_start(rw2[:, :, :], io["rw2"]).then_inc(const_in, 16)
            sp.dma_start(rb2[:, :], io["rb2"].partition_broadcast(P)).then_inc(const_in, 16)
            with sp.Fori(0, B) as i:
                for c in range(2):
                    sp.wait_ge(t_done, 2 * i + c + 1)
                    sp.dma_start(x2[c][:, :, :], chunk_rows(io["x2_scr"], 2 * i + c)).then_inc(in_done[c], 16)

        @block.scalar
        def _(act):
            act.sem_inc(relu_done, 4)
            act.wait_ge(const_in, 80)
            nc.scalar.activation(w_hi[:, :, :], w_raw[:, :, :], ACT.Copy).then_inc(w_split, 1)
            with act.Fori(0, B) as i:
                def split_x(c):
                    act.wait_ge(t_done, 2 * i + c + 1 + 2)
                    act.wait_ge(h_done, 8 * (2 * i + c) + 8)
                    nc.scalar.activation(x_hi[c][:, :, :], t_ps[:, :, :], ACT.Copy).then_inc(x_hi_done, 1)

                def relus(c):
                    act.wait_ge(l_done, 2 * i + c + 1)
                    for m in range(HM):
                        act.wait_ge(h_done, 8 * (2 * i + c) + m + 1 + 16)
                        nc.scalar.activation(hid[c][:, m, :], h_ps[m % 4][:, :], ACT.Relu, bias=rb1[:, m:m + 1]).then_inc(relu_done, 1)

                def copy_l(c):
                    act.wait_ge(l_done, 2 * i + c + 1 + 2)
                    act.wait_ge(lt_done, 2 * i + c + 1)
                    nc.scalar.activation(l_sb[:, :], l_ps[:, :], ACT.Copy).then_inc(l_copied, 1)

                split_x(0)
                relus(0)
                split_x(1)
                copy_l(0)
                relus(1)
                copy_l(1)

        @block.vector
        def _(dve):
            dve.sem_inc(x_lo_done, 1)
            dve.sem_inc(sum_done, 1)
            dve.wait_ge(w_split, 1)
            nc.vector.tensor_tensor(w_lo[:, :, :], w_raw[:, :, :], w_hi[:, :, :].bitcast(F32), ALU.subtract).then_inc(w_split, 1)
            dve.wait_ge(const_in, 80)
            with dve.Fori(0, B) as i:
                def split_x(c):
                    dve.wait_ge(x_hi_done, 2 * i + c + 1)
                    nc.vector.tensor_tensor(x_lo[c][:, :, :], t_ps[:, :, :], x_hi[c][:, :, :].bitcast(F32), ALU.subtract).then_inc(x_lo_done, 1)

                def choose(c):
                    n = 2 * i + c
                    dve.wait_ge(lt_done, n + 1 + 1)
                    nc.vector.tensor_reduce(part[:, :, :], lt_ps[:, :, :].rearrange("p t (j e) -> p t e j", j=4)[:, :, 0:E, :], AX.X, ALU.add).then_inc(sum_done, 1)
                    dve.wait_ge(sum_done, n + 1 + 1)
                    nc.vector.tensor_tensor(logit[:, :, :], part[:, :, :], rb2[:, :].unsqueeze(1).to_broadcast([P, TPC, E]), ALU.add).then_inc(logit_done, 1)
                    wait_alone(dve, logit_done, n + 1, io["apart"])
                    for t in range(TPC):
                        ins = nc.vector.max(best[:, t, :], logit[:, t, :])
                    ins.then_inc(best_done, 1)
                    wait_alone(dve, best_done, n + 1, io["apart"])
                    for t in range(TPC):
                        ins = nc.vector.max_index(where[:, t, :], best[:, t, :], logit[:, t, :])
                    ins.then_inc(pick, 1)
                    dve.wait_ge(pick, 2 * n + 1)
                    nc.vector.tensor_copy(keep["value"][:, bass.ds(TPC * n, TPC), :], best[:, :, 0:2])
                    nc.vector.tensor_copy(keep["expert"][:, bass.ds(TPC * n, TPC), :], where[:, :, 0:2]).then_inc(pick, 1)

                split_x(0)
                split_x(1)
                choose(0)
                choose(1)

        @block.tensor
        def _(pe):
            pe.sem_inc(t_done, 2)
            pe.sem_inc(h_done, 16)
            pe.sem_inc(l_done, 2)
            pe.sem_inc(lt_done, 1)
            pe.wait_ge(w_split, 2)
            pe.wait_ge(const_in, 80)
            with pe.Fori(0, B) as i:
                def transpose_x(c):
                    pe.wait_ge(in_done[c], 16 * i + 16)
                    pe.wait_ge(x_lo_done, 2 * i + c + 1)
                    for t in range(TPC):
                        for k in range(CK):
                            ins = nc.tensor.transpose(t_ps[:, k, t * P:(t + 1) * P], x2[c][:, t, k * P:(k + 1) * P], ident[:, :])
                    ins.then_inc(t_done, 1)

                def hidden(c):
                    pe.wait_ge(x_lo_done, 2 * i + c + 1 + 1)
                    for m in range(HM):
                        pe.wait_ge(relu_done, 8 * (2 * i + c) + m + 1)
                        prods = [(b[:, k, m * P:(m + 1) * P], a[:, k, :]) for k in range(CK)
                                 for a, b in parts3(x_hi[c], x_lo[c], w_hi, w_lo)]
                        for j, (a, b) in enumerate(prods):
                            ins = nc.tensor.matmul(h_ps[m % 4][:, :], a, b, start=(j == 0), stop=(j == len(prods) - 1))
                        ins.then_inc(h_done, 1)

                def logits(c):
                    n = 2 * i + c
                    pe.wait_ge(relu_done, 8 * n + 8 + 4)
                    for m in range(HM):
                        j = m % 4
                        ins = nc.tensor.matmul(l_ps[32 * j:32 * j + 32, :], rw2[:, m, :], hid[c][:, m, :], start=(m < 4), stop=(m >= 4))
                    ins.then_inc(l_done, 1)

                def transpose_l(c):
                    n = 2 * i + c
                    pe.wait_ge(l_copied, n + 1)
                    pe.wait_ge(sum_done, n + 1)
                    for t in range(TPC):
                        ins = nc.tensor.transpose(lt_ps[:, t, :], l_sb[:, t * P:(t + 1) * P], ident[:, :])
                    ins.then_inc(lt_done, 1)

                transpose_x(0)
                hidden(0)
                transpose_x(1)
                logits(0)
                hidden(1)
                transpose_l(0)
                logits(1)
                transpose_l(1)


def stage_dispatch(nc, io, keep):
    with Scope(nc, "di") as s:
        before = s.sb("before", [P, P], F32)
        ones = s.sb("ones", [P, P], F32)
        iota = s.sb("iota", [P, E], F32)
        hot = s.sb("hot", [P, TT, 2, E], F32)
        both = s.sb("both", [P, TT, E], F32)
        total = s.sb("total", [P, TT, E], F32)
        run = s.sb("run", [P, TT, E], F32)
        place = s.sb("place", [P, TT, E], F32)
        mine = s.sb("mine", [P, TT, 2, E], F32)
        pos = s.sb("pos", [P, TT, 2], F32)
        kept = s.sb("kept", [P, TT, 2], F32)
        get = s.sb("get", [P, TT, 2], F32)
        put = s.sb("put", [P, TT, 2], F32)
        put_u = s.sb("put_u", [P, TT * 2], U32)
        put_now = [s.sb(f"put_now{c}", [P, TPC * 2], U32) for c in range(2)]
        x2 = [s.sb(f"x2{c}", [P, TPC, C], F32) for c in range(2)]
        diff = s.sb("diff", [P, TT], F32)
        share = s.sb("share", [P, TT, 2], F32)
        c_ps = s.pb("c_ps", (P, TT * E))
        n_ps = s.pb("n_ps", (P, TT * E))

        const_in = s.sem("const_in")
        step = s.sem("step")
        hot_done = s.sem("hot_done")
        count_done = s.sem("count_done")
        diff_done, exp_done = s.sem("diff_done"), s.sem("exp_done")
        put_done = s.sem("put_done")
        now_done = s.sem("now_done")
        in_done = [s.sem(f"in_done{c}") for c in range(2)]
        sent = [s.sem(f"sent{c}") for c in range(2)]
        block = s.block()

        @block.sync
        def _(sp):
            sp.dma_start(before[:, :], io["before"]).then_inc(const_in, 16)
            sp.dma_start(iota[:, :], io["iota"].partition_broadcast(P)).then_inc(const_in, 16)
            for c in range(2):
                sp.dma_start(x2[c][:, :, :], chunk_rows(io["x2_scr"], c)).then_inc(in_done[c], 16)
            with sp.Fori(0, B - 1) as i:
                for c in range(2):
                    sp.wait_ge(sent[c], 128 * i + 128)
                    sp.dma_start(x2[c][:, :, :], chunk_rows(io["x2_scr"], 2 * i + c + 2)).then_inc(in_done[c], 16)

        @block.gpsimd
        def _(pool):
            pool.wait_ge(put_done, 1)

            def scatter(i, c):
                pool.wait_ge(in_done[c], 16 * i + 16)
                pool.tensor_copy(put_now[c][:, :], put_u[:, bass.ds(2 * TPC * (2 * i + c), 2 * TPC)]).then_inc(now_done, 1)
                wait_alone(pool, now_done, 2 * i + c + 1, io["apart"])
                for t in range(TPC):
                    for k in range(2):
                        pool.indirect_dma_start(io["rows_scr"], bass.IndirectOffsetOnAxis(put_now[c][:, 2 * t + k:2 * t + k + 1], 0),
                                                x2[c][:, t, :], None, bounds_check=SLOTS - 1, oob_is_err=False).then_inc(sent[c], 16)

            with pool.Fori(0, B) as i:
                for c in range(2):
                    scatter(i, c)
            for c in range(2):
                pool.wait_ge(sent[c], 128 * B)

        @block.scalar
        def _(act):
            act.wait_ge(diff_done, 1)
            nc.scalar.activation(diff[:, :], diff[:, :], ACT.Exp).then_inc(exp_done, 1)

        @block.vector
        def _(dve):
            n = [0]

            def then(ins):
                n[0] += 1
                ins.then_inc(step, 1)
                dve.wait_ge(step, n[0])

            nc.vector.memset(ones[:, :], 1.0)
            nc.vector.tensor_tensor(diff[:, :], keep["value"][:, :, 1], keep["value"][:, :, 0], ALU.subtract).then_inc(diff_done, 1)
            dve.wait_ge(const_in, 32)
            experts = keep["expert"][:, :, :].unsqueeze(3).to_broadcast([P, TT, 2, E])
            for k in range(2):
                ins = nc.vector.tensor_tensor(hot[:, :, k, :], experts[:, :, k, :], iota[:, :].unsqueeze(1).to_broadcast([P, TT, E]), ALU.is_equal)
            then(ins)
            nc.vector.tensor_tensor(both[:, :, :], hot[:, :, 0, :], hot[:, :, 1, :], ALU.add).then_inc(hot_done, 1)
            dve.wait_ge(count_done, 1)
            then(nc.vector.tensor_copy(total[:, :, :], n_ps[:, :].rearrange("p (t e) -> p t e", e=E)))
            for e in range(E):
                ins = nc.vector.tensor_tensor_scan(run[:, :, e], ones[:, 0:TT], total[:, :, e], 0.0, ALU.mult, ALU.add)
            then(ins)
            then(nc.vector.tensor_tensor(run[:, :, :], run[:, :, :], total[:, :, :], ALU.subtract))
            then(nc.vector.tensor_tensor(place[:, :, :], c_ps[:, :].rearrange("p (t e) -> p t e", e=E), run[:, :, :], ALU.add))
            for k in range(2):
                ins = nc.vector.tensor_tensor(mine[:, :, k, :], hot[:, :, k, :], place[:, :, :], ALU.mult)
            then(ins)
            then(nc.vector.tensor_reduce(pos[:, :, :], mine[:, :, :, :], AX.X, ALU.add))
            nc.vector.tensor_scalar(kept[:, :, :], pos[:, :, :], float(CAP), None, ALU.is_lt)
            then(nc.vector.tensor_scalar(get[:, :, :], pos[:, :, :], float(CAP - 1), None, ALU.min))
            then(nc.vector.scalar_tensor_tensor(get[:, :, :], keep["expert"][:, :, :], float(CAP), get[:, :, :], ALU.mult, ALU.add))
            nc.vector.tensor_copy(keep["get"][:, :], get[:, :, :].rearrange("p t k -> p (t k)"))
            then(nc.vector.scalar_tensor_tensor(put[:, :, :], kept[:, :, :], -float(SLOTS), get[:, :, :], ALU.mult, ALU.add))
            then(nc.vector.tensor_scalar(put[:, :, :], put[:, :, :], float(SLOTS), None, ALU.add))
            nc.vector.tensor_copy(put_u[:, :], put[:, :, :].rearrange("p t k -> p (t k)")).then_inc(put_done, 1)
            dve.wait_ge(exp_done, 1)
            then(nc.vector.tensor_scalar(share[:, :, 0], diff[:, :], 1.0, None, ALU.add))
            then(nc.vector.reciprocal(share[:, :, 0], share[:, :, 0]))
            then(nc.vector.tensor_tensor(share[:, :, 1], share[:, :, 0], diff[:, :], ALU.mult))
            then(nc.vector.tensor_tensor(keep["share"][:, :].rearrange("p (t k) -> p t k", k=2), share[:, :, :], kept[:, :, :], ALU.mult))

        @block.tensor
        def _(pe):
            pe.wait_ge(const_in, 32)
            pe.wait_ge(hot_done, 1)
            chosen = both[:, :, :].rearrange("p t e -> p (t e)")
            nc.tensor.matmul(c_ps[:, :], before[:, :], chosen, start=True, stop=True)
            nc.tensor.matmul(n_ps[:, :], ones[:, :], chosen, start=True, stop=True).then_inc(count_done, 1)


def stage_experts(nc, io, keep):
    with Scope(nc, "ex") as s:
        ident = s.sb("ident", [P, P], F32)
        w1_raw = s.sb("w1_raw", [P, CK, HID], F32)
        w2_raw = s.sb("w2_raw", [P, HM, C], F32)
        w1_hi = [s.sb(f"w1_hi{i}", [P, CK, HID], F32R) for i in range(2)]
        w1_lo = [s.sb(f"w1_lo{i}", [P, CK, HID], F32R) for i in range(2)]
        w2_hi = [s.sb(f"w2_hi{i}", [P, HM, C], F32R) for i in range(2)]
        w2_lo = [s.sb(f"w2_lo{i}", [P, HM, C], F32R) for i in range(2)]
        b1 = s.sb("b1", [P, E, HM], F32)
        b2 = [s.sb(f"b2{i}", [P, C], F32) for i in range(2)]
        rows = [s.sb(f"rows{c}", [P, TPC, C], F32) for c in range(2)]
        x_hi = [s.sb(f"x_hi{c}", [P, CK, CH], F32R) for c in range(2)]
        x_lo = [s.sb(f"x_lo{c}", [P, CK, CH], F32R) for c in range(2)]
        hid = [s.sb(f"hid{i}", [P, CH], F32) for i in range(2)]
        h_hi = [s.sb(f"h_hi{c}", [P, HM, CH], F32R) for c in range(2)]
        h_lo = [s.sb(f"h_lo{c}", [P, HM, CH], F32R) for c in range(2)]
        y = [s.sb(f"y{c}", [P, TPC, C], F32) for c in range(2)]
        t_ps = s.pb("t_ps", (P, CK, CH))
        h_ps = [s.pb(f"h_ps{i}") for i in range(2)]
        y_ps = [s.pb(f"y_ps{i}") for i in range(4)]

        const_in = s.sem("const_in")
        w_in = s.sem("w_in")
        w_hi_done, w_lo_done = s.sem("w_hi_done"), s.sem("w_lo_done")
        in_done = [s.sem(f"in_done{c}") for c in range(2)]
        t_done, x_hi_done, x_lo_done = s.sem("t_done"), s.sem("x_hi_done"), s.sem("x_lo_done")
        h_done, relu_done = s.sem("h_done"), s.sem("relu_done")
        h_hi_done, h_lo_done = s.sem("h_hi_done"), s.sem("h_lo_done")
        y_done, biased = s.sem("y_done"), s.sem("biased")
        out_done = [s.sem(f"out_done{c}") for c in range(2)]
        block = s.block()

        @block.sync
        def _(sp):
            sp.dma_start(ident[:, :], io["ident"]).then_inc(const_in, 16)
            sp.dma_start(b1[:, :, :], io["eb1"]).then_inc(const_in, 16)
            for c in range(2):
                sp.sem_inc(out_done[c], 16)
            rows_v = io["rows_scr"].rearrange("(n t p) e -> n p t e", p=P, t=TPC)
            y_v = io["y_scr"].rearrange("(n t p) e -> n p t e", p=P, t=TPC)
            for c in range(2):
                sp.dma_start(rows[c][:, :, :], rows_v[c]).then_inc(in_done[c], 16)

            def load_weights(e, par):
                sp.dma_start(w1_raw[:, :, :], io["ew1"].rearrange("e (c p) n -> e p c n", p=P)[e]).then_inc(w_in, 16)
                sp.dma_start(w2_raw[:, :, :], io["ew2"].rearrange("e (m p) n -> e p m n", p=P)[e]).then_inc(w_in, 16)
                sp.dma_start(b2[par][:, :], io["eb2"][e].partition_broadcast(P)).then_inc(w_in, 16)

            load_weights(0, 0)

            def expert(e, par, last):
                if not last:
                    sp.wait_ge(w_lo_done, 2 * e + 2)
                    sp.wait_ge(biased, 8 * e + 4)
                    load_weights(e + 1, 1 - par)
                for c in range(2):
                    h = 2 * e + c
                    if not last:
                        sp.wait_ge(t_done, h + 1)
                        sp.dma_start(rows[c][:, :, :], rows_v[h + 2]).then_inc(in_done[c], 16)
                    if c == 1 or not (isinstance(e, int) and e == 0):
                        hh = h - 1
                        sp.wait_ge(biased, 4 * hh + 4 + 4)
                        sp.dma_start(y_v[hh], y[(c + 1) % 2][:, :, :]).then_inc(out_done[(c + 1) % 2], 16)

            expert(0, 0, False)
            with sp.Fori(0, 3) as i:
                expert(2 * i + 1, 1, False)
                expert(2 * i + 2, 0, False)
            expert(E - 1, 1, True)
            sp.wait_ge(biased, 8 * E + 4)
            sp.dma_start(y_v[2 * E - 1], y[1][:, :, :]).then_inc(out_done[1], 16)
            for c in range(2):
                sp.wait_ge(out_done[c], 16 * E + 16)

        @block.scalar
        def _(act):
            act.sem_inc(relu_done, 2)
            act.wait_ge(const_in, 32)

            def split_weights(e, par):
                act.wait_ge(w_in, 48 * e + 48)
                if not (isinstance(e, int) and e < 2):
                    act.wait_ge(y_done, 8 * (e - 1))
                nc.scalar.activation(w1_hi[par][:, :, :], w1_raw[:, :, :], ACT.Copy).then_inc(w_hi_done, 1)
                nc.scalar.activation(w2_hi[par][:, :, :], w2_raw[:, :, :], ACT.Copy).then_inc(w_hi_done, 1)

            def split_x(h, c):
                act.wait_ge(t_done, h + 1)
                act.wait_ge(h_done, 8 * h + 8)
                nc.scalar.activation(x_hi[c][:, :, :], t_ps[:, :, :], ACT.Copy).then_inc(x_hi_done, 1)

            def relus(h, c, e):
                for m in range(HM):
                    act.wait_ge(h_done, 8 * h + m + 1 + 16)
                    act.wait_ge(h_lo_done, 8 * h + m + 1)
                    nc.scalar.activation(hid[m % 2][:, :], h_ps[m % 2][:, :], ACT.Relu,
                                         bias=b1[:, bass.ds(e, 1), m:m + 1].rearrange("p a b -> p (a b)") if not isinstance(e, int) else b1[:, e, m:m + 1]).then_inc(relu_done, 1)

            def expert(e, par, last):
                h = 2 * e
                split_x(h + 1, 1)
                relus(h, 0, e)
                if not last:
                    split_weights(e + 1, 1 - par)
                    split_x(h + 2, 0)
                relus(h + 1, 1, e)

            split_weights(0, 0)
            split_x(0, 0)
            expert(0, 0, False)
            with act.Fori(0, 3) as i:
                expert(2 * i + 1, 1, False)
                expert(2 * i + 2, 0, False)
            expert(E - 1, 1, True)

        @block.vector
        def _(dve):
            dve.sem_inc(h_lo_done, 2)
            dve.sem_inc(biased, 4)

            def split_weights(e, par):
                for j, (raw, hi, lo) in enumerate(((w1_raw, w1_hi, w1_lo), (w2_raw, w2_hi, w2_lo))):
                    dve.wait_ge(w_hi_done, 2 * e + j + 1)
                    nc.vector.tensor_tensor(lo[par][:, :, :], raw[:, :, :], hi[par][:, :, :].bitcast(F32), ALU.subtract).then_inc(w_lo_done, 1)

            def split_x(h, c):
                dve.wait_ge(x_hi_done, h + 1)
                nc.vector.tensor_tensor(x_lo[c][:, :, :], t_ps[:, :, :], x_hi[c][:, :, :].bitcast(F32), ALU.subtract).then_inc(x_lo_done, 1)

            def split_hidden(h, c, m):
                if m == 0 and not (isinstance(h, int) and h < 2):
                    dve.wait_ge(y_done, 4 * (h - 1))
                dve.wait_ge(relu_done, 8 * h + m + 1 + 2)
                nc.vector.tensor_copy(h_hi[c][:, m, :], hid[m % 2][:, :]).then_inc(h_hi_done, 1)
                dve.wait_ge(h_hi_done, 8 * h + m + 1)
                nc.vector.tensor_tensor(h_lo[c][:, m, :], hid[m % 2][:, :], h_hi[c][:, m, :].bitcast(F32), ALU.subtract).then_inc(h_lo_done, 1)

            def bias_y(h, e, c, par, t):
                if t == 0:
                    dve.wait_ge(out_done[c], 16 * e + 16)
                dve.wait_ge(y_done, 4 * h + t + 1)
                nc.vector.tensor_tensor(y[c][:, t, :], y_ps[t][:, 0:C], b2[par][:, :], ALU.add).then_inc(biased, 1)

            def expert(e, par, last, first):
                h = 2 * e
                split_x(h + 1, 1)
                for m in range(HM):
                    split_hidden(h, 0, m)
                if not first:
                    for t in range(TPC):
                        bias_y(h - 1, e - 1, 1, 1 - par, t)
                if not last:
                    split_weights(e + 1, 1 - par)
                    split_x(h + 2, 0)
                for m in range(HM):
                    split_hidden(h + 1, 1, m)
                for t in range(TPC):
                    bias_y(h, e, 0, par, t)

            split_weights(0, 0)
            split_x(0, 0)
            expert(0, 0, False, True)
            with dve.Fori(0, 3) as i:
                expert(2 * i + 1, 1, False, False)
                expert(2 * i + 2, 0, False, False)
            expert(E - 1, 1, True, False)
            for t in range(TPC):
                bias_y(2 * E - 1, E - 1, 1, 1, t)

        @block.tensor
        def _(pe):
            pe.sem_inc(h_done, 16)
            pe.wait_ge(const_in, 32)

            def transpose_rows(h, e, c):
                pe.wait_ge(in_done[c], 16 * e + 16)
                if not (isinstance(h, int) and h == 0):
                    pe.wait_ge(x_lo_done, h)
                for t in range(TPC):
                    for k in range(CK):
                        ins = nc.tensor.transpose(t_ps[:, k, t * P:(t + 1) * P], rows[c][:, t, k * P:(k + 1) * P], ident[:, :])
                ins.then_inc(t_done, 1)

            def hidden(h, c, e, par):
                pe.wait_ge(x_lo_done, h + 1)
                pe.wait_ge(w_lo_done, 2 * e + 2)
                for m in range(HM):
                    pe.wait_ge(relu_done, 8 * h + m + 1)
                    prods = [(b[:, k, m * P:(m + 1) * P], a[:, k, :]) for k in range(CK)
                             for a, b in parts3(x_hi[c], x_lo[c], w1_hi[par], w1_lo[par])]
                    for j, (a, b) in enumerate(prods):
                        ins = nc.tensor.matmul(h_ps[m % 2][:, :], a, b, start=(j == 0), stop=(j == len(prods) - 1))
                    ins.then_inc(h_done, 1)

            def results(h, c, par):
                pe.wait_ge(h_lo_done, 8 * h + 8 + 2)
                for t in range(TPC):
                    pe.wait_ge(biased, 4 * h + t + 1)
                    prods = [(a[:, m, t * P:(t + 1) * P], b[:, m, :]) for m in range(HM)
                             for a, b in parts3(h_hi[c], h_lo[c], w2_hi[par], w2_lo[par])]
                    for j, (a, b) in enumerate(prods):
                        ins = nc.tensor.matmul(y_ps[t][:, 0:C], a, b, start=(j == 0), stop=(j == len(prods) - 1))
                    ins.then_inc(y_done, 1)

            def expert(e, par, last, first):
                h = 2 * e
                transpose_rows(h + 1, e, 1)
                hidden(h, 0, e, par)
                if not first:
                    results(h - 1, 1, 1 - par)
                if not last:
                    transpose_rows(h + 2, e + 1, 0)
                hidden(h + 1, 1, e, par)
                results(h, 0, par)

            transpose_rows(0, 0, 0)
            expert(0, 0, False, True)
            with pe.Fori(0, 3) as i:
                expert(2 * i + 1, 1, False, False)
                expert(2 * i + 2, 0, False, False)
            expert(E - 1, 1, True, False)
            results(2 * E - 1, 1, 1)


def stage_combine(nc, io, keep):
    with Scope(nc, "co") as s:
        x2 = [s.sb(f"x2{c}", [P, TPC, C], F32) for c in range(2)]
        got = [s.sb(f"got{c}", [P, TPC, 2, C], F32) for c in range(2)]
        get_now = [s.sb(f"get_now{c}", [P, TPC * 2], U32) for c in range(2)]
        share_now = [s.sb(f"share_now{c}", [P, TPC * 2], F32) for c in range(2)]
        out = [s.sb(f"out{c}", [P, TPC, C], F32) for c in range(2)]
        norm = Norm(nc, s, io["apart"])
        in_done = [s.sem(f"in_done{c}") for c in range(2)]
        now_done = s.sem("now_done")
        got_done = [s.sem(f"got_done{c}") for c in range(2)]
        step = s.sem("step")
        norm_done = s.sem("norm_done")
        out_done = [s.sem(f"out_done{c}") for c in range(2)]
        block = s.block()

        @block.sync
        def _(sp):
            for c in range(2):
                sp.sem_inc(out_done[c], 16)
            with sp.Fori(0, B) as i:
                for c in range(2):
                    sp.wait_ge(norm_done, 2 * i + c + 1)
                    sp.dma_start(x2[c][:, :, :], chunk_rows(io["x2_scr"], 2 * i + c)).then_inc(in_done[c], 16)
                for c in range(2):
                    sp.wait_ge(norm_done, 2 * i + c + 1 + 2)
                    sp.dma_start(chunk_rows(io["out"], 2 * i + c), out[c][:, :, :]).then_inc(out_done[c], 16)
            for c in range(2):
                sp.wait_ge(out_done[c], 16 * B + 16)

        @block.gpsimd
        def _(pool):
            def gather(n, c):
                pool.wait_ge(norm_done, n + 1)
                pool.tensor_copy(get_now[c][:, :], keep["get"][:, bass.ds(2 * TPC * n, 2 * TPC)])
                pool.tensor_copy(share_now[c][:, :], keep["share"][:, bass.ds(2 * TPC * n, 2 * TPC)]).then_inc(now_done, 1)
                wait_alone(pool, now_done, n + 1, io["apart"])
                for t in range(TPC):
                    for k in range(2):
                        pool.indirect_dma_start(got[c][:, t, k, :], None, io["y_scr"],
                                                bass.IndirectOffsetOnAxis(get_now[c][:, 2 * t + k:2 * t + k + 1], 0)).then_inc(got_done[c], 16)

            gather(0, 0)
            with pool.Fori(0, B - 1) as i:
                gather(2 * i + 1, 1)
                gather(2 * i + 2, 0)
            gather(2 * B - 1, 1)

        @block.scalar
        def _(act):
            with act.Fori(0, B) as i:
                for c in range(2):
                    norm.take_root(act, 2 * i + c)

        @block.vector
        def _(dve):
            dve.sem_inc(norm_done, 2)
            with dve.Fori(0, B) as i:
                for c in range(2):
                    n = 2 * i + c
                    dve.wait_ge(in_done[c], 16 * i + 16)
                    dve.wait_ge(now_done, n + 1)
                    dve.wait_ge(got_done[c], 128 * i + 128)
                    for k in range(2):
                        for t in range(TPC):
                            ins = nc.vector.scalar_tensor_tensor(x2[c][:, t, :], got[c][:, t, k, :], share_now[c][:, 2 * t + k:2 * t + k + 1],
                                                                 x2[c][:, t, :], ALU.mult, ALU.add)
                        ins.then_inc(step, 1)
                        dve.wait_ge(step, 2 * n + k + 1)
                    dve.wait_ge(out_done[c], 16 * i + 16)
                    norm.apply(dve, n, x2[c], out[c]).then_inc(norm_done, 1)


def consts():
    f = np.float32
    pos = np.arange(S, dtype=f)
    inv = (f(1.0) / f(10000.0) ** (np.arange(0, D, 2, dtype=f) / f(D))).astype(f)
    ang = (pos[:, None] * inv[None, :]).astype(f)
    sin, cos = np.sin(ang).astype(f), np.cos(ang).astype(f)
    cos, sin = np.tile(cos, (1, 2)), np.concatenate([-sin, sin], 1)
    scale = f(D) ** f(-0.5)
    rope = np.stack([np.stack([cos * scale, cos], 1), np.stack([sin * scale, sin], 1)], 1)
    rope = np.ascontiguousarray(rope.reshape(KT, P, 2, 2, D).transpose(1, 0, 2, 3, 4)).astype(f)
    k = np.arange(S)
    qb = np.arange(KT)[:, None]
    past = (k[None, :] // P) < qb
    tab = np.concatenate([np.where(past, k[None, :] - P * qb, 0), np.where(past, -1, 0)], 0).astype(f)
    one = ((k[None, :] // P) == qb).astype(f)
    q_rows = np.concatenate([one, one * (k[None, :] % P)], 0)
    a = np.arange(P)
    e = np.arange(HL)
    return {
        "head_of": (a[:, None] // D == e[None, :]).astype(f),
        "before": (a[:, None] < a[None, :]).astype(f),
        "iota": np.arange(E, dtype=f),
        "rope": rope,
        "ident": np.eye(P, dtype=f),
        "bias_tab": np.tile(tab, (P // 16, 1)).astype(f),
        "q_rows": np.concatenate([q_rows, q_rows], 0).astype(f),
        "min_t": np.minimum(a[None, :] - a[:, None], 0).astype(f),
        "min_mat": np.minimum(a[:, None] - a[None, :], 0).astype(f),
    }


def padded_wo(w):
    out = np.zeros((H, 2 * D, C), w.dtype)
    out[:, :D] = w.T.reshape(H, D, C)
    return out.reshape(H * 2 * D, C)


def padded_rw2(w):
    out = np.zeros((P, HM, 32), w.dtype)
    out[:, :, :E] = w.reshape(HM, P, E).transpose(1, 0, 2)
    return out


_DRAM_IN = {
    "x": ("x", lambda a: a.reshape(T, C)),
    "xT": ("x", lambda a: a.reshape(T, C).T),
    "ctxT": ("ctx_1024", lambda a: a.reshape(B * L, C).T),
    "mask": ("mask_Bx1x1xS2_ik0", lambda a: a.reshape(1, B * L)),
    "wqkvT": ("L0_attn_qkv_w", lambda a: a.T),
    "projT": ("L0_attn_proj_w", lambda a: a.T),
    "proj_b": ("L0_attn_proj_b", lambda a: a),
    "slopes": ("L0_attn_slopes", lambda a: a),
    "slope_rep": ("L0_attn_slopes", lambda a: np.repeat(a, 16).reshape(2, P).T),
    "wqT": ("L0_xattn_Wq", lambda a: a.T),
    "bq2": ("L0_xattn_bq", lambda a: a.reshape(CK, P).T),
    "wkT": ("L0_xattn_Wk", lambda a: a.T),
    "bk2": ("L0_xattn_bk", lambda a: a.reshape(CK, P).T),
    "wvT": ("L0_xattn_Wv", lambda a: a.T),
    "bv": ("L0_xattn_bv", lambda a: a),
    "woT": ("L0_xattn_Wo", padded_wo),
    "bo": ("L0_xattn_bo", lambda a: a),
    "rw1": ("L0_ffn_rw1", lambda a: a),
    "rb1": ("L0_ffn_rb1", lambda a: a.reshape(HM, P).T),
    "rw2": ("L0_ffn_rw2", padded_rw2),
    "rb2": ("L0_ffn_rb2", lambda a: a),
    "ew1": ("L0_ffn_ew1", lambda a: a),
    "eb1": ("L0_ffn_eb1", lambda a: a.reshape(E, HM, P).transpose(2, 0, 1)),
    "ew2": ("L0_ffn_ew2", lambda a: a),
    "eb2": ("L0_ffn_eb2", lambda a: a),
}


def build(nc, io, upto=9):
    nc.disable_value_cache = True

    def scratch(name, shape):
        io[name] = nc.dram_tensor(name, shape, F32, kind="Internal").ap()

    scratch("qk_scr", [NG, 2, 2, HG * D, S])
    scratch("bias_scr", [2, H * 16, S])
    scratch("top_scr", [2, 32, P])
    scratch("att_scr", [NG, P, KT, HG * D])
    scratch("x1_scr", [T, C])
    scratch("q2_scr", [T // CH, 2, CK, P, CH])
    scratch("x2_scr", [T, C])
    scratch("rows_scr", [SLOTS, C])
    scratch("y_scr", [SLOTS, C])
    with nc.semaphore("apart") as apart:
        io["apart"] = apart
        with Scope(nc, "keep") as k:
            keep = {"v": k.sb("v", [P, NG, KT, HG * VW], F32), "q_stack": k.sb("q_stack", [P, HG, S], F32R),
                    "k_stack": k.sb("k_stack", [P, HG, S], F32R), "q_rows": k.sb("q_rows", [P, S], F32),
                    "ident": k.sb("ident", [P, P], F32), "min_mat": k.sb("min_mat", [P, P], F32),
                    "min_bf": k.sb("min_bf", [P, P], BF16), "min_t_bf": k.sb("min_t_bf", [P, P], BF16),
                    "slope8": k.sb("slope8", [P, H], F32), "slope_parts": k.sb("slope_parts", [P, 3, H], F32), "slope_eye": k.sb("slope_eye", [P, 3, H, P], BF16),
                    "stack_in": k.sem("stack_in")}
            stage_qkv(nc, io, keep)
            if upto >= 2:
                stage_attention(nc, io, keep)
        if upto >= 3:
            stage_self_out(nc, io)
        if upto >= 4:
            stage_cross(nc, io)
        if upto >= 5:
            with nc.sbuf_tensor("keep_value", [P, TT, 2], F32) as value, nc.sbuf_tensor("keep_expert", [P, TT, 2], F32) as expert, \
                    nc.sbuf_tensor("keep_get", [P, TT * 2], U32) as get, nc.sbuf_tensor("keep_share", [P, TT * 2], F32) as share:
                keep = {"value": value, "expert": expert, "get": get, "share": share}
                if upto >= 5:
                    stage_router(nc, io, keep)
                if upto >= 6:
                    stage_dispatch(nc, io, keep)
                if upto >= 7:
                    stage_experts(nc, io, keep)
                if upto >= 8:
                    stage_combine(nc, io, keep)


def kernel(**inputs):
    import concourse.bacc as bacc
    from concourse.bass_utils import run_bass_kernel_spmd

    nc = bacc.Bacc("TRN2", target_bir_lowering=False, num_devices=1)
    arrays = {name: np.ascontiguousarray(layout(np.asarray(inputs[source]))) for name, (source, layout) in _DRAM_IN.items()}
    arrays.update(consts())
    io = {name: nc.dram_tensor(name, a.shape, mybir.dt.from_np(a.dtype), kind="ExternalInput").ap() for name, a in arrays.items()}
    io["out"] = nc.dram_tensor("out", (T, C), F32, kind="ExternalOutput").ap()
    build(nc, io)
    r = run_bass_kernel_spmd(nc, [arrays], core_ids=[0])
    return r.results[0]["out"].reshape(B, S, C)
```

```python
import numpy as np
import concourse.bass as bass
from concourse import mybir
from contextlib import ExitStack

F32 = mybir.dt.float32
F32R = mybir.dt.float32r
BF16 = mybir.dt.bfloat16
I32 = mybir.dt.int32
U32 = mybir.dt.uint32
ALU = mybir.AluOpType
ACT = mybir.ActivationFunctionType
AX = mybir.AxisListType

P = 128
B, S, C = 4, 1024, 256
T = B * S
TT = T // P
H, D = 16, 16
CK = C // P
CH = 512
TPC = CH // P
HG = 4
NG = B * H // HG
KT = S // P
VW = D + 1


class Scope:

    def __init__(self, nc, stage):
        self.nc, self.stage, self.ctx = nc, stage, ExitStack()

    def __enter__(self):
        self.ctx.__enter__()
        return self

    def __exit__(self, *a):
        return self.ctx.__exit__(*a)

    def sb(self, name, shape, dt):
        return self.ctx.enter_context(self.nc.sbuf_tensor(f"{self.stage}_{name}", shape, dt))

    def pb(self, name, shape=(P, 512), dt=F32):
        return self.ctx.enter_context(self.nc.psum_tensor(f"{self.stage}_{name}", list(shape), dt))

    def sem(self, name):
        return self.ctx.enter_context(self.nc.semaphore(f"{self.stage}_{name}"))

    def block(self):
        return self.ctx.enter_context(self.nc.Block())


def wait_alone(eng, sem, value, apart):
    eng.wait_ge(sem, value)
    eng.sem_inc(apart, 1)


def parts3(hi_a, lo_a, hi_b, lo_b):
    return ((hi_a, hi_b), (hi_a, lo_b), (lo_a, hi_b))


def load_stacks(sp, io, g, qs, ks, stack_in):
    for part, qk, tile, row in ((0, 0, qs, 0), (0, 0, qs, 16), (1, 0, qs, 32), (0, 1, ks, 0), (1, 1, ks, 16), (0, 1, ks, 32)):
        src = io["qk_scr"][bass.ds(g.n, 1), part, qk].rearrange("o (h d) t -> (o d) h t", d=D)
        sp.dma_start(tile[row:row + D, :, :].bitcast(F32), src).then_inc(stack_in, 16)
    for part in range(2):
        src = io["bias_scr"][part].rearrange("(h r) t -> r h t", r=16)[:, bass.ds((g.n % HG) * HG, HG), :]
        sp.dma_start(ks[ROW_BIAS + 16 * part:ROW_BIAS + 16 * part + 16, :, :].bitcast(F32), src).then_inc(stack_in, 16)


ROW_BIAS, ROW_MAX, ROWS = 64, 96, P


def stage_qkv(nc, io, keep):
    with Scope(nc, "qkv") as s:
        x_all = s.sb("x_all", [P, CK, T], F32)
        w = s.sb("w", [P, CK, 3 * C], F32)
        w_hi = s.sb("w_hi", [P, CK, 3 * C], F32R)
        w_lo = s.sb("w_lo", [P, CK, 3 * C], F32R)
        x_hi = [s.sb(f"x_hi{i}", [P, CK, CH], F32R) for i in range(2)]
        x_lo = [s.sb(f"x_lo{i}", [P, CK, CH], F32R) for i in range(2)]
        rope = s.sb("rope", [P, KT, 2, 2, D], F32)
        ident, min_mat, slope8, slope_eye = keep["ident"], keep["min_mat"], keep["slope8"], keep["slope_eye"]
        min_t = s.sb("min_t", [P, P], F32)
        slope_bf = s.sb("slope_bf", [P, 3, H], BF16)
        slope_left = s.sb("slope_left", [P, 3, H], F32)
        slope_parts = keep["slope_parts"]
        y_cos = [s.sb(f"y_cos{i}", [P, 2 * C], F32) for i in range(2)]
        y_sin = [s.sb(f"y_sin{i}", [P, 2 * C], F32) for i in range(2)]
        y = [s.sb(f"y{i}", [P, 2 * C], F32) for i in range(2)]
        t_hi = [s.sb(f"t_hi{i}", [P, 4, CH], F32R) for i in range(2)]
        t_lo = [s.sb(f"t_lo{i}", [P, 4, CH], F32R) for i in range(2)]
        btab = s.sb("btab", [P, S], F32)
        bval = s.sb("bval", [P, S], F32)
        b_hi, b_lo = [[t[1][:, 2 * i:2 * i + 2, :].rearrange("p a t -> p (a t)") for i in range(2)] for t in (t_hi, t_lo)]
        slope = s.sb("slope", [P, 2], F32)
        qk_ps = [s.pb(f"qk_ps{i}") for i in range(2)]
        v_ps = [s.pb(f"v_ps{i}") for i in range(2)]
        t_ps = [s.pb(f"t_ps{k}") for k in range(4)]

        w_in = s.sem("w_in")
        x_in = [s.sem(f"x_in{c}") for c in range(2)]
        const_in = s.sem("const_in")
        bias_in = s.sem("bias_in")
        w_split = s.sem("w_split")
        xhi_done = s.sem("xhi_done")
        xlo_done = s.sem("xlo_done")
        qkv_done = s.sem("qkv_done")
        rope_done = s.sem("rope_done")
        v_done = s.sem("v_done")
        y_done = s.sem("y_done")
        t_done = s.sem("t_done")
        thi_done = s.sem("thi_done")
        tlo_done = s.sem("tlo_done")
        out_done = [s.sem(f"out_done{i}") for i in range(2)]
        slope_step = s.sem("slope_step")
        bstep = s.sem("bstep")
        bout = s.sem("bout")
        vones = s.sem("vones")
        rows_done = s.sem("rows_done")
        block = s.block()

        @block.sync
        def _(sp):
            for c in range(2):
                sp.sem_inc(out_done[c], 256)
            sp.dma_start(w[:, :, :], io["wqkvT"].rearrange("(c p) n -> p c n", p=P)).then_inc(w_in, 16)
            sp.dma_start(btab[:, :], io["bias_tab"]).then_inc(bias_in, 16)
            sp.dma_start(slope[:, :], io["slope_rep"]).then_inc(bias_in, 16)
            sp.dma_start(keep["q_rows"][ROW_BIAS:ROW_MAX, :], io["q_rows"]).then_inc(bias_in, 16)
            sp.dma_start(slope8[:, :], io["slopes"].partition_broadcast(P)).then_inc(bias_in, 16)
            sp.dma_start(ident[:, :], io["ident"]).then_inc(bias_in, 16)
            sp.dma_start(min_mat[:, :], io["min_mat"]).then_inc(bias_in, 16)
            sp.dma_start(min_t[:, :], io["min_t"]).then_inc(bias_in, 16)
            xt = io["xT"].rearrange("(c p) t -> p c t", p=P)
            for half in range(2):
                for q in range(2):
                    n0 = half * (T // 2) + q * (T // 4)
                    sp.dma_start(x_all[:, :, n0:n0 + T // 4], xt[:, :, n0:n0 + T // 4]).then_inc(x_in[half], 16)
                if half == 0:
                    sp.dma_start(rope[:, :, :, :, :], io["rope"]).then_inc(const_in, 16)
            for half in range(2):
                sp.wait_ge(bstep, 3 * half + 3)
                for part, tile in ((0, b_hi[half]), (1, b_lo[half])):
                    sp.dma_start(io["bias_scr"][part, half * P:(half + 1) * P, :], tile.bitcast(F32)).then_inc(bout, 16)

            def store(i):
                for c in range(2):
                    sp.wait_ge(thi_done, 2 * i + c + 1)
                    sp.wait_ge(tlo_done, 2 * i + c + 2)
                    for k in range(4):
                        for part, tile in ((0, t_hi[c][:, k, :]), (1, t_lo[c][:, k, :])):
                            for r in range(2):
                                g = i * 4 + 2 * (k % 2) + r
                                sp.dma_start(io["qk_scr"][g, part, k // 2, :, c * CH:(c + 1) * CH],
                                             tile[64 * r:64 * r + 64].bitcast(F32)).then_inc(out_done[c], 16)

            with sp.Fori(0, B - 1) as i:
                store(i)
            for c in range(2):
                sp.wait_ge(out_done[c], 512)
            sp.wait_ge(bout, 64)
            sp.wait_ge(rows_done, 1)
            sp.wait_ge(vones, 3)
            load_stacks(sp, io, Group.of(0), keep["q_stack"], keep["k_stack"], keep["stack_in"])
            store(B - 1)
            for c in range(2):
                sp.wait_ge(out_done[c], 256 * B + 256)

        @block.gpsimd
        def _(pool):
            pool.sem_inc(y_done, 2)
            pool.memset(keep["v"][:, :, :, :], 1.0).then_inc(vones, 1)
            pool.memset(keep["q_stack"][:, :, :].bitcast(F32), 0.0)
            pool.memset(keep["k_stack"][:, :, :].bitcast(F32), 0.0).then_inc(vones, 1)
            pool.wait_ge(vones, 2)
            pool.memset(keep["k_stack"][ROW_MAX:ROW_MAX + 2, :, :].bitcast(F32), 1.0).then_inc(vones, 1)
            pool.wait_ge(vones, 3)
            with pool.Fori(0, B) as i:
                for m in range(8):
                    pool.wait_ge(rope_done, 8 * i + m + 1 + 2)
                    pool.wait_ge(t_done, 8 * i + m + 1)
                    pool.tensor_tensor(y[m % 2][:, :], y_cos[m % 2][:, :], y_sin[m % 2][:, :], ALU.add).then_inc(y_done, 1)

        @block.scalar
        def _(act):
            act.sem_inc(v_done, 2)
            act.wait_ge(w_in, 16)
            nc.scalar.activation(w_hi[:, :, :], w[:, :, :], ACT.Copy).then_inc(w_split, 1)
            act.wait_ge(vones, 2)
            act.wait_ge(bias_in, 112)
            for h in range(HG):
                ins = nc.scalar.activation(keep["q_stack"][ROW_BIAS:ROW_MAX, h, :], keep["q_rows"][ROW_BIAS:ROW_MAX, :], ACT.Copy)
            ins.then_inc(rows_done, 1)
            act.wait_ge(bout, 64)
            with act.Fori(0, B) as i:
                for c in range(2):
                    for half in range(2):
                        act.wait_ge(x_in[half], 32)
                    act.wait_ge(qkv_done, 8 * i + 4 * c + 4)
                    nc.scalar.activation(x_hi[c][:, :, :], x_all[:, :, bass.ds(i * (2 * CH) + c * CH, CH)],
                                         ACT.Copy).then_inc(xhi_done, 1)
                for m in range(8):
                    act.wait_ge(qkv_done, 8 * i + m + 1 + 8)
                    v_out = keep["v"][:, bass.ds(4 * i, 4), m, :].rearrange("p g (h e) -> p g h e", e=VW)
                    nc.scalar.activation(v_out[:, :, :, 0:D], v_ps[m % 2][:, 0:C].rearrange("p (g h d) -> p g h d", g=4, d=D),
                                         ACT.Copy).then_inc(v_done, 1)
                    if m in (4, 7):
                        c = 0 if m == 4 else 1
                        act.wait_ge(t_done, 8 * i + 4 * c + 4 + 2)
                        act.wait_ge(out_done[c], 256 * i + 256)
                        for k in range(4):
                            ins = nc.scalar.activation(t_hi[c][:, k, :], t_ps[k][:, :], ACT.Copy)
                        ins.then_inc(thi_done, 1)

        @block.vector
        def _(dve):
            dve.sem_inc(rope_done, 2)
            dve.sem_inc(tlo_done, 1)
            dve.wait_ge(bias_in, 112)
            for half in range(2):
                nc.vector.tensor_scalar(bval[:, :], btab[:, :], slope[:, half:half + 1], 8.0, ALU.mult, ALU.mult).then_inc(bstep, 1)
                dve.wait_ge(bstep, 3 * half + 1)
                nc.vector.tensor_copy(b_hi[half], bval[:, :]).then_inc(bstep, 1)
                dve.wait_ge(bstep, 3 * half + 2)
                nc.vector.tensor_tensor(b_lo[half], bval[:, :], b_hi[half].bitcast(F32), ALU.subtract).then_inc(bstep, 1)
                dve.wait_ge(bstep, 3 * half + 3)
            nc.vector.tensor_copy(keep["min_bf"][:, :], min_mat[:, :])
            nc.vector.tensor_copy(keep["min_t_bf"][:, :], min_t[:, :])
            nc.vector.tensor_scalar(slope8[:, :], slope8[:, :], 8.0, None, ALU.mult).then_inc(slope_step, 1)
            dve.wait_ge(slope_step, 1)
            for part in range(3):
                left = slope_left[:, part, :] if part else slope8[:, :]
                nc.vector.tensor_copy(slope_bf[:, part, :], left).then_inc(slope_step, 1)
                dve.wait_ge(slope_step, 2 * part + 2)
                if part < 2:
                    nc.vector.tensor_tensor(slope_left[:, part + 1, :], left, slope_bf[:, part, :], ALU.subtract).then_inc(slope_step, 1)
                    dve.wait_ge(slope_step, 2 * part + 3)
            nc.vector.tensor_copy(slope_parts[:, :, :], slope_bf[:, :, :]).then_inc(slope_step, 1)
            dve.wait_ge(slope_step, 7)
            for h in range(H):
                nc.vector.tensor_scalar(slope_eye[:, 0, h, :], ident[:, :], slope_parts[:, 0, h:h + 1], None, ALU.mult)
            dve.wait_ge(w_split, 1)
            nc.vector.tensor_tensor(w_lo[:, :, :], w[:, :, :], w_hi[:, :, :].bitcast(F32), ALU.subtract).then_inc(w_split, 1)
            dve.wait_ge(const_in, 16)
            with dve.Fori(0, B) as i:
                for c in range(2):
                    dve.wait_ge(xhi_done, 2 * i + c + 1)
                    nc.vector.tensor_tensor(x_lo[c][:, :, :], x_all[:, :, bass.ds(i * (2 * CH) + c * CH, CH)],
                                            x_hi[c][:, :, :].bitcast(F32), ALU.subtract).then_inc(xlo_done, 1)
                for m in range(8):
                    dve.wait_ge(qkv_done, 8 * i + m + 1 + 8)
                    dve.wait_ge(y_done, 8 * i + m + 1)
                    qk = qk_ps[m % 2][:, :].rearrange("p (k h d) -> p k h d", k=2, h=H)
                    swapped = qk_ps[m % 2][:, :].rearrange("p (k h s e) -> p k h s e", k=2, h=H, s=2)[:, :, :, ::-1, :]
                    cos = rope[:, m, 0, :, :].unsqueeze(2).to_broadcast([P, 2, H, D])
                    nc.vector.tensor_tensor(y_cos[m % 2][:, :].rearrange("p (k h d) -> p k h d", k=2, h=H), qk, cos, ALU.mult)
                    for k in range(2):
                        sin = rope[:, m, 1, k, :].rearrange("p (s e) -> p s e", s=2).unsqueeze(1).to_broadcast([P, H, 2, D // 2])
                        ins = nc.vector.tensor_tensor(
                            y_sin[m % 2][:, k * C:(k + 1) * C].rearrange("p (h s e) -> p h s e", h=H, s=2),
                            swapped[:, k], sin, ALU.mult)
                    ins.then_inc(rope_done, 1)
                    if m in (4, 7):
                        c = 0 if m == 4 else 1
                        dve.wait_ge(thi_done, 2 * i + c + 1)
                        for k in range(4):
                            ins = nc.vector.tensor_tensor(t_lo[c][:, k, :], t_ps[k][:, :], t_hi[c][:, k, :].bitcast(F32), ALU.subtract)
                        ins.then_inc(tlo_done, 1)

        @block.tensor
        def _(pe):
            pe.sem_inc(qkv_done, 8)
            pe.sem_inc(t_done, 2)
            pe.wait_ge(w_split, 2)
            pe.wait_ge(bias_in, 112)

            def transposes(i, m):
                pe.wait_ge(y_done, 8 * i + m + 1 + 2)
                if m % 4 == 0:
                    pe.wait_ge(tlo_done, 2 * i + m // 4 + 1)
                for k in range(4):
                    ins = nc.tensor.transpose(t_ps[k][:, (m % 4) * P:(m % 4 + 1) * P], y[m % 2][:, k * P:(k + 1) * P], ident[:, :])
                ins.then_inc(t_done, 1)

            with pe.Fori(0, B) as i:
                for m in range(8):
                    c = m // 4
                    if m % 4 == 0:
                        pe.wait_ge(xlo_done, 2 * i + c + 1)
                    pe.wait_ge(rope_done, 8 * i + m + 1)
                    pe.wait_ge(v_done, 8 * i + m + 1)
                    tok = slice((m % 4) * P, (m % 4 + 1) * P)
                    for out, cols in ((qk_ps[m % 2][:, :], slice(0, 2 * C)), (v_ps[m % 2][:, 0:C], slice(2 * C, 3 * C))):
                        prods = [(a[:, kc, tok], b[:, kc, cols]) for kc in range(CK)
                                 for a, b in parts3(x_hi[c], x_lo[c], w_hi, w_lo)]
                        for n, (a, b) in enumerate(prods):
                            ins = nc.tensor.matmul(out, a, b, start=(n == 0), stop=(n == len(prods) - 1))
                    ins.then_inc(qkv_done, 1)
                    if m:
                        transposes(i, m - 1)
                transposes(i, 7)


class Group:

    def __init__(self, n, buf, lap):
        self.n, self.buf, self.lap = n, buf, lap

    @staticmethod
    def of(n):
        return Group(n, n % 3, n // 3)

    def plus(self, k):
        if isinstance(self.n, int):
            return Group.of(self.n + k)
        b = self.buf + k
        return Group(self.n + k, b % 3, self.lap + b // 3)


def windows(eng, window):
    window(Group.of(0), True, False)
    with eng.Fori(0, 4) as i:
        for u in range(3):
            g = Group(3 * i + (u + 1), (u + 1) % 3, i + (u + 1) // 3)
            window(g, True, True)
    for n in range(13, NG):
        window(Group.of(n), n < NG - 1, True)


STEPS = 2 * KT
TILES = 4 * STEPS
RING = 3
TOP0_AT = 39


def ring_order(first, with_max):
    order = []
    for st in range(STEPS):
        order += [("max", 4 * st + h) for h in range(4) if with_max]
        if st == 1:
            order.append(("top", 1))
        if st == 2 and not first:
            order.append(("acc", 1))
        if st == 9 and with_max:
            order.append(("top", 0))
        if st == 10:
            order.append(("acc", 0))
    return order


PROLOGUE = [("max", u) for u in range(TOP0_AT + 1)] + [("top", 0)] + [("max", u) for u in range(TOP0_AT + 1, TILES)]
FIRST, MIDDLE, LAST = ring_order(True, True), ring_order(False, True), ring_order(False, False)


class Place:

    def __init__(self, g, what):
        n = None if g is None else g.n
        if n is None:
            at, order, bank0 = 0, PROLOGUE, 0
        elif isinstance(n, int) and n == 0:
            at, order, bank0 = len(PROLOGUE), FIRST, len(PROLOGUE)
        else:
            short = len(PROLOGUE) + len(FIRST) - len(MIDDLE)
            at, bank0 = short + len(MIDDLE) * n, short + len(MIDDLE) * g.buf
            order = LAST if isinstance(n, int) and n == NG - 1 else MIDDLE
            if what == ("acc", "end"):
                self.at, self.bank = at + len(LAST), (bank0 + len(LAST)) % RING
                return
        i = order.index(what)
        self.at, self.bank = at + i, (bank0 + i) % RING
def stage_attention(nc, io, keep):
    with Scope(nc, "att") as s:
        qs = [keep["q_stack"]] + [s.sb(f"q_stack{i}", [P, HG, S], F32R) for i in (1, 2)]
        ks = [keep["k_stack"]] + [s.sb(f"k_stack{i}", [P, HG, S], F32R) for i in (1, 2)]
        vg = [s.sb(f"v_group{i}", [P, KT, HG * VW + 32 - VW + 1], F32) for i in range(3)]
        w_exp = [[s.sb(f"w_exp{i}{h}", [P, CH], F32) for h in range(HG)] for i in range(2)]
        ident, min_mat, min_bf, min_t_bf = keep["ident"], keep["min_mat"], keep["min_bf"], keep["min_t_bf"]
        slope8, slope_eye = keep["slope8"], keep["slope_eye"]
        zeros = s.sb("zeros", [P, 8 * C], F32)
        row_max = [s.sb(f"row_max{i}", [P, HG * 4, 2], F32) for i in range(2)]
        top = s.sb("top", [P, HG * 4], F32)
        neg_top = s.sb("neg_top", [P, 2, HG * 4], F32R)
        neg_top_t = [s.sb(f"neg_top_t{i}", [32, P], F32R) for i in range(2)]
        acc_sb = [s.sb(f"acc_sb{i}", [P, CH], F32) for i in range(2)]
        recip = s.sb("recip", [P, 4, HG], F32)
        att = [s.sb(f"att{i}", [P, 4, HG, D], F32) for i in range(2)]
        s_ps = [s.pb(f"s_ps{h}") for h in range(HG)]
        ring = [s.pb(f"ring{i}") for i in range(3)]
        a_ps = s.pb("a_ps")

        stack_in = [keep["stack_in"]] + [s.sem(f"stack_in{i}") for i in (1, 2)]
        top_in = [s.sem(f"top_in{i}") for i in range(2)]
        top_out = [s.sem(f"top_out{i}") for i in range(2)]
        score_done = s.sem("score_done")
        diag_done = s.sem("diag_done")
        exp_done = s.sem("exp_done")
        pv_done = s.sem("pv_done")
        acc_done = s.sem("acc_done")
        recip_done = s.sem("recip_done")
        att_out = [s.sem(f"att_out{i}") for i in range(2)]
        ring_full = s.sem("ring_full")
        ring_free = s.sem("ring_free")
        top_step = s.sem("top_step")
        top_ready = s.sem("top_ready")
        top_copied = s.sem("top_copied")
        v_ready = s.sem("v_ready")
        pool_prep = s.sem("pool_prep")
        act_prep = s.sem("act_prep")
        zeroed = s.sem("zeroed")
        block = s.block()

        def move_top(sp, g, half, place):
            sp.wait_ge(ring_free, place.at + 1 + RING)
            sp.dma_start(io["top_scr"][half], neg_top_t[half][:, :].bitcast(F32)).then_inc(top_out[half], 16)
            sp.wait_ge(top_out[half], 16 * g.n + 32)
            sp.dma_start(qs[g.buf][ROW_MAX:ROW_MAX + 2, :, half * CH:(half + 1) * CH].bitcast(F32),
                         io["top_scr"][half].rearrange("(a h q) t -> a h (q t)", a=2, h=HG)).then_inc(top_in[half], 16)

        def store_att(sp, g, c, place):
            sp.wait_ge(ring_free, place.at + 1 + RING)
            sp.dma_start(io["att_scr"][bass.ds(g.n, 1), :, 4 * c:4 * c + 4, :].rearrange("o p q e -> (o p) q e"),
                         att[c][:, :, :, :].rearrange("p q h d -> p q (h d)")).then_inc(att_out[c], 16)

        @block.sync
        def _(sp):
            for half in range(2):
                sp.sem_inc(top_out[half], 16)
                sp.sem_inc(att_out[half], 16)
            sp.wait_ge(pool_prep, 2)
            sp.wait_ge(act_prep, 2)
            load_stacks(sp, io, Group.of(1), qs[1], ks[1], stack_in[1])
            move_top(sp, Group.of(0), 0, Place(None, ("top", 0)))

            def window(g, with_max, has_last):
                if has_last:
                    sp.wait_ge(score_done, TILES * g.n)
                if not isinstance(g.n, int) or g.n < NG - 2:
                    if isinstance(g.n, int) and g.n == 0:
                        sp.wait_ge(pool_prep, 4)
                        sp.wait_ge(act_prep, 3)
                    new = g.plus(2)
                    load_stacks(sp, io, new, qs[new.buf], ks[new.buf], stack_in[new.buf])
                move_top(sp, g, 1, Place(g, ("top", 1)))
                if has_last:
                    store_att(sp, g.plus(-1), 1, Place(g, ("acc", 1)))
                if with_max:
                    move_top(sp, g.plus(1), 0, Place(g, ("top", 0)))
                store_att(sp, g, 0, Place(g, ("acc", 0)))

            windows(sp, window)
            last = Group.of(NG - 1)
            store_att(sp, last, 1, Place(last, ("acc", "end")))
            for c in range(2):
                sp.wait_ge(att_out[c], 16 * NG + 16)

        @block.gpsimd
        def _(pool):
            for i in (1, 2):
                pool.memset(qs[i][:, :, :].bitcast(F32), 0.0)
                pool.memset(ks[i][:, :, :].bitcast(F32), 0.0).then_inc(pool_prep, 1)
                pool.wait_ge(pool_prep, 2 * i - 1)
                pool.memset(ks[i][ROW_MAX:ROW_MAX + 2, :, :].bitcast(F32), 1.0).then_inc(pool_prep, 1)
                pool.wait_ge(pool_prep, 2 * i)
                if i == 1:
                    for j in range(3):
                        pool.memset(vg[j][:, :, :], 0.0)
            pool.memset(zeros[:, :], 0.0).then_inc(pool_prep, 1)
            pool.wait_ge(pool_prep, 5)
            rows = io["rows_scr"].rearrange("(a p r) e -> a p (r e)", a=8, p=P)
            for a in range(8):
                pool.dma_start(rows[a], zeros[:, :]).then_inc(zeroed, 16)

            def take_v(g):
                dst = vg[g.buf][:, :, 0:HG * VW].unsqueeze(1)
                pool.tensor_copy(dst, keep["v"][:, bass.ds(g.n, 1), :, :]).then_inc(v_ready, 1)

            take_v(Group.of(0))

            def window(g, with_max, has_last):
                if with_max:
                    if has_last:
                        pool.wait_ge(pv_done, STEPS * (g.n - 1) + 2)
                    take_v(g.plus(1))

            windows(pool, window)
            pool.wait_ge(zeroed, 128)

        @block.scalar
        def _(act):
            act.sem_inc(exp_done, 4)
            act.sem_inc(acc_done, 1)
            for part in (1, 2):
                for h in range(H):
                    ins = nc.scalar.activation(slope_eye[:, part, h, :], ident[:, :], ACT.Copy, scale=keep["slope_parts"][:, part, h:h + 1])
            ins.then_inc(act_prep, 1)
            for i in (1, 2):
                act.wait_ge(pool_prep, 2 * i - 1)
                for h in range(HG):
                    ins = nc.scalar.activation(qs[i][ROW_BIAS:ROW_MAX, h, :], keep["q_rows"][ROW_BIAS:ROW_MAX, :], ACT.Copy)
                ins.then_inc(act_prep, 1)

            def copy_acc(g, c):
                act.wait_ge(pv_done, STEPS * g.n + KT * (c + 1) + 2)
                nc.scalar.activation(acc_sb[c][:, :], a_ps[:, :], ACT.Copy).then_inc(acc_done, 1)

            def window(g, with_max, has_last):
                for st in range(STEPS):
                    c, kt = divmod(st, KT)
                    for h in range(HG):
                        if kt // 4 == c and h % 2 == 0:
                            f = (2 * st if c == 0 else 8 + 2 * (st - 12)) + h // 2
                            act.wait_ge(diag_done, 16 * g.n + f + 1)
                        else:
                            act.wait_ge(score_done, 64 * g.n + 4 * st + h + 1)
                        if h == 0:
                            act.wait_ge(pv_done, STEPS * g.n + st + 1)
                        nc.scalar.activation(w_exp[st % 2][h][:, :], s_ps[h][:, :], ACT.Exp).then_inc(exp_done, 1)
                        if st == 1 and h == 1 and has_last:
                            copy_acc(g.plus(-1), 1)
                        if st == 9 and h == 1:
                            copy_acc(g, 0)

            windows(act, window)
            copy_acc(Group.of(NG - 1), 1)

        @block.vector
        def _(dve):
            dve.sem_inc(ring_free, RING)
            def maxima(g, u, place):
                dve.wait_ge(ring_full, place.at + 1)
                half, v = divmod(u, 32)
                nc.vector.tensor_reduce(row_max[half][:, v // 2, v % 2:v % 2 + 1], ring[place.bank][:, :], AX.X, ALU.max).then_inc(ring_free, 1)

            def top_parts(g, half, place):
                dve.wait_ge(ring_free, place.at + 1 + RING)
                nc.vector.tensor_reduce(top[:, :], row_max[half][:, :, :], AX.X, ALU.max).then_inc(top_step, 1)
                dve.wait_ge(top_step, 4 * g.n + 2 * half + 1)
                nc.vector.tensor_scalar(neg_top[:, 0, :], top[:, :], -1.0, None, ALU.mult).then_inc(top_step, 1)
                dve.wait_ge(top_step, 4 * g.n + 2 * half + 2)
                nc.vector.scalar_tensor_tensor(neg_top[:, 1, :], top[:, :], -1.0, neg_top[:, 0, :].bitcast(F32),
                                               ALU.mult, ALU.subtract).then_inc(top_ready, 1)

            def copy_top(g, half, place):
                dve.wait_ge(ring_full, place.at + 1)
                dve.wait_ge(top_out[half], 16 * g.n + 16)
                nc.vector.tensor_copy(neg_top_t[half][:, :], ring[place.bank][0:32, 0:P]).then_inc(ring_free, 1)

            def normalise(g, c, place):
                dve.wait_ge(ring_full, place.at + 1)
                sums = ring[place.bank][:, :].rearrange("p (q h e) -> p q h e", q=4, h=HG)
                nc.vector.reciprocal(recip[:, :, :], sums[:, :, :, D]).then_inc(recip_done, 1)
                dve.wait_ge(recip_done, 2 * g.n + c + 1)
                dve.wait_ge(att_out[c], 16 * g.n + 16)
                nc.vector.tensor_tensor(att[c][:, :, :, :], sums[:, :, :, 0:D],
                                        recip[:, :, :].unsqueeze(3).to_broadcast([P, 4, HG, D]), ALU.mult).then_inc(ring_free, 1)

            g0 = Group.of(0)
            for u in range(TILES):
                place = Place(None, ("max", u))
                maxima(g0, u, place)
                if u % 32 == 31:
                    top_parts(g0, u // 32, place)
                if u == TOP0_AT:
                    copy_top(g0, 0, Place(None, ("top", 0)))

            def window(g, with_max, has_last):
                for st in range(STEPS):
                    c, kt = divmod(st, KT)
                    for h in range(HG):
                        if kt // 4 == c and h % 2 == 0:
                            dve.wait_ge(score_done, TILES * g.n + 4 * st + h + 1)
                            d = s_ps[h][:, (kt % 4) * P:(kt % 4 + 1) * P]
                            slope = slope8[:, bass.ds((g.n % HG) * HG + h, 1)]
                            nc.vector.scalar_tensor_tensor(d, min_mat[:, :], slope, d, ALU.mult, ALU.add).then_inc(diag_done, 1)
                        if with_max:
                            maxima(g.plus(1), 4 * st + h, Place(g, ("max", 4 * st + h)))
                    if with_max and st % 8 == 7:
                        top_parts(g.plus(1), st // 8, Place(g, ("max", 4 * st + 3)))
                    if st == 1:
                        copy_top(g, 1, Place(g, ("top", 1)))
                    if st == 2 and has_last:
                        normalise(g.plus(-1), 1, Place(g, ("acc", 1)))
                    if st == 9 and with_max:
                        copy_top(g.plus(1), 0, Place(g, ("top", 0)))
                    if st == 10:
                        normalise(g, 0, Place(g, ("acc", 0)))

            windows(dve, window)
            last = Group.of(NG - 1)
            normalise(last, 1, Place(last, ("acc", "end")))

        @block.tensor
        def _(pe):
            pe.sem_inc(pv_done, 2)

            def max_scores(g, u, place):
                half, v = divmod(u, 32)
                h, v = divmod(v, 8)
                qt, kk = half * 4 + v // 2, v % 2
                pe.wait_ge(ring_free, place.at + 1)
                diag = qt // 4 == kk
                out = ring[place.bank]
                ins = nc.tensor.matmul(out[:, :], qs[g.buf][0:ROW_MAX, h, qt * P:(qt + 1) * P],
                                       ks[g.buf][0:ROW_MAX, h, kk * CH:(kk + 1) * CH], start=True, stop=not diag)
                if diag:
                    ins = nc.tensor.matmul(out[:, (qt % 4) * P:(qt % 4 + 1) * P], min_bf[:, :],
                                           slope_eye[:, 0, bass.ds((g.n % HG) * HG + h, 1), :].rearrange("p o q -> p (o q)"),
                                           start=False, stop=True)
                ins.then_inc(ring_full, 1)

            def transpose_top(g, half, place):
                pe.wait_ge(top_ready, 2 * g.n + half + 1)
                pe.wait_ge(ring_free, place.at + 1)
                nc.tensor.transpose(ring[place.bank][0:32, 0:P], neg_top[:, :, :].rearrange("p a b -> p (a b)").bitcast(F32),
                                    ident[:, :]).then_inc(ring_full, 1)

            def values(g, st):
                c, kt = divmod(st, KT)
                pe.wait_ge(exp_done, 64 * g.n + 4 * st + 4 + 4)
                if st == 0:
                    pe.wait_ge(v_ready, g.n + 1)
                if kt == 0:
                    pe.wait_ge(acc_done, 2 * g.n + c + 1)
                for h in range(HG):
                    ins = nc.tensor.matmul(a_ps[32 * h:32 * h + 32, :], vg[g.buf][:, kt, h * VW:h * VW + 32],
                                           w_exp[st % 2][h][:, :], start=(kt == 0), stop=(kt == KT - 1))
                ins.then_inc(pv_done, 1)

            def transpose_acc(g, c, place):
                pe.wait_ge(acc_done, 2 * g.n + c + 1 + 1)
                pe.wait_ge(ring_free, place.at + 1)
                for q in range(4):
                    ins = nc.tensor.transpose(ring[place.bank][:, q * P:(q + 1) * P], acc_sb[c][:, q * P:(q + 1) * P], ident[:, :])
                ins.then_inc(ring_full, 1)

            g0 = Group.of(0)
            pe.wait_ge(stack_in[0], 128)
            for u in range(TILES):
                max_scores(g0, u, Place(None, ("max", u)))
                if u == TOP0_AT:
                    transpose_top(g0, 0, Place(None, ("top", 0)))

            def window(g, with_max, has_last):
                if with_max:
                    n = g.plus(1)
                    pe.wait_ge(stack_in[n.buf], 128 * n.lap + 128)
                for st in range(STEPS):
                    c, kt = divmod(st, KT)
                    if kt == 0:
                        pe.wait_ge(top_in[c], 16 * g.n + 16)
                    for h in range(HG):
                        pe.wait_ge(exp_done, TILES * g.n + 4 * st + h + 1)
                        diag = kt // 4 == c and h % 2 == 1
                        ins = nc.tensor.matmul(s_ps[h][:, :], ks[g.buf][:, h, kt * P:(kt + 1) * P],
                                               qs[g.buf][:, h, c * CH:(c + 1) * CH], start=True, stop=not diag)
                        for part in range(3 if diag else 0):
                            eye = slope_eye[:, part, bass.ds((g.n % HG) * HG + h, 1), :].rearrange("p o q -> p (o q)")
                            ins = nc.tensor.matmul(s_ps[h][:, (kt % 4) * P:(kt % 4 + 1) * P], min_t_bf[:, :], eye, start=False, stop=part == 2)
                        ins.then_inc(score_done, 1)
                        if with_max:
                            max_scores(n, 4 * st + h, Place(g, ("max", 4 * st + h)))
                    if st:
                        values(g, st - 1)
                    elif has_last:
                        values(g.plus(-1), STEPS - 1)
                    if st == 1:
                        transpose_top(g, 1, Place(g, ("top", 1)))
                    if st == 2 and has_last:
                        transpose_acc(g.plus(-1), 1, Place(g, ("acc", 1)))
                    if st == 9 and with_max:
                        transpose_top(n, 0, Place(g, ("top", 0)))
                    if st == 10:
                        transpose_acc(g, 0, Place(g, ("acc", 0)))

            pe.wait_ge(act_prep, 1)
            windows(pe, window)
            last = Group.of(NG - 1)
            values(last, STEPS - 1)
            transpose_acc(last, 1, Place(last, ("acc", "end")))


EPS = 1e-5


class Norm:

    def __init__(self, nc, s, apart):
        self.nc, self.apart = nc, apart
        self.stats = s.sb("stats", [P, TPC, 6], F32)
        self.mv = s.sb("mv", [P, TPC, 2], F32)
        self.var = s.sb("var", [P, TPC, 1], F32)
        self.root = s.sb("root", [P, TPC, 1], F32)
        self.inv = s.sb("inv", [P, TPC, 1], F32)
        self.half = s.sb("half", [P, TPC, 1], F32)
        self.step = s.sem("norm_step")
        self.root_done = s.sem("root_done")

    def apply(self, dve, n, x, out):
        self.moments(dve, n, x)
        return self.scale(dve, n, x, out)

    def moments(self, dve, n, x):
        nc, at = self.nc, 7 * n
        for t in range(TPC):
            ins = nc.vector.bn_stats(self.stats[:, t, :], x[:, t, :])
        ins.then_inc(self.step, 1)
        wait_alone(dve, self.step, at + 1, self.apart)
        for t in range(TPC):
            ins = nc.vector.bn_aggr(self.mv[:, t, :], self.stats[:, t, :])
        ins.then_inc(self.step, 1)
        dve.wait_ge(self.step, at + 2)
        nc.vector.tensor_scalar(self.var[:, :, :], self.mv[:, :, 1:2], EPS, None, ALU.add).then_inc(self.step, 1)

    def scale(self, dve, n, x, out):
        nc, at = self.nc, 7 * n
        dve.wait_ge(self.root_done, n + 1)
        nc.vector.reciprocal(self.inv[:, :, :], self.root[:, :, :]).then_inc(self.step, 1)
        dve.wait_ge(self.step, at + 4)
        nc.vector.scalar_tensor_tensor(self.half[:, :, :], self.inv[:, :, :], -0.5, self.var[:, :, :], ALU.mult, ALU.mult).then_inc(self.step, 1)
        dve.wait_ge(self.step, at + 5)
        nc.vector.tensor_tensor(self.half[:, :, :], self.half[:, :, :], self.inv[:, :, :], ALU.mult).then_inc(self.step, 1)
        dve.wait_ge(self.step, at + 6)
        nc.vector.scalar_tensor_tensor(self.inv[:, :, :], self.half[:, :, :], 1.5, self.inv[:, :, :], ALU.add, ALU.mult).then_inc(self.step, 1)
        dve.wait_ge(self.step, at + 7)
        for t in range(TPC):
            ins = nc.vector.tensor_scalar(out[:, t, :], x[:, t, :], self.mv[:, t, 0:1], self.inv[:, t, :], ALU.subtract, ALU.mult)
        return ins

    def take_root(self, act, n):
        act.wait_ge(self.step, 7 * n + 3)
        self.nc.scalar.activation(self.root[:, :, :], self.var[:, :, :], ACT.Sqrt).then_inc(self.root_done, 1)


def chunk_rows(ap, n):
    return ap.rearrange("(n t p) e -> n p t e", p=P, t=TPC)[n]


def stage_self_out(nc, io):
    with Scope(nc, "so") as s:
        w_raw = s.sb("w_raw", [P, 2, CK, C], F32)
        w_hi = s.sb("w_hi", [P, 2, CK, C], F32R)
        w_lo = s.sb("w_lo", [P, 2, CK, C], F32R)
        proj_b = s.sb("proj_b", [P, C], F32)
        bq = s.sb("bq", [P, CK], F32)
        ident = s.sb("ident", [P, P], F32)
        att = [s.sb(f"att{i}", [P, TPC, C], F32) for i in range(2)]
        x = [s.sb(f"x{i}", [P, TPC, C], F32) for i in range(2)]
        a_hi = [s.sb(f"a_hi{i}", [P, CK, CH], F32R) for i in range(2)]
        a_lo = [s.sb(f"a_lo{i}", [P, CK, CH], F32R) for i in range(2)]
        res = [s.sb(f"res{i}", [P, TPC, C], F32) for i in range(2)]
        x1 = [s.sb(f"x1{i}", [P, TPC, C], F32) for i in range(2)]
        x1_hi = [s.sb(f"x1_hi{i}", [P, CK, CH], F32R) for i in range(2)]
        x1_lo = [s.sb(f"x1_lo{i}", [P, CK, CH], F32R) for i in range(2)]
        q_sum = [s.sb(f"q_sum{i}", [P, CK, CH], F32) for i in range(2)]
        q_hi = [s.sb(f"q_hi{i}", [P, CK, CH], F32R) for i in range(2)]
        q_lo = [s.sb(f"q_lo{i}", [P, CK, CH], F32R) for i in range(2)]
        norm = Norm(nc, s, io["apart"])
        t_ps = s.pb("t_ps", (P, CK, CH))
        r_ps = s.pb("r_ps", (P, TPC, C))
        t1_ps = s.pb("t1_ps", (P, CK, CH))
        q_ps = s.pb("q_ps", (P, CK, CH))

        const_in = s.sem("const_in")
        w_split = s.sem("w_split")
        in_done = [s.sem(f"in_done{i}") for i in range(2)]
        t_done, t_hi, t_lo = s.sem("t_done"), s.sem("t_hi"), s.sem("t_lo")
        r_done, x_biased = s.sem("r_done"), s.sem("x_biased")
        res_done, x1_done = s.sem("res_done"), s.sem("x1_done")
        t1_done, x1_hi_done, x1_lo_done = s.sem("t1_done"), s.sem("x1_hi_done"), s.sem("x1_lo_done")
        q_done, q_sum_done = s.sem("q_done"), s.sem("q_sum_done")
        q_hi_done, q_lo_done = s.sem("q_hi_done"), s.sem("q_lo_done")
        out_done = [s.sem(f"out_done{i}") for i in range(2)]
        q_out = [s.sem(f"q_out{i}") for i in range(2)]
        block = s.block()

        @block.sync
        def _(sp):
            for j, name in enumerate(("projT", "wqT")):
                sp.dma_start(w_raw[:, j], io[name].rearrange("(c p) n -> p c n", p=P)).then_inc(const_in, 16)
            sp.dma_start(ident[:, :], io["ident"]).then_inc(const_in, 16)
            sp.dma_start(proj_b[:, :], io["proj_b"].partition_broadcast(P)).then_inc(const_in, 16)
            sp.dma_start(bq[:, :], io["bq2"]).then_inc(const_in, 16)
            for c in range(2):
                sp.sem_inc(out_done[c], 16)
                sp.sem_inc(q_out[c], 32)
            def load(i, c):
                n = 2 * i + c
                sp.wait_ge(r_done, n + 1)
                sp.wait_ge(res_done, n + 1)
                for hq in range(4):
                    src = io["att_scr"][bass.ds(4 * i + hq, 1), :, 4 * c:4 * c + 4, :].rearrange("o p q e -> (o p) q e")
                    sp.dma_start(att[c][:, :, hq * 64:hq * 64 + 64], src).then_inc(in_done[c], 16)
                sp.dma_start(x[c][:, :, :], io["x"].rearrange("(n t p) e -> n p t e", p=P, t=TPC)[n]).then_inc(in_done[c], 16)

            def store(i, c):
                n = 2 * i + c
                sp.wait_ge(x1_done, n + 1 + 2)
                sp.dma_start(io["x1_scr"].rearrange("(n t p) e -> n p t e", p=P, t=TPC)[n], x1[c][:, :, :]).then_inc(out_done[c], 16)

            def store_q(i, c):
                n = 2 * i + c
                sp.wait_ge(q_lo_done, n + 1 + 2)
                for part, tile in ((0, q_hi[c]), (1, q_lo[c])):
                    sp.dma_start(io["q2_scr"][n, part].rearrange("k p t -> p k t"), tile[:, :, :].bitcast(F32)).then_inc(q_out[c], 16)

            load(0, 0)
            load(0, 1)
            for c in range(2):
                load(1, c)
                store(0, c)
            with sp.Fori(1, B - 1) as i:
                for c in range(2):
                    load(i + 1, c)
                    store_q(i - 1, c)
                    store(i, c)
            for c in range(2):
                store_q(B - 2, c)
                store(B - 1, c)
            for c in range(2):
                store_q(B - 1, c)
            for c in range(2):
                sp.wait_ge(out_done[c], 16 * B + 16)
                sp.wait_ge(q_out[c], 32 * B + 32)

        @block.gpsimd
        def _(pool):
            pool.wait_ge(const_in, 80)
            with pool.Fori(0, B) as i:
                for c in range(2):
                    n = 2 * i + c
                    pool.wait_ge(in_done[c], 80 * i + 80)
                    pool.tensor_tensor(x[c][:, :, :], x[c][:, :, :], proj_b[:, :].unsqueeze(1).to_broadcast([P, TPC, C]), ALU.add).then_inc(x_biased, 1)

        @block.scalar
        def _(act):
            act.sem_inc(t_hi, 1)
            act.sem_inc(x1_hi_done, 1)
            act.wait_ge(const_in, 80)
            nc.scalar.activation(w_hi[:, :, :, :], w_raw[:, :, :, :], ACT.Copy).then_inc(w_split, 1)

            def split_att(i, c):
                n = 2 * i + c
                act.wait_ge(t_done, n + 1)
                act.wait_ge(r_done, n + 1)
                nc.scalar.activation(a_hi[c][:, :, :], t_ps[:, :, :], ACT.Copy).then_inc(t_hi, 1)

            def split_x1(i, c):
                n = 2 * i + c
                act.wait_ge(t1_done, n + 1)
                act.wait_ge(q_done, n + 1)
                nc.scalar.activation(x1_hi[c][:, :, :], t1_ps[:, :, :], ACT.Copy).then_inc(x1_hi_done, 1)

            def split_q(i, c):
                n = 2 * i + c
                act.wait_ge(q_sum_done, n + 1 + 1)
                act.wait_ge(q_out[c], 32 * i + 32)
                nc.scalar.activation(q_hi[c][:, :, :], q_sum[c][:, :, :], ACT.Copy).then_inc(q_hi_done, 1)

            def body(i, new, old):
                for c in range(2):
                    if new:
                        split_att(i, c)
                    if old:
                        split_x1(i - 1, c)
                    if new:
                        norm.take_root(act, 2 * i + c)
                    if old:
                        split_q(i - 1, c)

            body(0, True, False)
            with act.Fori(1, B) as i:
                body(i, True, True)
            body(B, False, True)

        @block.vector
        def _(dve):
            dve.sem_inc(t_lo, 1)
            dve.sem_inc(x1_lo_done, 1)
            dve.sem_inc(q_sum_done, 1)
            dve.sem_inc(res_done, 2)
            dve.sem_inc(x1_done, 2)
            dve.sem_inc(q_lo_done, 2)
            dve.wait_ge(w_split, 1)
            nc.vector.tensor_tensor(w_lo[:, :, :, :], w_raw[:, :, :, :], w_hi[:, :, :, :].bitcast(F32), ALU.subtract).then_inc(w_split, 1)

            def split_att(i, c):
                dve.wait_ge(t_hi, 2 * i + c + 1 + 1)
                nc.vector.tensor_tensor(a_lo[c][:, :, :], t_ps[:, :, :], a_hi[c][:, :, :].bitcast(F32), ALU.subtract).then_inc(t_lo, 1)

            def residual(i, c):
                n = 2 * i + c
                dve.wait_ge(r_done, n + 1 + 2)
                dve.wait_ge(x_biased, n + 1)
                nc.vector.tensor_tensor(res[c][:, :, :], r_ps[:, :, :], x[c][:, :, :], ALU.add).then_inc(res_done, 1)

            def moments(i, c):
                dve.wait_ge(res_done, 2 * i + c + 1 + 2)
                norm.moments(dve, 2 * i + c, res[c])

            def scale(i, c):
                dve.wait_ge(out_done[c], 16 * i + 16)
                norm.scale(dve, 2 * i + c, res[c], x1[c]).then_inc(x1_done, 1)

            def split_x1(i, c):
                dve.wait_ge(x1_hi_done, 2 * i + c + 1 + 1)
                nc.vector.tensor_tensor(x1_lo[c][:, :, :], t1_ps[:, :, :], x1_hi[c][:, :, :].bitcast(F32), ALU.subtract).then_inc(x1_lo_done, 1)

            def bias_q(i, c):
                n = 2 * i + c
                dve.wait_ge(q_done, n + 1 + 2)
                for k in range(CK):
                    ins = nc.vector.tensor_scalar(q_sum[c][:, k, :], q_ps[:, k, :], bq[:, k:k + 1], float(D) ** -0.5, ALU.add, ALU.mult)
                ins.then_inc(q_sum_done, 1)

            def split_q(i, c):
                n = 2 * i + c
                dve.wait_ge(q_hi_done, n + 1)
                nc.vector.tensor_tensor(q_lo[c][:, :, :], q_sum[c][:, :, :], q_hi[c][:, :, :].bitcast(F32), ALU.subtract).then_inc(q_lo_done, 1)

            def body(i, new, old):
                for c in range(2):
                    if new:
                        split_att(i, c)
                    if old:
                        split_x1(i - 1, c)
                    if new:
                        residual(i, c)
                        moments(i, c)
                    if old:
                        bias_q(i - 1, c)
                    if new:
                        scale(i, c)
                    if old:
                        split_q(i - 1, c)

            body(0, True, False)
            with dve.Fori(1, B) as i:
                body(i, True, True)
            body(B, False, True)

        @block.tensor
        def _(pe):
            pe.sem_inc(r_done, 2)
            pe.sem_inc(q_done, 2)
            pe.wait_ge(w_split, 2)
            pe.wait_ge(const_in, 80)

            def transpose(i, c, src, dst):
                for t in range(TPC):
                    for k in range(CK):
                        ins = nc.tensor.transpose(dst[:, k, t * P:(t + 1) * P], src[:, t, k * P:(k + 1) * P], ident[:, :])
                return ins

            def transpose_att(i, c):
                pe.wait_ge(in_done[c], 80 * i + 80)
                pe.wait_ge(t_lo, 2 * i + c + 1)
                transpose(i, c, att[c], t_ps).then_inc(t_done, 1)

            def project(i, c):
                n = 2 * i + c
                pe.wait_ge(t_lo, n + 1 + 1)
                pe.wait_ge(res_done, n + 2)
                for t in range(TPC):
                    prods = [(a[:, k, t * P:(t + 1) * P], b[:, 0, k, :]) for k in range(CK)
                             for a, b in parts3(a_hi[c], a_lo[c], w_hi, w_lo)]
                    for m, (a, b) in enumerate(prods):
                        ins = nc.tensor.matmul(r_ps[:, t, :], a, b, start=(m == 0), stop=(m == len(prods) - 1))
                ins.then_inc(r_done, 1)

            def transpose_x1(i, c):
                n = 2 * i + c
                pe.wait_ge(x1_done, n + 1 + 2)
                pe.wait_ge(x1_lo_done, n + 1)
                transpose(i, c, x1[c], t1_ps).then_inc(t1_done, 1)

            def queries(i, c):
                n = 2 * i + c
                pe.wait_ge(x1_lo_done, n + 1 + 1)
                pe.wait_ge(q_sum_done, n + 1)
                for m in range(CK):
                    prods = [(b[:, 1, k, m * P:(m + 1) * P], a[:, k, :]) for k in range(CK)
                             for a, b in parts3(x1_hi[c], x1_lo[c], w_hi, w_lo)]
                    for j, (a, b) in enumerate(prods):
                        ins = nc.tensor.matmul(q_ps[:, m, :], a, b, start=(j == 0), stop=(j == len(prods) - 1))
                ins.then_inc(q_done, 1)

            def body(i, new, old):
                for c in range(2):
                    if new:
                        transpose_att(i, c)
                    if old:
                        transpose_x1(i - 1, c)
                    if new:
                        project(i, c)
                    if old:
                        queries(i - 1, c)

            body(0, True, False)
            with pe.Fori(1, B) as i:
                body(i, True, True)
            body(B, False, True)


L = 77
HL = H // CK
GL = HG * L
NEG = -1000000000000000.0


CPB = 2
TPB = CPB * TPC


def cross_schedule(first, last=False):
    order = []
    for m in range(TPB):
        ago, tile = (1, m + TPB - 2) if m < 2 else (0, m - 2)
        if not (first and ago) and not (last and not ago):
            order += [("transpose", ago, tile, half) for half in range(2)]
        if m % TPC == 1 and not (first and m == 1) and not (last and m != 1):
            order += [("values", int(m == 1), int(m == 1), j) for j in range(2)]
        if m % TPC == 2 and not (first and m == 2) and not (last and m != 2):
            order.append(("project", int(m == 2), int(m == 2), 0))
    return order


class Use:

    def __init__(self, i, what, end=False):
        first, rest = cross_schedule(True), cross_schedule(False)
        order = cross_schedule(False, True) if end else first if isinstance(i, int) and i == 0 else rest
        n = order.index(what)
        start = 0 if order is first else len(first)
        self.bank = (start + n) % 2
        if n >= 2:
            self.before = order[n - 2]
        elif order is first:
            self.before = None
        else:
            kind, ago, which, half = (first if isinstance(i, int) and i == 1 else rest)[n - 2]
            self.before = (kind, ago + 1, which, half)


def stage_cross(nc, io):
    with Scope(nc, "cr") as s:
        ctx = s.sb("ctx", [P, CK, B * L], F32)
        ctx_hi = s.sb("ctx_hi", [P, CK, B * L], F32R)
        ctx_lo = s.sb("ctx_lo", [P, CK, B * L], F32R)
        kv_raw = s.sb("kv_raw", [P, 2, CK, C], F32)
        kv_hi = s.sb("kv_hi", [P, 2, CK, C], F32R)
        kv_lo = s.sb("kv_lo", [P, 2, CK, C], F32R)
        bk = s.sb("bk", [P, CK], F32)
        bv = s.sb("bv", [P, C], F32)
        head_of = s.sb("head_of", [P, HL], F32)
        k_sum = s.sb("k_sum", [P, CK, B * L], F32)
        k_hi = s.sb("k_hi", [P, CK, B * L], F32)
        k_lo = s.sb("k_lo", [P, CK, B * L], F32)
        k_blk = s.sb("k_blk", [P, 2, B, CK, HL * L], F32R)
        v_all = s.sb("v_all", [L, B, C + D], F32)
        v_now = s.sb("v_now", [L, C + D], F32)
        mask_i = s.sb("mask_i", [P, B * L], I32)
        mask_f = s.sb("mask_f", [P, B * L], F32)
        mask_w = s.sb("mask_w", [P, B, HG, L], F32R)
        mask_sel = s.sb("mask_sel", [P, P], F32R)
        wo_raw = s.sb("wo_raw", [P, HG, C], F32)
        wo_hi = s.sb("wo_hi", [P, HG, C], F32R)
        wo_lo = s.sb("wo_lo", [P, HG, C], F32R)
        bo = s.sb("bo", [P, C], F32)
        ident = s.sb("ident", [P, P], F32)
        q = [[s.sb(f"q{c}{part}", [P, CK, CH], F32R) for part in range(2)] for c in range(2)]
        x1 = [s.sb(f"x1{c}", [P, TPC, C], F32) for c in range(2)]
        e = [s.sb(f"e{i}", [P, H, L], F32) for i in range(4)]
        w_t = s.sb("w_t", [L, H, CH], F32)
        top = [s.sb(f"top{i}", [P, H], F32) for i in range(2)]
        tot = [s.sb(f"tot{i}", [P, H], F32) for i in range(2)]
        rec = [s.sb(f"rec{i}", [P, H], F32) for i in range(2)]
        o_hi = s.sb("o_hi", [P, HG, CH], F32R)
        o_lo = s.sb("o_lo", [P, HG, CH], F32R)
        res = s.sb("res", [P, TPC, C], F32)
        x2 = [s.sb(f"x2{c}", [P, TPC, C], F32) for c in range(2)]
        norm = Norm(nc, s, io["apart"])
        s_ps = [s.pb(f"s_ps{i}", (P, 2, 512)) for i in range(2)]
        t_ps = [s.pb(f"t_ps{i}", (P, 2, 512)) for i in range(2)]

        ctx_in, const_in = s.sem("ctx_in"), s.sem("const_in")
        hi_done, lo_done = s.sem("hi_done"), s.sem("lo_done")
        k_done, v_done = s.sem("k_done"), s.sem("v_done")
        prep = s.sem("prep")
        q_in = [s.sem(f"q_in{c}") for c in range(2)]
        x_in = [s.sem(f"x_in{c}") for c in range(2)]
        v_ready = s.sem("v_ready")
        x_biased = s.sem("x_biased")
        s_done = s.sem("s_done")
        top_done = s.sem("top_done")
        sub_done = s.sem("sub_done")
        exp_done = s.sem("exp_done")
        tot_done, rec_done = s.sem("tot_done"), s.sem("rec_done")
        w_done = s.sem("w_done")
        t_done = s.sem("t_done")
        wt_done = s.sem("wt_done")
        pv_done = s.sem("pv_done")
        o_hi_done, o_lo_done = s.sem("o_hi_done"), s.sem("o_lo_done")
        r_done = s.sem("r_done")
        res_done = s.sem("res_done")
        x2_done = s.sem("x2_done")
        out_done = [s.sem(f"out_done{c}") for c in range(2)]
        block = s.block()

        @block.sync
        def _(sp):
            sp.dma_start(ctx[:, :, :], io["ctxT"].rearrange("(c p) n -> p c n", p=P)).then_inc(ctx_in, 16)
            for j, name in enumerate(("wkT", "wvT")):
                sp.dma_start(kv_raw[:, j], io[name].rearrange("(c p) n -> p c n", p=P)).then_inc(ctx_in, 16)
            sp.dma_start(bk[:, :], io["bk2"]).then_inc(const_in, 16)
            sp.dma_start(bv[:, :], io["bv"].partition_broadcast(P)).then_inc(const_in, 16)
            sp.dma_start(head_of[:, :], io["head_of"]).then_inc(const_in, 16)
            sp.dma_start(ident[:, :], io["ident"]).then_inc(const_in, 16)
            sp.dma_start(bo[:, :], io["bo"].partition_broadcast(P)).then_inc(const_in, 16)
            for row in (0, 32):
                sp.dma_start(mask_i[row:row + 1, :], io["mask"]).then_inc(const_in, 16)
            sp.dma_start(wo_raw[:, :, :], io["woT"].rearrange("(g p) n -> p g n", p=P)).then_inc(const_in, 16)
            for c in range(2):
                sp.sem_inc(out_done[c], 16)

            def load_q(n, c):
                for part in range(2):
                    sp.dma_start(q[c][part][:, :, :].bitcast(F32), io["q2_scr"][n, part].rearrange("k p t -> p k t")).then_inc(q_in[c], 16)

            def load_x(n, c):
                sp.dma_start(x1[c][:, :, :], chunk_rows(io["x1_scr"], n)).then_inc(x_in[c], 16)

            def store(n, c):
                sp.wait_ge(x2_done, n + 1)
                sp.dma_start(chunk_rows(io["x2_scr"], n), x2[c][:, :, :]).then_inc(out_done[c], 16)

            def body(i, first, last):
                if not first:
                    store(2 * i - 2, 0)
                    sp.wait_ge(res_done, 2 * i)
                    load_x(2 * i + 1, 1)
                if not last:
                    sp.wait_ge(s_done, 2 * TPB * i + 2 * TPC)
                    load_q(2 * i + 2, 0)
                if not first:
                    store(2 * i - 1, 1)
                if not last:
                    sp.wait_ge(res_done, 2 * i + 1)
                    load_x(2 * i + 2, 0)
                    sp.wait_ge(s_done, 2 * TPB * (i + 1))
                    load_q(2 * i + 3, 1)

            load_q(0, 0)
            load_q(1, 1)
            load_x(0, 0)
            load_x(1, 1)
            body(0, True, False)
            with sp.Fori(1, B - 1) as i:
                body(i, False, False)
            body(B - 1, False, True)
            for c in range(2):
                store(2 * B - 2 + c, c)
            for c in range(2):
                sp.wait_ge(out_done[c], 16 * B + 16)

        @block.gpsimd
        def _(pool):
            pool.wait_ge(prep, 20)

            def bias_x(i, c):
                pool.wait_ge(x_in[c], 16 * i + 16)
                pool.tensor_tensor(x1[c][:, :, :], x1[c][:, :, :], bo[:, :].unsqueeze(1).to_broadcast([P, TPC, C]), ALU.add).then_inc(x_biased, 1)

            def body(i, first):
                for m in range(TPB):
                    if m == 2:
                        if not first:
                            pool.wait_ge(pv_done, 4 * i + 2)
                        pool.tensor_copy(v_now[:, :].unsqueeze(1), v_all[:, bass.ds(i, 1), :]).then_inc(v_ready, 1)
                    if m == 3:
                        bias_x(i, 0)
                    if m == 7:
                        bias_x(i, 1)
                    pool.wait_ge(rec_done, TPB * i + m + 1)
                    pool.tensor_tensor(e[m % 4][:, :, :], e[m % 4][:, :, :], rec[m % 2][:, :].unsqueeze(2).to_broadcast([P, H, L]), ALU.mult).then_inc(w_done, 1)

            body(0, True)
            with pool.Fori(1, B) as i:
                body(i, False)

        @block.scalar
        def _(act):
            act.wait_ge(ctx_in, 48)
            nc.scalar.activation(ctx_hi[:, :, :], ctx[:, :, :], ACT.Copy).then_inc(hi_done, 1)
            nc.scalar.activation(kv_hi[:, :, :, :], kv_raw[:, :, :, :], ACT.Copy).then_inc(hi_done, 1)
            act.wait_ge(const_in, 128)
            nc.scalar.activation(wo_hi[:, :, :], wo_raw[:, :, :], ACT.Copy).then_inc(hi_done, 1)

            def weights(i, m):
                act.wait_ge(sub_done, 2 * (TPB * i + m) + 2 + 2)
                nc.scalar.activation(e[m % 4][:, :, :], e[m % 4][:, :, :], ACT.Exp).then_inc(exp_done, 1)

            def copy_t(i, use, ago, m):
                for half in range(2):
                    act.wait_ge(t_done, 2 * (TPB * (i - ago) + m) + half + 1 + 8)
                    if m % TPC == 0 and half == 0:
                        act.wait_ge(pv_done, 4 * (i - ago) + 2 * (m // TPC) + 2)
                    nc.scalar.activation(
                        w_t[:, half * HL:(half + 1) * HL, (m % TPC) * P:(m % TPC + 1) * P].rearrange("p (g h) q -> p g h q", g=2),
                        t_ps[use(("transpose", ago, m, half)).bank][0:L, :, :].rearrange("p g (h q) -> p g h q", h=HG),
                        ACT.Copy).then_inc(wt_done, 1)

            def split_o(i, use, ago, c):
                n = 2 * (i - ago) + c
                act.wait_ge(r_done, n + 1)
                for j in range(2):
                    act.wait_ge(pv_done, 2 * n + j + 1 + 2)
                    nc.scalar.activation(o_hi[:, 2 * j:2 * j + 2, :], t_ps[use(("values", ago, c, j)).bank][:, :, :], ACT.Copy).then_inc(o_hi_done, 1)

            def body(i, first):
                def use(what):
                    return Use(i, what)
                for m in range(TPB):
                    if m >= 2:
                        copy_t(i, use, 0, m - 2)
                    elif not first:
                        copy_t(i, use, 1, m + TPB - 2)
                    weights(i, m)
                    if m == 5:
                        split_o(i, use, 0, 0)
                    if m == 1 and not first:
                        split_o(i, use, 1, 1)
                    if m == 3 and not first:
                        norm.take_root(act, 2 * i - 1)
                    if m == 7:
                        norm.take_root(act, 2 * i)

            body(0, True)
            with act.Fori(1, B) as i:
                body(i, False)

            def use(what):
                return Use(B, what, True)
            copy_t(B, use, 1, TPB - 2)
            copy_t(B, use, 1, TPB - 1)
            split_o(B, use, 1, 1)
            norm.take_root(act, 2 * B - 1)

        @block.vector
        def _(dve):
            nc.vector.memset(v_all[:, :, :], 0.0)
            nc.vector.memset(mask_w[:, :, :, :].bitcast(F32), 0.0)
            nc.vector.memset(mask_sel[:, :].bitcast(F32), 0.0).then_inc(prep, 1)
            dve.wait_ge(prep, 1)
            nc.vector.memset(mask_sel[0:1, :].bitcast(F32), 1.0)
            nc.vector.memset(mask_sel[32:33, :].bitcast(F32), 1.0)
            dve.wait_ge(hi_done, 1)
            nc.vector.tensor_tensor(ctx_lo[:, :, :], ctx[:, :, :], ctx_hi[:, :, :].bitcast(F32), ALU.subtract)
            dve.wait_ge(hi_done, 2)
            nc.vector.tensor_tensor(kv_lo[:, :, :, :], kv_raw[:, :, :, :], kv_hi[:, :, :, :].bitcast(F32), ALU.subtract).then_inc(lo_done, 1)
            dve.wait_ge(const_in, 128)
            for row in (0, 32):
                ins = nc.vector.tensor_copy(mask_f[row:row + 1, :], mask_i[row:row + 1, :])
            ins.then_inc(prep, 1)
            dve.wait_ge(prep, 2)
            for row in (0, 32):
                ins = nc.vector.tensor_scalar(mask_f[row:row + 1, :], mask_f[row:row + 1, :], NEG, None, ALU.mult)
            ins.then_inc(prep, 1)
            dve.wait_ge(prep, 3)

            def on_heads(row):
                return mask_f[row:row + 1, :].rearrange("p (b k) -> p b k", b=B).unsqueeze(2).to_broadcast([1, B, HG, L])
            for row in (0, 32):
                ins = nc.vector.tensor_copy(mask_w[row:row + 1, :, :, :], on_heads(row))
            ins.then_inc(prep, 1)
            dve.wait_ge(prep, 4)
            nc.vector.tensor_tensor(mask_w[32:33, :, :, :], on_heads(32), mask_w[32:33, :, :, :].bitcast(F32), ALU.subtract).then_inc(prep, 1)
            dve.wait_ge(k_done, 1)
            for k in range(CK):
                ins = nc.vector.tensor_scalar(k_sum[:, k, :], s_ps[0][:, k, 0:B * L], bk[:, k:k + 1], None, ALU.add)
            ins.then_inc(prep, 1)
            dve.wait_ge(prep, 6)
            nc.vector.tensor_copy(k_hi[:, :, :].bitcast(F32R), k_sum[:, :, :]).then_inc(prep, 1)
            dve.wait_ge(prep, 7)
            nc.vector.tensor_tensor(k_lo[:, :, :], k_sum[:, :, :], k_hi[:, :, :], ALU.subtract).then_inc(prep, 1)
            dve.wait_ge(prep, 8)
            heads = head_of[:, :].unsqueeze(2).to_broadcast([P, HL, L])
            for part, src in enumerate((k_hi, k_lo)):
                for b in range(B):
                    for k in range(CK):
                        ins = nc.vector.tensor_tensor(k_blk[:, part, b, k, :].rearrange("p (h n) -> p h n", h=HL),
                                                      src[:, k, b * L:(b + 1) * L].unsqueeze(1).to_broadcast([P, HL, L]), heads, ALU.mult)
            ins.then_inc(prep, 1)
            dve.wait_ge(v_done, 1)
            for b in range(B):
                ins = nc.vector.tensor_tensor(v_all[:, b, 0:C], t_ps[b // 2][0:L, b % 2, 0:C], bv[0:L, :], ALU.add)
            ins.then_inc(prep, 1)
            dve.wait_ge(hi_done, 3)
            nc.vector.tensor_tensor(wo_lo[:, :, :], wo_raw[:, :, :], wo_hi[:, :, :].bitcast(F32), ALU.subtract).then_inc(prep, 10)
            dve.sem_inc(sub_done, 2)

            def shift(i, m):
                tile = TPB * i + m
                views = [x[:, :, 0:GL].rearrange("p g (h n) -> p g h n", h=HG) for x in s_ps]
                for half in range(2):
                    dve.wait_ge(s_done, 2 * tile + half + 1)
                    ins = nc.vector.tensor_reduce(top[m % 2][:, half * HL:(half + 1) * HL].rearrange("p (g h) -> p g h", g=2), views[half], AX.X, ALU.max)
                ins.then_inc(top_done, 1)
                dve.wait_ge(top_done, tile + 1)
                dve.wait_ge(t_done, 2 * tile + 2)
                for half in range(2):
                    nc.vector.tensor_tensor(e[m % 4][:, half * HL:(half + 1) * HL, :].rearrange("p (g h) n -> p g h n", g=2), views[half],
                                            top[m % 2][:, half * HL:(half + 1) * HL].rearrange("p (g h) -> p g h", g=2).unsqueeze(3).to_broadcast([P, 2, HG, L]),
                                            ALU.subtract).then_inc(sub_done, 1)

            def totals(i, m):
                dve.wait_ge(exp_done, TPB * i + m + 1)
                nc.vector.tensor_reduce(tot[m % 2][:, :], e[m % 4][:, :, :], AX.X, ALU.add).then_inc(tot_done, 1)
                dve.wait_ge(tot_done, TPB * i + m + 1)
                if not (isinstance(i, int) and i == 0 and m < 2):
                    dve.wait_ge(w_done, TPB * i + m - 1)
                nc.vector.reciprocal(rec[m % 2][:, :], tot[m % 2][:, :]).then_inc(rec_done, 1)

            def split_o(i, use, ago, c):
                n = 2 * (i - ago) + c
                for j in range(2):
                    dve.wait_ge(o_hi_done, 2 * n + j + 1)
                    nc.vector.tensor_tensor(o_lo[:, 2 * j:2 * j + 2, :], t_ps[use(("values", ago, c, j)).bank][:, :, :],
                                            o_hi[:, 2 * j:2 * j + 2, :].bitcast(F32), ALU.subtract).then_inc(o_lo_done, 1)

            def residual(i, use, ago, c):
                n = 2 * (i - ago) + c
                dve.wait_ge(r_done, n + 1 + 1)
                dve.wait_ge(x_biased, n + 1)
                nc.vector.tensor_tensor(res[:, :, :], t_ps[use(("project", ago, c, 0)).bank][:, :, :].rearrange("p g (t e) -> p (g t) e", t=2),
                                        x1[c][:, :, :], ALU.add).then_inc(res_done, 1)

            def moments(n):
                dve.wait_ge(res_done, n + 1)
                norm.moments(dve, n, res)

            def scale(n, i, c):
                dve.wait_ge(out_done[c], 16 * i + 16)
                norm.scale(dve, n, res, x2[c]).then_inc(x2_done, 1)

            def body(i, first):
                def use(what):
                    return Use(i, what)
                for m in range(TPB):
                    if m == 3 and not first:
                        residual(i, use, 1, 1)
                    if m == 7:
                        residual(i, use, 0, 0)
                    if m == 6:
                        split_o(i, use, 0, 0)
                    if m == 2 and not first:
                        split_o(i, use, 1, 1)
                    shift(i, m)
                    if m == 3 and not first:
                        moments(2 * i - 1)
                    if m == 4 and not first:
                        scale(2 * i - 1, i - 1, 1)
                    if m == 7:
                        moments(2 * i)
                    if m == 0 and not first:
                        scale(2 * i - 2, i - 1, 0)
                    totals(i, m)

            body(0, True)
            with dve.Fori(1, B) as i:
                body(i, False)

            def use(what):
                return Use(B, what, True)
            split_o(B, use, 1, 1)
            scale(2 * B - 2, B - 1, 0)
            dve.wait_ge(x2_done, 2 * B - 1)
            residual(B, use, 1, 1)
            moments(2 * B - 1)
            scale(2 * B - 1, B - 1, 1)

        @block.tensor
        def _(pe):
            pe.sem_inc(t_done, 8)
            pe.sem_inc(pv_done, 2)
            pe.sem_inc(r_done, 1)
            pe.wait_ge(lo_done, 1)
            for m in range(CK):
                prods = [(b[:, 0, k, m * P:(m + 1) * P], a[:, k, :]) for k in range(CK)
                         for a, b in parts3(ctx_hi, ctx_lo, kv_hi, kv_lo)]
                for j, (a, b) in enumerate(prods):
                    ins = nc.tensor.matmul(s_ps[0][:, m, 0:B * L], a, b, start=(j == 0), stop=(j == len(prods) - 1))
            ins.then_inc(k_done, 1)
            for n in range(B):
                prods = [(a[:, k, n * L:(n + 1) * L], b[:, 1, k, :]) for k in range(CK)
                         for a, b in parts3(ctx_hi, ctx_lo, kv_hi, kv_lo)]
                for j, (a, b) in enumerate(prods):
                    ins = nc.tensor.matmul(t_ps[n // 2][0:L, n % 2, 0:C], a, b, start=(j == 0), stop=(j == len(prods) - 1))
            ins.then_inc(v_done, 1)
            pe.wait_ge(prep, 20)

            def scores(i, m):
                c, t = divmod(m, TPC)
                if t == 0:
                    pe.wait_ge(q_in[c], 32 * i + 32)
                tok = slice(t * P, (t + 1) * P)
                for k in range(CK):
                    pe.wait_ge(sub_done, 2 * (TPB * i + m) + k + 1)
                    for half in range(2):
                        cols = slice(half * GL, (half + 1) * GL)
                        for j, (a, b) in enumerate(((0, 0), (0, 1), (1, 0))):
                            nc.tensor.matmul(s_ps[k][:, half, 0:GL], q[c][a][:, k, tok], k_blk[:, b, bass.ds(i, 1), k, cols].rearrange("p o n -> p (o n)"),
                                             start=(j == 0), stop=False)
                        ins = nc.tensor.matmul(s_ps[k][:, half, 0:GL], mask_sel[:, :], mask_w[:, bass.ds(i, 1), :, :].rearrange("p o h n -> p (o h n)"),
                                               start=False, stop=True)
                    ins.then_inc(s_done, 1)

            def wait_free(i, u):
                if u.before is None:
                    return
                kind, ago, which, half = u.before
                j = i - ago
                if kind == "transpose":
                    pe.wait_ge(wt_done, 2 * (TPB * j + which) + half + 1)
                elif kind == "values":
                    pe.wait_ge(o_lo_done, 2 * (2 * j + which) + half + 1)
                else:
                    pe.wait_ge(res_done, 2 * j + which + 1)

            def transpose_w(i, use, ago, m):
                pe.wait_ge(w_done, TPB * (i - ago) + m + 1)
                for half in range(2):
                    u = use(("transpose", ago, m, half))
                    wait_free(i, u)
                    for h in range(HL):
                        ins = nc.tensor.transpose(t_ps[u.bank][0:L, h // HG, (h % HG) * P:(h % HG + 1) * P], e[m % 4][:, half * HL + h, :], ident[:, :])
                    ins.then_inc(t_done, 1)

            def values(i, use, ago, c):
                n = 2 * (i - ago) + c
                pe.wait_ge(wt_done, 8 * n + 8)
                pe.wait_ge(v_ready, i - ago + 1)
                for j in range(2):
                    u = use(("values", ago, c, j))
                    wait_free(i, u)
                    for g in range(2):
                        for h in range(HG):
                            head = (2 * j + g) * HG + h
                            ins = nc.tensor.matmul(t_ps[u.bank][32 * h:32 * h + 32, g, :], v_now[:, head * D:head * D + 32], w_t[:, head, :], start=True, stop=True)
                    ins.then_inc(pv_done, 1)

            def project(i, use, ago, c):
                n = 2 * (i - ago) + c
                u = use(("project", ago, c, 0))
                pe.wait_ge(o_lo_done, 2 * n + 2)
                wait_free(i, u)
                for t in range(TPC):
                    prods = [(a[:, g, t * P:(t + 1) * P], b[:, g, :]) for g in range(HG)
                             for a, b in parts3(o_hi, o_lo, wo_hi, wo_lo)]
                    for j, (a, b) in enumerate(prods):
                        ins = nc.tensor.matmul(t_ps[u.bank][:, t // 2, (t % 2) * C:(t % 2 + 1) * C], a, b, start=(j == 0), stop=(j == len(prods) - 1))
                ins.then_inc(r_done, 1)

            def body(i, first):
                def use(what):
                    return Use(i, what)
                for m in range(TPB):
                    scores(i, m)
                    if m >= 2:
                        transpose_w(i, use, 0, m - 2)
                    elif not first:
                        transpose_w(i, use, 1, m + TPB - 2)
                    if m == 1 and not first:
                        values(i, use, 1, 1)
                    if m == 2 and not first:
                        project(i, use, 1, 1)
                    if m == 5:
                        values(i, use, 0, 0)
                    if m == 6:
                        project(i, use, 0, 0)

            body(0, True)
            body(1, False)
            with pe.Fori(2, B) as i:
                body(i, False)

            def use(what):
                return Use(B, what, True)
            transpose_w(B, use, 1, TPB - 2)
            transpose_w(B, use, 1, TPB - 1)
            values(B, use, 1, 1)
            project(B, use, 1, 1)


E = 8
CAP = 1024
HID = 1024
HM = HID // P
SLOTS = E * CAP


def stage_router(nc, io, keep):
    with Scope(nc, "ro") as s:
        ident = s.sb("ident", [P, P], F32)
        w_raw = s.sb("w_raw", [P, CK, HID], F32)
        w_hi = s.sb("w_hi", [P, CK, HID], F32R)
        w_lo = s.sb("w_lo", [P, CK, HID], F32R)
        rb1 = s.sb("rb1", [P, HM], F32)
        rw2 = s.sb("rw2", [P, HM, 32], F32)
        rb2 = s.sb("rb2", [P, E], F32)
        x2 = [s.sb(f"x2{c}", [P, TPC, C], F32) for c in range(2)]
        x_send = [s.sb(f"x_send{c}", [P, TPC, C], F32) for c in range(2)]
        x_hi = [s.sb(f"x_hi{c}", [P, CK, CH], F32R) for c in range(2)]
        x_lo = [s.sb(f"x_lo{c}", [P, CK, CH], F32R) for c in range(2)]
        hid = [s.sb(f"hid{c}", [P, HM, CH], F32) for c in range(2)]
        l_sb = s.sb("l_sb", [P, CH], F32)
        part = s.sb("part", [P, TPC, E], F32)
        logit = s.sb("logit", [P, TPC, E], F32)
        best = s.sb("best", [P, TPC, 8], F32)
        where = s.sb("where", [P, TPC, 8], U32)
        before = s.sb("before", [P, P], F32)
        ones = s.sb("ones", [P, P], F32)
        iota = s.sb("iota", [P, E], F32)
        hot = s.sb("hot", [P, TPC, 2, E], F32)
        both = s.sb("both", [P, TPC + 1, E], F32)
        base = s.sb("base", [P, E], F32)
        place = s.sb("place", [P, TPC, E], F32)
        mine = s.sb("mine", [P, TPC, 2, E], F32)
        pos = s.sb("pos", [P, TPC, 2], F32)
        get = s.sb("get", [P, TPC, 2], F32)
        put = s.sb("put", [P, TPC, 2], F32)
        put_u = [s.sb(f"put_u{c}", [P, TPC * 2], U32) for c in range(2)]
        value = s.sb("value", [P, TT, 2], F32)
        expert = s.sb("expert", [P, TPC, 2], F32)
        kept = s.sb("kept", [P, TT, 2], F32)
        diff = s.sb("diff", [P, TT], F32)
        share = s.sb("share", [P, TT, 2], F32)
        t_ps = s.pb("t_ps", (P, CK, CH))
        h_ps = [s.pb(f"h_ps{i}") for i in range(4)]
        l_ps = s.pb("l_ps")
        lt_ps = s.pb("lt_ps", (P, TPC, P))

        const_in = s.sem("const_in")
        w_split = s.sem("w_split")
        in_done = [s.sem(f"in_done{c}") for c in range(2)]
        send_in = [s.sem(f"send_in{c}") for c in range(2)]
        t_done, x_hi_done, x_lo_done = s.sem("t_done"), s.sem("x_hi_done"), s.sem("x_lo_done")
        h_done, relu_done = s.sem("h_done"), s.sem("relu_done")
        l_done, l_copied = s.sem("l_done"), s.sem("l_copied")
        lt_done = s.sem("lt_done")
        sum_done, logit_done = s.sem("sum_done"), s.sem("logit_done")
        best_done, pick = s.sem("best_done"), s.sem("pick")
        count_done = s.sem("count_done")
        place_step = s.sem("place_step")
        share_step = s.sem("share_step")
        exp_done = s.sem("exp_done")
        sent = [s.sem(f"sent{c}") for c in range(2)]
        block = s.block()

        @block.sync
        def _(sp):
            sp.dma_start(w_raw[:, :, :], io["rw1"].rearrange("(c p) n -> p c n", p=P)).then_inc(const_in, 16)
            sp.dma_start(ident[:, :], io["ident"]).then_inc(const_in, 16)
            sp.dma_start(rb1[:, :], io["rb1"]).then_inc(const_in, 16)
            sp.dma_start(rw2[:, :, :], io["rw2"]).then_inc(const_in, 16)
            sp.dma_start(rb2[:, :], io["rb2"].partition_broadcast(P)).then_inc(const_in, 16)
            sp.dma_start(before[:, :], io["before"]).then_inc(const_in, 16)
            sp.dma_start(iota[:, :], io["iota"].partition_broadcast(P)).then_inc(const_in, 16)
            def load(n, c):
                sp.dma_start(x2[c][:, :, :], chunk_rows(io["x2_scr"], n)).then_inc(in_done[c], 16)

            def load_send(n, c):
                sp.dma_start(x_send[c][:, :, :], chunk_rows(io["x2_scr"], n)).then_inc(send_in[c], 16)

            for c in range(2):
                load(c, c)
                load_send(c, c)
            with sp.Fori(0, B - 1) as i:
                for c in range(2):
                    sp.wait_ge(t_done, 2 * i + c + 1)
                    load(2 * i + c + 2, c)
                    sp.wait_ge(sent[c], 128 * i + 128)
                    load_send(2 * i + c + 2, c)

        @block.gpsimd
        def _(pool):
            with pool.Fori(0, B) as i:
                for c in range(2):
                    pool.wait_ge(send_in[c], 16 * i + 16)
                    wait_alone(pool, place_step, 10 * (2 * i + c) + 11, io["apart"])
                    for t in range(TPC):
                        for k in range(2):
                            pool.indirect_dma_start(io["rows_scr"], bass.IndirectOffsetOnAxis(put_u[c][:, 2 * t + k:2 * t + k + 1], 0),
                                                    x_send[c][:, t, :], None, bounds_check=SLOTS - 1, oob_is_err=False).then_inc(sent[c], 16)
            for c in range(2):
                pool.wait_ge(sent[c], 128 * B)

        @block.scalar
        def _(act):
            act.sem_inc(relu_done, 4)
            act.wait_ge(const_in, 112)
            nc.scalar.activation(w_hi[:, :, :], w_raw[:, :, :], ACT.Copy).then_inc(w_split, 1)

            def split_x(n, c):
                act.wait_ge(t_done, n + 1)
                act.wait_ge(h_done, 8 * n + 8)
                nc.scalar.activation(x_hi[c][:, :, :], t_ps[:, :, :], ACT.Copy).then_inc(x_hi_done, 1)

            def relus(n, c):
                act.wait_ge(l_done, n + 1)
                for m in range(HM):
                    act.wait_ge(h_done, 8 * n + m + 1 + 16)
                    nc.scalar.activation(hid[c][:, m, :], h_ps[m % 4][:, :], ACT.Relu, bias=rb1[:, m:m + 1]).then_inc(relu_done, 1)

            def copy_l(n):
                act.wait_ge(l_done, n + 1 + 2)
                act.wait_ge(lt_done, n + 1)
                nc.scalar.activation(l_sb[:, :], l_ps[:, :], ACT.Copy).then_inc(l_copied, 1)

            def body(i, last):
                for c in range(2):
                    n = 2 * i + c
                    relus(n, c)
                    copy_l(n)
                    if not (last and c == 1):
                        split_x(n + 1, 1 - c)

            split_x(0, 0)
            with act.Fori(0, B - 1) as i:
                body(i, False)
            body(B - 1, True)
            act.wait_ge(share_step, 1)
            nc.scalar.activation(diff[:, :], diff[:, :], ACT.Exp).then_inc(exp_done, 1)

        @block.vector
        def _(dve):
            dve.sem_inc(x_lo_done, 1)
            nc.vector.memset(ones[:, :], 1.0)
            nc.vector.memset(both[:, TPC, :], 0.0)
            nc.vector.memset(base[:, :], 0.0).then_inc(place_step, 1)
            dve.wait_ge(w_split, 1)
            nc.vector.tensor_tensor(w_lo[:, :, :], w_raw[:, :, :], w_hi[:, :, :].bitcast(F32), ALU.subtract).then_inc(w_split, 1)
            dve.wait_ge(const_in, 112)

            def split_x(n, c):
                dve.wait_ge(x_hi_done, n + 1)
                nc.vector.tensor_tensor(x_lo[c][:, :, :], t_ps[:, :, :], x_hi[c][:, :, :].bitcast(F32), ALU.subtract).then_inc(x_lo_done, 1)

            def choose(n):
                dve.wait_ge(lt_done, n + 1 + 1)
                nc.vector.tensor_reduce(part[:, :, :], lt_ps[:, :, :].rearrange("p t (j e) -> p t e j", j=4)[:, :, 0:E, :], AX.X, ALU.add).then_inc(sum_done, 1)
                dve.wait_ge(sum_done, n + 1)
                nc.vector.tensor_tensor(logit[:, :, :], part[:, :, :], rb2[:, :].unsqueeze(1).to_broadcast([P, TPC, E]), ALU.add).then_inc(logit_done, 1)
                wait_alone(dve, logit_done, n + 1, io["apart"])
                for t in range(TPC):
                    ins = nc.vector.max(best[:, t, :], logit[:, t, :])
                ins.then_inc(best_done, 1)
                wait_alone(dve, best_done, n + 1, io["apart"])
                for t in range(TPC):
                    ins = nc.vector.max_index(where[:, t, :], best[:, t, :], logit[:, t, :])
                ins.then_inc(pick, 1)
                dve.wait_ge(pick, 2 * n + 1)
                nc.vector.tensor_copy(value[:, bass.ds(TPC * n, TPC), :], best[:, :, 0:2])
                nc.vector.tensor_copy(expert[:, :, :], where[:, :, 0:2]).then_inc(pick, 1)
                dve.wait_ge(pick, 2 * n + 2)
                for k in range(2):
                    ins = nc.vector.tensor_tensor(hot[:, :, k, :], expert[:, :, k:k + 1].to_broadcast([P, TPC, E]),
                                                  iota[:, :].unsqueeze(1).to_broadcast([P, TPC, E]), ALU.is_equal)
                ins.then_inc(place_step, 1)
                dve.wait_ge(place_step, 10 * n + 2)
                nc.vector.tensor_tensor(both[:, 0:TPC, :], hot[:, :, 0, :], hot[:, :, 1, :], ALU.add).then_inc(place_step, 1)

            def find_places(n, c):
                counts = lt_ps[:, 0, 0:(TPC + 1) * E].rearrange("p (t e) -> p t e", e=E)
                dve.wait_ge(count_done, n + 1)
                nc.vector.tensor_tensor(place[:, :, :], counts[:, 0:TPC, :], base[:, :].unsqueeze(1).to_broadcast([P, TPC, E]), ALU.add).then_inc(place_step, 1)
                dve.wait_ge(place_step, 10 * n + 4)
                nc.vector.tensor_tensor(base[:, :], base[:, :], counts[:, TPC, :], ALU.add).then_inc(place_step, 1)
                for k in range(2):
                    ins = nc.vector.tensor_tensor(mine[:, :, k, :], hot[:, :, k, :], place[:, :, :], ALU.mult)
                ins.then_inc(place_step, 1)
                dve.wait_ge(place_step, 10 * n + 6)
                nc.vector.tensor_reduce(pos[:, :, :], mine[:, :, :, :], AX.X, ALU.add).then_inc(place_step, 1)
                dve.wait_ge(place_step, 10 * n + 7)
                nc.vector.tensor_scalar(get[:, :, :], pos[:, :, :], float(CAP - 1), None, ALU.min)
                nc.vector.tensor_scalar(kept[:, bass.ds(TPC * n, TPC), :], pos[:, :, :], float(CAP), None, ALU.is_lt)
                nc.vector.tensor_scalar(put[:, :, :], pos[:, :, :], float(CAP), float(SLOTS), ALU.is_ge, ALU.mult).then_inc(place_step, 1)
                dve.wait_ge(place_step, 10 * n + 8)
                nc.vector.scalar_tensor_tensor(get[:, :, :], expert[:, :, :], float(CAP), get[:, :, :], ALU.mult, ALU.add).then_inc(place_step, 1)
                dve.wait_ge(place_step, 10 * n + 9)
                nc.vector.tensor_copy(keep["get"][:, bass.ds(2 * TPC * n, 2 * TPC)], get[:, :, :].rearrange("p t k -> p (t k)"))
                nc.vector.tensor_tensor(put[:, :, :], put[:, :, :], get[:, :, :], ALU.add).then_inc(place_step, 1)
                dve.wait_ge(place_step, 10 * n + 10)
                if not (isinstance(n, int) and n < 2):
                    dve.wait_ge(send_in[c], 8 * (n - c) + 16)
                nc.vector.tensor_copy(put_u[c][:, :], put[:, :, :].rearrange("p t k -> p (t k)")).then_inc(place_step, 1)

            def body(i, first, last):
                for c in range(2):
                    n = 2 * i + c
                    if not (first and c == 0):
                        find_places(n - 1, 1 - c)
                    if not (last and c == 1):
                        split_x(n + 1, 1 - c)
                    choose(n)

            split_x(0, 0)
            body(0, True, False)
            with dve.Fori(1, B - 1) as i:
                body(i, False, False)
            body(B - 1, False, True)
            find_places(2 * B - 1, 1)
            nc.vector.tensor_tensor(diff[:, :], value[:, :, 1], value[:, :, 0], ALU.subtract).then_inc(share_step, 1)
            dve.wait_ge(exp_done, 1)
            nc.vector.tensor_scalar(share[:, :, 0], diff[:, :], 1.0, None, ALU.add).then_inc(share_step, 1)
            dve.wait_ge(share_step, 2)
            nc.vector.reciprocal(share[:, :, 0], share[:, :, 0]).then_inc(share_step, 1)
            dve.wait_ge(share_step, 3)
            nc.vector.tensor_tensor(share[:, :, 1], share[:, :, 0], diff[:, :], ALU.mult).then_inc(share_step, 1)
            dve.wait_ge(share_step, 4)
            nc.vector.tensor_tensor(keep["share"][:, :].rearrange("p (t k) -> p t k", k=2), share[:, :, :], kept[:, :, :], ALU.mult)

        @block.tensor
        def _(pe):
            pe.sem_inc(h_done, 16)
            pe.sem_inc(l_done, 2)
            pe.sem_inc(lt_done, 1)
            pe.wait_ge(w_split, 2)
            pe.wait_ge(const_in, 112)

            def transpose_x(n, c):
                pe.wait_ge(in_done[c], 8 * (n - c) + 16)
                pe.wait_ge(x_lo_done, n + 1)
                for t in range(TPC):
                    for k in range(CK):
                        ins = nc.tensor.transpose(t_ps[:, k, t * P:(t + 1) * P], x2[c][:, t, k * P:(k + 1) * P], ident[:, :])
                ins.then_inc(t_done, 1)

            def hidden(n, c):
                pe.wait_ge(x_lo_done, n + 1 + 1)
                for m in range(HM):
                    pe.wait_ge(relu_done, 8 * n + m + 1)
                    prods = [(b[:, k, m * P:(m + 1) * P], a[:, k, :]) for k in range(CK)
                             for a, b in parts3(x_hi[c], x_lo[c], w_hi, w_lo)]
                    for j, (a, b) in enumerate(prods):
                        ins = nc.tensor.matmul(h_ps[m % 4][:, :], a, b, start=(j == 0), stop=(j == len(prods) - 1))
                    ins.then_inc(h_done, 1)

            def logits(n, c):
                pe.wait_ge(relu_done, 8 * n + 8 + 4)
                for m in range(HM):
                    j = m % 4
                    ins = nc.tensor.matmul(l_ps[32 * j:32 * j + 32, :], rw2[:, m, :], hid[c][:, m, :], start=(m < 4), stop=(m >= 4))
                ins.then_inc(l_done, 1)

            def transpose_l(n):
                pe.wait_ge(l_copied, n + 1)
                pe.wait_ge(place_step, 10 * n + 1)
                for t in range(TPC):
                    ins = nc.tensor.transpose(lt_ps[:, t, :], l_sb[:, t * P:(t + 1) * P], ident[:, :])
                ins.then_inc(lt_done, 1)

            def count(n):
                pe.wait_ge(place_step, 10 * n + 3)
                counts = lt_ps[:, 0, 0:(TPC + 1) * E].rearrange("p (t e) -> p t e", e=E)
                nc.tensor.matmul(counts, before[:, :], both[:, :, :], start=True, stop=False)
                for t in range(TPC):
                    ins = nc.tensor.matmul(counts[:, t + 1:, :], ones[:, :], both[:, t:t + 1, :].to_broadcast([P, TPC - t, E]),
                                           start=False, stop=(t == TPC - 1))
                ins.then_inc(count_done, 1)

            def body(i, first, last):
                for c in range(2):
                    n = 2 * i + c
                    hidden(n, c)
                    if not (first and c == 0):
                        count(n - 1)
                    logits(n, c)
                    if not (last and c == 1):
                        transpose_x(n + 1, 1 - c)
                    transpose_l(n)

            transpose_x(0, 0)
            body(0, True, False)
            with pe.Fori(1, B - 1) as i:
                body(i, False, False)
            body(B - 1, False, True)
            count(2 * B - 1)


def stage_experts(nc, io, keep):
    with Scope(nc, "ex") as s:
        ident = s.sb("ident", [P, P], F32)
        w1_raw = s.sb("w1_raw", [P, CK, HID], F32)
        w2_raw = s.sb("w2_raw", [P, HM, C], F32)
        w1_hi = [s.sb(f"w1_hi{i}", [P, CK, HID], F32R) for i in range(2)]
        w1_lo = [s.sb(f"w1_lo{i}", [P, CK, HID], F32R) for i in range(2)]
        w2_hi = [s.sb(f"w2_hi{i}", [P, HM, C], F32R) for i in range(2)]
        w2_lo = [s.sb(f"w2_lo{i}", [P, HM, C], F32R) for i in range(2)]
        b1 = s.sb("b1", [P, E, HM], F32)
        b2 = [s.sb(f"b2{i}", [P, C], F32) for i in range(2)]
        rows = [s.sb(f"rows{c}", [P, TPC, C], F32) for c in range(2)]
        x_hi = [s.sb(f"x_hi{c}", [P, CK, CH], F32R) for c in range(2)]
        x_lo = [s.sb(f"x_lo{c}", [P, CK, CH], F32R) for c in range(2)]
        hid = [s.sb(f"hid{i}", [P, CH], F32) for i in range(2)]
        h_hi = [s.sb(f"h_hi{c}", [P, HM, CH], F32R) for c in range(2)]
        h_lo = [s.sb(f"h_lo{c}", [P, HM, CH], F32R) for c in range(2)]
        y = [s.sb(f"y{c}", [P, TPC, C], F32) for c in range(2)]
        t_ps = s.pb("t_ps", (P, CK, CH))
        h_ps = [s.pb(f"h_ps{i}") for i in range(2)]
        y_ps = [s.pb(f"y_ps{i}") for i in range(4)]

        const_in = s.sem("const_in")
        w_in = s.sem("w_in")
        b2_in = s.sem("b2_in")
        w_hi_done, w_lo_done = s.sem("w_hi_done"), s.sem("w_lo_done")
        in_done = [s.sem(f"in_done{c}") for c in range(2)]
        t_done, x_hi_done, x_lo_done = s.sem("t_done"), s.sem("x_hi_done"), s.sem("x_lo_done")
        h_done, relu_done = s.sem("h_done"), s.sem("relu_done")
        h_hi_done, h_lo_done = s.sem("h_hi_done"), s.sem("h_lo_done")
        y_done, biased = s.sem("y_done"), s.sem("biased")
        out_done = [s.sem(f"out_done{c}") for c in range(2)]
        block = s.block()

        def weight_part(par, part):
            rows = slice(part, part + 1) if part < 2 else slice((part - 2) * HM // 2, (part - 1) * HM // 2)
            return [x[:, rows, :] for x in ((w1_hi[par], w1_lo[par], w1_raw) if part < 2 else (w2_hi[par], w2_lo[par], w2_raw))]

        @block.sync
        def _(sp):
            sp.dma_start(ident[:, :], io["ident"]).then_inc(const_in, 16)
            sp.dma_start(b1[:, :, :], io["eb1"]).then_inc(const_in, 16)
            for c in range(2):
                sp.sem_inc(out_done[c], 16)
            rows_v = io["rows_scr"].rearrange("(n t p) e -> n p t e", p=P, t=TPC)
            y_v = io["y_scr"].rearrange("(n t p) e -> n p t e", p=P, t=TPC)
            for c in range(2):
                sp.dma_start(rows[c][:, :, :], rows_v[c]).then_inc(in_done[c], 16)

            def load_weights(e, par):
                sp.dma_start(w1_raw[:, :, :], io["ew1"].rearrange("e (c p) n -> e p c n", p=P)[e]).then_inc(w_in, 16)
                sp.dma_start(w2_raw[:, :, :], io["ew2"].rearrange("e (m p) n -> e p m n", p=P)[e]).then_inc(w_in, 16)

            def load_bias(e, par):
                sp.dma_start(b2[par][:, :], io["eb2"][e].partition_broadcast(P)).then_inc(b2_in, 16)

            load_weights(0, 0)
            load_bias(0, 0)

            def expert(e, par, last):
                if not last:
                    sp.wait_ge(w_lo_done, 4 * e + 4)
                    load_weights(e + 1, 1 - par)
                for c in range(2):
                    h = 2 * e + c
                    if not last:
                        sp.wait_ge(t_done, h + 1)
                        sp.dma_start(rows[c][:, :, :], rows_v[h + 2]).then_inc(in_done[c], 16)
                    if c == 1 or not (isinstance(e, int) and e == 0):
                        hh = h - 1
                        sp.wait_ge(biased, 4 * hh + 4 + 4)
                        sp.dma_start(y_v[hh], y[(c + 1) % 2][:, :, :]).then_inc(out_done[(c + 1) % 2], 16)
                    if c == 0 and not last:
                        load_bias(e + 1, 1 - par)

            expert(0, 0, False)
            with sp.Fori(0, 3) as i:
                expert(2 * i + 1, 1, False)
                expert(2 * i + 2, 0, False)
            expert(E - 1, 1, True)
            sp.wait_ge(biased, 8 * E + 4)
            sp.dma_start(y_v[2 * E - 1], y[1][:, :, :]).then_inc(out_done[1], 16)
            for c in range(2):
                sp.wait_ge(out_done[c], 16 * E + 16)

        @block.gpsimd
        def _(pool):
            def split_weights(e, par):
                for part in range(4):
                    pool.wait_ge(w_hi_done, 4 * e + part + 1)
                    hi, lo, raw = weight_part(par, part)
                    pool.tensor_tensor(lo, raw, hi.bitcast(F32), ALU.subtract).then_inc(w_lo_done, 1)

            pool.wait_ge(w_lo_done, 4)
            split_weights(1, 1)
            with pool.Fori(1, E // 2) as i:
                split_weights(2 * i, 0)
                split_weights(2 * i + 1, 1)

        @block.scalar
        def _(act):
            act.sem_inc(relu_done, 2)
            act.wait_ge(const_in, 32)

            def split_weights(e, par, part):
                if part == 0:
                    act.wait_ge(w_in, 32 * e + 32)
                    if not (isinstance(e, int) and e < 2):
                        act.wait_ge(y_done, 8 * (e - 1))
                hi, _, raw = weight_part(par, part)
                nc.scalar.activation(hi, raw, ACT.Copy).then_inc(w_hi_done, 1)

            def split_x(h, c):
                act.wait_ge(t_done, h + 1)
                act.wait_ge(h_done, 8 * h + 8)
                nc.scalar.activation(x_hi[c][:, :, :], t_ps[:, :, :], ACT.Copy).then_inc(x_hi_done, 1)

            def relus(h, c, e, new=None):
                for m in range(HM):
                    if new and m % 2:
                        split_weights(*new, m // 2)
                    act.wait_ge(h_done, 8 * h + m + 1 + 16)
                    act.wait_ge(h_lo_done, 8 * h + m + 1)
                    nc.scalar.activation(hid[m % 2][:, :], h_ps[m % 2][:, :], ACT.Relu,
                                         bias=b1[:, bass.ds(e, 1), m:m + 1].rearrange("p a b -> p (a b)") if not isinstance(e, int) else b1[:, e, m:m + 1]).then_inc(relu_done, 1)

            def expert(e, par, last):
                h = 2 * e
                split_x(h + 1, 1)
                relus(h, 0, e)
                if not last:
                    split_x(h + 2, 0)
                relus(h + 1, 1, e, None if last else (e + 1, 1 - par))

            for part in range(4):
                split_weights(0, 0, part)
            split_x(0, 0)
            expert(0, 0, False)
            with act.Fori(0, 3) as i:
                expert(2 * i + 1, 1, False)
                expert(2 * i + 2, 0, False)
            expert(E - 1, 1, True)

        @block.vector
        def _(dve):
            dve.sem_inc(h_lo_done, 2)
            dve.sem_inc(biased, 4)

            def split_weights(e, par):
                for part in range(4):
                    dve.wait_ge(w_hi_done, 4 * e + part + 1)
                    hi, lo, raw = weight_part(par, part)
                    nc.vector.tensor_tensor(lo, raw, hi.bitcast(F32), ALU.subtract).then_inc(w_lo_done, 1)

            def split_x(h, c):
                dve.wait_ge(x_hi_done, h + 1)
                nc.vector.tensor_tensor(x_lo[c][:, :, :], t_ps[:, :, :], x_hi[c][:, :, :].bitcast(F32), ALU.subtract).then_inc(x_lo_done, 1)

            def split_hidden(h, c, m):
                if m == 0 and not (isinstance(h, int) and h < 2):
                    dve.wait_ge(y_done, 4 * (h - 1))
                dve.wait_ge(relu_done, 8 * h + m + 1 + 2)
                nc.vector.tensor_copy(h_hi[c][:, m, :], hid[m % 2][:, :]).then_inc(h_hi_done, 1)
                dve.wait_ge(h_hi_done, 8 * h + m + 1)
                nc.vector.tensor_tensor(h_lo[c][:, m, :], hid[m % 2][:, :], h_hi[c][:, m, :].bitcast(F32), ALU.subtract).then_inc(h_lo_done, 1)

            def bias_y(h, e, c, par, t):
                if t == 0:
                    dve.wait_ge(out_done[c], 16 * e + 16)
                if t == 0:
                    dve.wait_ge(b2_in, 16 * e + 16)
                dve.wait_ge(y_done, 4 * h + t + 1)
                nc.vector.tensor_tensor(y[c][:, t, :], y_ps[t][:, 0:C], b2[par][:, :], ALU.add).then_inc(biased, 1)

            def expert(e, par, last, first):
                h = 2 * e
                split_x(h + 1, 1)
                for m in range(HM):
                    split_hidden(h, 0, m)
                if not first:
                    for t in range(TPC):
                        bias_y(h - 1, e - 1, 1, 1 - par, t)
                if not last:
                    split_x(h + 2, 0)
                for m in range(HM):
                    split_hidden(h + 1, 1, m)
                for t in range(TPC):
                    bias_y(h, e, 0, par, t)

            split_weights(0, 0)
            split_x(0, 0)
            expert(0, 0, False, True)
            with dve.Fori(0, 3) as i:
                expert(2 * i + 1, 1, False, False)
                expert(2 * i + 2, 0, False, False)
            expert(E - 1, 1, True, False)
            for t in range(TPC):
                bias_y(2 * E - 1, E - 1, 1, 1, t)

        @block.tensor
        def _(pe):
            pe.sem_inc(h_done, 16)
            pe.wait_ge(const_in, 32)

            def transpose_rows(h, e, c):
                pe.wait_ge(in_done[c], 16 * e + 16)
                if not (isinstance(h, int) and h == 0):
                    pe.wait_ge(x_lo_done, h)
                for t in range(TPC):
                    for k in range(CK):
                        ins = nc.tensor.transpose(t_ps[:, k, t * P:(t + 1) * P], rows[c][:, t, k * P:(k + 1) * P], ident[:, :])
                ins.then_inc(t_done, 1)

            def hidden(h, c, e, par):
                pe.wait_ge(x_lo_done, h + 1)
                pe.wait_ge(w_lo_done, 4 * e + 4)
                for m in range(HM):
                    pe.wait_ge(relu_done, 8 * h + m + 1)
                    prods = [(b[:, k, m * P:(m + 1) * P], a[:, k, :]) for k in range(CK)
                             for a, b in parts3(x_hi[c], x_lo[c], w1_hi[par], w1_lo[par])]
                    for j, (a, b) in enumerate(prods):
                        ins = nc.tensor.matmul(h_ps[m % 2][:, :], a, b, start=(j == 0), stop=(j == len(prods) - 1))
                    ins.then_inc(h_done, 1)

            def results(h, c, par):
                pe.wait_ge(h_lo_done, 8 * h + 8 + 2)
                for t in range(TPC):
                    pe.wait_ge(biased, 4 * h + t + 1)
                    prods = [(a[:, m, t * P:(t + 1) * P], b[:, m, :]) for m in range(HM)
                             for a, b in parts3(h_hi[c], h_lo[c], w2_hi[par], w2_lo[par])]
                    for j, (a, b) in enumerate(prods):
                        ins = nc.tensor.matmul(y_ps[t][:, 0:C], a, b, start=(j == 0), stop=(j == len(prods) - 1))
                    ins.then_inc(y_done, 1)

            def expert(e, par, last, first):
                h = 2 * e
                transpose_rows(h + 1, e, 1)
                hidden(h, 0, e, par)
                if not first:
                    results(h - 1, 1, 1 - par)
                if not last:
                    transpose_rows(h + 2, e + 1, 0)
                hidden(h + 1, 1, e, par)
                results(h, 0, par)

            transpose_rows(0, 0, 0)
            expert(0, 0, False, True)
            with pe.Fori(0, 3) as i:
                expert(2 * i + 1, 1, False, False)
                expert(2 * i + 2, 0, False, False)
            expert(E - 1, 1, True, False)
            results(2 * E - 1, 1, 1)


def stage_combine(nc, io, keep):
    with Scope(nc, "co") as s:
        x2 = [s.sb(f"x2{c}", [P, TPC, C], F32) for c in range(2)]
        got = [s.sb(f"got{c}", [P, TPC, 2, C], F32) for c in range(2)]
        get_now = [s.sb(f"get_now{c}", [P, TPC * 2], U32) for c in range(2)]
        share_now = [s.sb(f"share_now{c}", [P, TPC * 2], F32) for c in range(2)]
        out = [s.sb(f"out{c}", [P, TPC, C], F32) for c in range(2)]
        norm = Norm(nc, s, io["apart"])
        in_done = [s.sem(f"in_done{c}") for c in range(2)]
        now_done = s.sem("now_done")
        got_done = [s.sem(f"got_done{c}") for c in range(2)]
        step = s.sem("step")
        norm_done = s.sem("norm_done")
        out_done = [s.sem(f"out_done{c}") for c in range(2)]
        block = s.block()

        @block.sync
        def _(sp):
            for c in range(2):
                sp.sem_inc(out_done[c], 16)
            with sp.Fori(0, B) as i:
                for c in range(2):
                    sp.wait_ge(norm_done, 2 * i + c + 1)
                    sp.dma_start(x2[c][:, :, :], chunk_rows(io["x2_scr"], 2 * i + c)).then_inc(in_done[c], 16)
                for c in range(2):
                    sp.wait_ge(norm_done, 2 * i + c + 1 + 2)
                    sp.dma_start(chunk_rows(io["out"], 2 * i + c), out[c][:, :, :]).then_inc(out_done[c], 16)
            for c in range(2):
                sp.wait_ge(out_done[c], 16 * B + 16)

        @block.gpsimd
        def _(pool):
            def gather(n, c):
                pool.wait_ge(norm_done, n + 1)
                pool.tensor_copy(get_now[c][:, :], keep["get"][:, bass.ds(2 * TPC * n, 2 * TPC)])
                pool.tensor_copy(share_now[c][:, :], keep["share"][:, bass.ds(2 * TPC * n, 2 * TPC)]).then_inc(now_done, 1)
                wait_alone(pool, now_done, n + 1, io["apart"])
                for t in range(TPC):
                    for k in range(2):
                        pool.indirect_dma_start(got[c][:, t, k, :], None, io["y_scr"],
                                                bass.IndirectOffsetOnAxis(get_now[c][:, 2 * t + k:2 * t + k + 1], 0)).then_inc(got_done[c], 16)

            gather(0, 0)
            with pool.Fori(0, B - 1) as i:
                gather(2 * i + 1, 1)
                gather(2 * i + 2, 0)
            gather(2 * B - 1, 1)

        @block.scalar
        def _(act):
            with act.Fori(0, B) as i:
                for c in range(2):
                    norm.take_root(act, 2 * i + c)

        @block.vector
        def _(dve):
            dve.sem_inc(norm_done, 2)
            with dve.Fori(0, B) as i:
                for c in range(2):
                    n = 2 * i + c
                    dve.wait_ge(in_done[c], 16 * i + 16)
                    dve.wait_ge(now_done, n + 1)
                    dve.wait_ge(got_done[c], 128 * i + 128)
                    for k in range(2):
                        for t in range(TPC):
                            ins = nc.vector.scalar_tensor_tensor(x2[c][:, t, :], got[c][:, t, k, :], share_now[c][:, 2 * t + k:2 * t + k + 1],
                                                                 x2[c][:, t, :], ALU.mult, ALU.add)
                        ins.then_inc(step, 1)
                        dve.wait_ge(step, 2 * n + k + 1)
                    dve.wait_ge(out_done[c], 16 * i + 16)
                    norm.apply(dve, n, x2[c], out[c]).then_inc(norm_done, 1)


def consts():
    f = np.float32
    pos = np.arange(S, dtype=f)
    inv = (f(1.0) / f(10000.0) ** (np.arange(0, D, 2, dtype=f) / f(D))).astype(f)
    ang = (pos[:, None] * inv[None, :]).astype(f)
    sin, cos = np.sin(ang).astype(f), np.cos(ang).astype(f)
    cos, sin = np.tile(cos, (1, 2)), np.concatenate([-sin, sin], 1)
    scale = f(D) ** f(-0.5)
    rope = np.stack([np.stack([cos * scale, cos], 1), np.stack([sin * scale, sin], 1)], 1)
    rope = np.ascontiguousarray(rope.reshape(KT, P, 2, 2, D).transpose(1, 0, 2, 3, 4)).astype(f)
    k = np.arange(S)
    qb = np.arange(KT)[:, None]
    past = (k[None, :] // P) < qb
    tab = np.concatenate([np.where(past, k[None, :] - P * qb, 0), np.where(past, -1, 0)], 0).astype(f)
    one = ((k[None, :] // P) == qb).astype(f)
    q_rows = np.concatenate([one, one * (k[None, :] % P)], 0)
    a = np.arange(P)
    e = np.arange(HL)
    return {
        "head_of": (a[:, None] // D == e[None, :]).astype(f),
        "before": (a[:, None] < a[None, :]).astype(f),
        "iota": np.arange(E, dtype=f),
        "rope": rope,
        "ident": np.eye(P, dtype=f),
        "bias_tab": np.tile(tab, (P // 16, 1)).astype(f),
        "q_rows": np.concatenate([q_rows, q_rows], 0).astype(f),
        "min_t": np.minimum(a[None, :] - a[:, None], 0).astype(f),
        "min_mat": np.minimum(a[:, None] - a[None, :], 0).astype(f),
    }


def padded_wo(w):
    out = np.zeros((H, 2 * D, C), w.dtype)
    out[:, :D] = w.T.reshape(H, D, C)
    return out.reshape(H * 2 * D, C)


def padded_rw2(w):
    out = np.zeros((P, HM, 32), w.dtype)
    out[:, :, :E] = w.reshape(HM, P, E).transpose(1, 0, 2)
    return out


_DRAM_IN = {
    "x": ("x", lambda a: a.reshape(T, C)),
    "xT": ("x", lambda a: a.reshape(T, C).T),
    "ctxT": ("ctx_1024", lambda a: a.reshape(B * L, C).T),
    "mask": ("mask_Bx1x1xS2_ik0", lambda a: a.reshape(1, B * L)),
    "wqkvT": ("L0_attn_qkv_w", lambda a: a.T),
    "projT": ("L0_attn_proj_w", lambda a: a.T),
    "proj_b": ("L0_attn_proj_b", lambda a: a),
    "slopes": ("L0_attn_slopes", lambda a: a),
    "slope_rep": ("L0_attn_slopes", lambda a: np.repeat(a, 16).reshape(2, P).T),
    "wqT": ("L0_xattn_Wq", lambda a: a.T),
    "bq2": ("L0_xattn_bq", lambda a: a.reshape(CK, P).T),
    "wkT": ("L0_xattn_Wk", lambda a: a.T),
    "bk2": ("L0_xattn_bk", lambda a: a.reshape(CK, P).T),
    "wvT": ("L0_xattn_Wv", lambda a: a.T),
    "bv": ("L0_xattn_bv", lambda a: a),
    "woT": ("L0_xattn_Wo", padded_wo),
    "bo": ("L0_xattn_bo", lambda a: a),
    "rw1": ("L0_ffn_rw1", lambda a: a),
    "rb1": ("L0_ffn_rb1", lambda a: a.reshape(HM, P).T),
    "rw2": ("L0_ffn_rw2", padded_rw2),
    "rb2": ("L0_ffn_rb2", lambda a: a),
    "ew1": ("L0_ffn_ew1", lambda a: a),
    "eb1": ("L0_ffn_eb1", lambda a: a.reshape(E, HM, P).transpose(2, 0, 1)),
    "ew2": ("L0_ffn_ew2", lambda a: a),
    "eb2": ("L0_ffn_eb2", lambda a: a),
}


def build(nc, io, upto=9):
    nc.disable_value_cache = True

    def scratch(name, shape):
        io[name] = nc.dram_tensor(name, shape, F32, kind="Internal").ap()

    scratch("qk_scr", [NG, 2, 2, HG * D, S])
    scratch("bias_scr", [2, H * 16, S])
    scratch("top_scr", [2, 32, P])
    scratch("att_scr", [NG, P, KT, HG * D])
    scratch("x1_scr", [T, C])
    scratch("q2_scr", [T // CH, 2, CK, P, CH])
    scratch("x2_scr", [T, C])
    scratch("rows_scr", [SLOTS, C])
    scratch("y_scr", [SLOTS, C])
    with nc.semaphore("apart") as apart:
        io["apart"] = apart
        with Scope(nc, "keep") as k:
            keep = {"v": k.sb("v", [P, NG, KT, HG * VW], F32), "q_stack": k.sb("q_stack", [P, HG, S], F32R),
                    "k_stack": k.sb("k_stack", [P, HG, S], F32R), "q_rows": k.sb("q_rows", [P, S], F32),
                    "ident": k.sb("ident", [P, P], F32), "min_mat": k.sb("min_mat", [P, P], F32),
                    "min_bf": k.sb("min_bf", [P, P], BF16), "min_t_bf": k.sb("min_t_bf", [P, P], BF16),
                    "slope8": k.sb("slope8", [P, H], F32), "slope_parts": k.sb("slope_parts", [P, 3, H], F32), "slope_eye": k.sb("slope_eye", [P, 3, H, P], BF16),
                    "stack_in": k.sem("stack_in")}
            stage_qkv(nc, io, keep)
            if upto >= 2:
                stage_attention(nc, io, keep)
        if upto >= 3:
            stage_self_out(nc, io)
        if upto >= 4:
            stage_cross(nc, io)
        if upto >= 5:
            with Scope(nc, "moe") as k:
                keep = {"get": k.sb("get", [P, TT * 2], U32), "share": k.sb("share", [P, TT * 2], F32)}
                stage_router(nc, io, keep)
                if upto >= 7:
                    stage_experts(nc, io, keep)
                if upto >= 8:
                    stage_combine(nc, io, keep)


def kernel(**inputs):
    import concourse.bacc as bacc
    from concourse.bass_utils import run_bass_kernel_spmd

    nc = bacc.Bacc("TRN2", target_bir_lowering=False, num_devices=1)
    arrays = {name: np.ascontiguousarray(layout(np.asarray(inputs[source]))) for name, (source, layout) in _DRAM_IN.items()}
    arrays.update(consts())
    io = {name: nc.dram_tensor(name, a.shape, mybir.dt.from_np(a.dtype), kind="ExternalInput").ap() for name, a in arrays.items()}
    io["out"] = nc.dram_tensor("out", (T, C), F32, kind="ExternalOutput").ap()
    build(nc, io)
    r = run_bass_kernel_spmd(nc, [arrays], core_ids=[0])
    return r.results[0]["out"].reshape(B, S, C)
```
